# Optimizing a Trainium2 kernel written in Bass

```python
import numpy as np
import jax
import jax.numpy as jnp

def _softmax(x, axis=-1):
    return jax.nn.softmax(x, axis=axis)

def _gelu(x):
    return jax.nn.gelu(x, approximate=True)

def _silu(x):
    return jax.nn.silu(x)

def _sigmoid(x):
    return jax.nn.sigmoid(x)

def _layernorm(x, axis=-1, eps=1e-05):
    m = jnp.mean(x, axis=axis, keepdims=True)
    v = jnp.var(x, axis=axis, keepdims=True)
    return (x - m) / jnp.sqrt(v + eps)

def _scatter_add(tgt, idx, src, axis=0):
    return tgt.at[idx].add(src)

def _segment_sum(src, seg, n):
    return jax.ops.segment_sum(src, seg, n)
kernel_name = 'mk_adaln_d1_jaxref_r8_e789e4'

def setup_inputs(seed: int=0):
    np.random.seed(seed)
    _w = jnp.asarray

    def _L0_attn_setup():
        import jax, jax.numpy as jnp
        import numpy as np
        EMBED_DIM = 256
        NUM_HEADS = 16
        HEAD_DIM = EMBED_DIM // NUM_HEADS
        D_K = 128
        SCALE = 1.0 / float(np.sqrt(HEAD_DIM))
        LAYER_DEPTH = 6 / 12
        BATCH, SEQ = (2, 256)
        key = jax.random.key(seed)
        ks = jax.random.split(key, 8)
        return {'hidden_states': jax.random.normal(ks[0], (BATCH, SEQ, EMBED_DIM), jnp.float32), 'c_attn_w': jax.random.normal(ks[1], (EMBED_DIM, 3 * EMBED_DIM), jnp.float32) * 0.02, 'c_attn_b': jax.random.normal(ks[2], (3 * EMBED_DIM,), jnp.float32) * 0.02, 'c_proj_w': jax.random.normal(ks[3], (EMBED_DIM, EMBED_DIM), jnp.float32) * 0.02, 'c_proj_b': jax.random.normal(ks[4], (EMBED_DIM,), jnp.float32) * 0.02, 'cam_gate': jax.random.normal(ks[5], (D_K,), jnp.float32) * 0.1, 'cam_w0': jax.random.normal(ks[6], (1,), jnp.float32), 'cam_w1': jax.random.normal(ks[7], (1,), jnp.float32)}
    _L0_attn_in = _L0_attn_setup()

    def _L0_ffn_setup():
        import jax, jax.numpy as jnp
        import numpy as np
        N_EXPERTS = 8
        TOP_K = 2
        N_GROUP = 4
        TOPK_GROUP = 2
        ROUTED_SCALE = 1.0

        def _group_limited_topk(scores):
            T, N = scores.shape
            E = N // N_GROUP
            group_scores = scores.reshape(T, N_GROUP, E).max(axis=-1)
            _, gidx = jax.lax.top_k(group_scores, TOPK_GROUP)
            gmask = jax.nn.one_hot(gidx, N_GROUP, dtype=scores.dtype).sum(1)
            smask = jnp.repeat(gmask, E, axis=1)
            masked = jnp.where(smask > 0, scores, jnp.zeros((), scores.dtype))
            topk_w, topk_i = jax.lax.top_k(masked, TOP_K)
            return (topk_w, topk_i)
        key = jax.random.key(seed)
        ks = jax.random.split(key, 8)
        B, S, H, F, FS, N = (2, 128, 256, 176, 352, N_EXPERTS)
        std = jnp.float32(0.02)
        return {'hidden_states': jax.random.normal(ks[0], (B, S, H), jnp.float32), 'gate_weight': jax.random.normal(ks[1], (N, H), jnp.float32) * std, 'gate_w': jax.random.normal(ks[2], (N, F, H), jnp.float32) * std, 'up_w': jax.random.normal(ks[3], (N, F, H), jnp.float32) * std, 'down_w': jax.random.normal(ks[4], (N, H, F), jnp.float32) * std, 'sh_gate_w': jax.random.normal(ks[5], (FS, H), jnp.float32) * std, 'sh_up_w': jax.random.normal(ks[6], (FS, H), jnp.float32) * std, 'sh_down_w': jax.random.normal(ks[7], (H, FS), jnp.float32) * std}
    _L0_ffn_in = _L0_ffn_setup()
    _L0_c = _w((lambda *s: np.random.randn(*s).astype(np.float32) * 0.05)(8, 256))
    _L0_wmod = _w((lambda *s: np.random.randn(*s).astype(np.float32) * 0.05)(256, 6 * 256) * 256 ** (-0.5))
    _d = {'L0_attn_hidden_states': _L0_attn_in['hidden_states'], 'L0_attn_c_attn_w': _L0_attn_in['c_attn_w'], 'L0_attn_c_attn_b': _L0_attn_in['c_attn_b'], 'L0_attn_c_proj_w': _L0_attn_in['c_proj_w'], 'L0_attn_c_proj_b': _L0_attn_in['c_proj_b'], 'L0_attn_cam_gate': _L0_attn_in['cam_gate'], 'L0_attn_cam_w0': _L0_attn_in['cam_w0'], 'L0_attn_cam_w1': _L0_attn_in['cam_w1'], 'L0_ffn_gate_weight': _L0_ffn_in['gate_weight'], 'L0_ffn_gate_w': _L0_ffn_in['gate_w'], 'L0_ffn_up_w': _L0_ffn_in['up_w'], 'L0_ffn_down_w': _L0_ffn_in['down_w'], 'L0_ffn_sh_gate_w': _L0_ffn_in['sh_gate_w'], 'L0_ffn_sh_up_w': _L0_ffn_in['sh_up_w'], 'L0_ffn_sh_down_w': _L0_ffn_in['sh_down_w'], 'L0_c': _L0_c, 'L0_wmod': _L0_wmod}
    _x0 = _d['L0_attn_hidden_states']
    _d['L0_attn_hidden_states'] = jax.random.normal(jax.random.fold_in(jax.random.key(seed), 1), (8, 256, 256), dtype=_x0.dtype)
    del _x0
    return _d

def reference(L0_attn_hidden_states, L0_attn_c_attn_w, L0_attn_c_attn_b, L0_attn_c_proj_w, L0_attn_c_proj_b, L0_attn_cam_gate, L0_attn_cam_w0, L0_attn_cam_w1, L0_ffn_gate_weight, L0_ffn_gate_w, L0_ffn_up_w, L0_ffn_down_w, L0_ffn_sh_gate_w, L0_ffn_sh_up_w, L0_ffn_sh_down_w, L0_c, L0_wmod):

    def _L0_attn_ref(hidden_states, c_attn_w, c_attn_b, c_proj_w, c_proj_b, cam_gate, cam_w0, cam_w1):
        import jax, jax.numpy as jnp
        import numpy as np
        EMBED_DIM = 256
        NUM_HEADS = 16
        HEAD_DIM = EMBED_DIM // NUM_HEADS
        D_K = 128
        SCALE = 1.0 / float(np.sqrt(HEAD_DIM))
        LAYER_DEPTH = 6 / 12
        BATCH, SEQ = (2, 256)
        qkv = hidden_states @ c_attn_w + c_attn_b
        Q, K, V = jnp.split(qkv, 3, axis=2)
        attn_scores = jnp.einsum('bse,bte->bst', Q, K) * SCALE
        Q_cam, K_cam, V_cam = (Q[:, :, :D_K], K[:, :, :D_K], V[:, :, :D_K])
        base_A = jax.lax.stop_gradient(jax.nn.softmax(jnp.einsum('bsd,btd->bst', Q_cam, K_cam) * SCALE, axis=-1))
        layer_weight = jax.nn.sigmoid(cam_w0[0] + cam_w1[0] * LAYER_DEPTH)
        cam_ctx = jnp.einsum('bst,btd->bsd', base_A, V_cam)
        cam_bias = jnp.einsum('bsd,btd->bst', jnp.tanh(cam_ctx * cam_gate), K_cam)
        cam_bias = cam_bias * (SCALE * layer_weight)
        final_attn = jax.nn.softmax(attn_scores + cam_bias, axis=-1)
        context = jnp.einsum('bst,bte->bse', final_attn, V)
        output = context @ c_proj_w + c_proj_b
        return output

    def _L0_ffn_ref(hidden_states, gate_weight, gate_w, up_w, down_w, sh_gate_w, sh_up_w, sh_down_w):
        import jax, jax.numpy as jnp
        import numpy as np
        N_EXPERTS = 8
        TOP_K = 2
        N_GROUP = 4
        TOPK_GROUP = 2
        ROUTED_SCALE = 1.0

        def _group_limited_topk(scores):
            T, N = scores.shape
            E = N // N_GROUP
            group_scores = scores.reshape(T, N_GROUP, E).max(axis=-1)
            _, gidx = jax.lax.top_k(group_scores, TOPK_GROUP)
            gmask = jax.nn.one_hot(gidx, N_GROUP, dtype=scores.dtype).sum(1)
            smask = jnp.repeat(gmask, E, axis=1)
            masked = jnp.where(smask > 0, scores, jnp.zeros((), scores.dtype))
            topk_w, topk_i = jax.lax.top_k(masked, TOP_K)
            return (topk_w, topk_i)
        B, S, H = hidden_states.shape
        h = hidden_states.reshape(-1, H)
        logits = h.astype(jnp.float32) @ gate_weight.astype(jnp.float32).T
        scores = jax.nn.softmax(logits, axis=-1)
        topk_w, topk_i = _group_limited_topk(scores)
        topk_w = (topk_w * ROUTED_SCALE).astype(h.dtype)
        wmat = (jax.nn.one_hot(topk_i, N_EXPERTS, dtype=topk_w.dtype) * topk_w[..., None]).sum(axis=1)
        g = jnp.einsum('th,nfh->ntf', h, gate_w)
        u = jnp.einsum('th,nfh->ntf', h, up_w)
        e = jnp.einsum('ntf,nhf->nth', jax.nn.silu(g) * u, down_w)
        routed = jnp.einsum('nth,tn->th', e, wmat)
        sg = h @ sh_gate_w.T
        su = h @ sh_up_w.T
        shared = jax.nn.silu(sg) * su @ sh_down_w.T
        return (routed + shared).reshape(B, S, H)
    x = L0_attn_hidden_states
    mod = (_silu(L0_c) @ L0_wmod).reshape(L0_c.shape[0], 6, 1, -1)
    sa, ca, ga, sb, cb, gb = (mod[:, 0], mod[:, 1], mod[:, 2], mod[:, 3], mod[:, 4], mod[:, 5])
    ga = (2 * (ga >= 0) - 1) * jnp.maximum(jnp.abs(ga), 0.25)
    gb = (2 * (gb >= 0) - 1) * jnp.maximum(jnp.abs(gb), 0.25)
    h = _layernorm(x, axis=-1) * (1 + ca) + sa
    x = x + ga * _L0_attn_ref(h, L0_attn_c_attn_w, L0_attn_c_attn_b, L0_attn_c_proj_w, L0_attn_c_proj_b, L0_attn_cam_gate, L0_attn_cam_w0, L0_attn_cam_w1)
    h = _layernorm(x, axis=-1) * (1 + cb) + sb
    x = x + gb * _L0_ffn_ref(h, L0_ffn_gate_weight, L0_ffn_gate_w, L0_ffn_up_w, L0_ffn_down_w, L0_ffn_sh_gate_w, L0_ffn_sh_up_w, L0_ffn_sh_down_w)
    return x

_drawn_inputs = setup_inputs


def setup_inputs(seed=0):
    import zlib

    import numpy as np

    out = dict(_drawn_inputs(seed))
    spreads = {}
    factors = {'L0_attn_c_attn_w': 8.0,
     'L0_attn_c_attn_b': 8.0,
     'L0_attn_c_proj_w': 8.0,
     'L0_attn_c_proj_b': 8.0,
     'L0_attn_cam_gate': 8.0,
     'L0_ffn_gate_weight': 8.0,
     'L0_ffn_gate_w': 8.0,
     'L0_ffn_up_w': 8.0,
     'L0_ffn_down_w': 8.0,
     'L0_ffn_sh_gate_w': 8.0,
     'L0_ffn_sh_up_w': 8.0,
     'L0_ffn_sh_down_w': 8.0,
     'L0_c': 7.549,
     'L0_wmod': 7.431}
    for name, (base, spread) in spreads.items():
        noise = np.random.default_rng([zlib.crc32(name.encode()), seed]).standard_normal(out[name].shape)
        drawn = base * np.exp(spread * noise) if base else spread * noise
        out[name] = jnp.asarray(drawn.astype(out[name].dtype))
    for name, factor in factors.items():
        out[name] = (out[name] * factor).astype(out[name].dtype)
    return out
```

```python
from contextlib import ExitStack

import numpy as np

import concourse.bass as bass
from concourse import mybir

ALU = mybir.AluOpType
ACT = mybir.ActivationFunctionType
F32 = mybir.dt.float32
F32R = mybir.dt.float32r
BF16 = mybir.dt.bfloat16
U32 = mybir.dt.uint32
I32 = mybir.dt.int32
AX = mybir.AxisListType
ds = bass.ds

P = 128
EPS = 1e-5
GUARD = 0.25
HEAD_DIM = 16
SCALE = float(HEAD_DIM) ** -0.5
LAYER_DEPTH = 0.5
META = 4
SKIP = 1 << 20


def adaln_block(nc, x_in, w_qkv, b_cols, w_proj, b_proj, gate_col, cam_w0, cam_w1,
                router_t, gu_t, down_t, sh_gu_t, sh_down_t, c_t, w_mod, out):
    B, S, D = x_in.shape
    NE = router_t.shape[1]
    F = down_t.shape[1]
    FS = sh_down_t.shape[0]
    KD = D // P
    TT = S // P
    T = B * S
    NPAIR = B // 2
    NT = (2 * T + NE * (P - 1)) // P
    REGION = T + P
    ROW = D + META
    FH = F // 2
    FT = [(f, min(P, FS - f)) for f in range(0, FS, P)]
    UNR = 3
    assert D == KD * P == 256 and S == TT * P == 256 and NT % UNR == 0 and F <= 256

    with ExitStack() as ctx:
        def sb(name, shape, dt=F32):
            return ctx.enter_context(nc.sbuf_tensor(name, shape, dt))

        def hilo(name, shape):
            return sb(name + "_hi", shape, F32R), sb(name + "_lo", shape, F32R)

        def sem(name):
            return ctx.enter_context(nc.semaphore(name))

        s_c_in = sem("c_in")
        s_wmod_in = sem("wmod_in")
        s_wqkv_in = sem("wqkv_in")
        s_wproj_in = sem("wproj_in")
        s_wrt_in = sem("wrt_in")
        s_wsgu_in = sem("wsgu_in")
        s_wsd_in = sem("wsd_in")
        s_mrow_ready = sem("mrow_ready")
        s_modrow_out = sem("modrow_out")
        s_const = sem("const")
        s_ident_ready = sem("ident_ready")
        s_cols_in = sem("cols_in")
        s_c_exp = sem("c_exp")
        s_lw_sum = sem("lw_sum")
        s_lw_exp = sem("lw_exp")
        s_whi = sem("whi")
        s_kscaled = sem("kscaled")
        s_c_chain = sem("c_chain")
        s_silu_c = sem("silu_c")
        s_cols_ready = sem("cols_ready")
        s_wlo = sem("wlo")
        s_mod_mm = sem("mod_mm")
        s_mod_copied = sem("mod_copied")
        s_guard = sem("guard")
        s_modT = sem("modT")
        s_sacol_ready = sem("sacol_ready")
        s_xn_ready = sem("xn_ready")
        s_xt_done = sem("xt_done")
        s_h_lo = sem("h_lo")
        s_qk_hi = sem("qk_hi")
        s_qk_lo = sem("qk_lo")
        s_qk_done = sem("qk_done")
        s_v_done = sem("v_done")
        s_qp_hi = sem("qp_hi")
        s_qp_lo = sem("qp_lo")
        s_s2_done = sem("s2_done")
        s_s1_done = sem("s1_done")
        s_norm2 = sem("norm2")
        s_norm1 = sem("norm1")
        s_pt2_done = sem("pt2_done")
        s_pt1_done = sem("pt1_done")
        s_pt2_hi = sem("pt2_hi")
        s_pt2_lo = sem("pt2_lo")
        s_pt1_hi = sem("pt1_hi")
        s_pt1_lo = sem("pt1_lo")
        s_v_hi = sem("v_hi")
        s_v_lo = sem("v_lo")
        s_c2_done = sem("c2_done")
        s_c1_done = sem("c1_done")
        s_ctx_hi = sem("ctx_hi")
        s_ctx_lo = sem("ctx_lo")
        s_o_done = sem("o_done")
        s_h2_ready = sem("h2_ready")
        s_h2t_done = sem("h2t_done")
        s_h2_hi = sem("h2_hi")
        s_h2_lo = sem("h2_lo")
        s_lg_done = sem("lg_done")
        s_lg_copied = sem("lg_copied")
        s_lt_done = sem("lt_done")
        s_both_ready = sem("both_ready")
        s_rank_done = sem("rank_done")
        s_max2 = sem("max2")
        s_max1 = sem("max1")
        s_exp2 = sem("exp2")
        s_exp1 = sem("exp1")
        s_ht_ready = sem("ht_ready")
        s_tanh_done = sem("tanh_done")
        s_rl2 = sem("rl2")
        s_rl1 = sem("rl1")
        s_h_hi = sem("h_hi")
        s_qf_ready = sem("qf_ready")
        s_qp_ready = sem("qp_ready")
        s_xg_ready = sem("xg_ready")
        s_y_ready = sem("y_ready")
        s_x1_ready = sem("x1_ready")
        s_ln1_chain = sem("ln1_chain")
        s_ln2_chain = sem("ln2_chain")
        s_xa0_in = sem("xa0_in")
        s_xa1_in = sem("xa1_in")
        s_xn2_ready = sem("xn2_ready")
        s_rt_a = sem("rt_a")
        s_rt_exp = sem("rt_exp")
        s_rt_b = sem("rt_b")
        s_rt_c = sem("rt_c")
        s_rt_pos = sem("rt_pos")
        s_slots_ready = sem("slots_ready")
        s_xr0_in = sem("xr0_in")
        s_xr1_in = sem("xr1_in")
        s_mb0_in = sem("mb0_in")
        s_mb1_in = sem("mb1_in")
        s_sc0 = sem("sc0")
        s_sc1 = sem("sc1")
        s_h2_chain = sem("h2_chain")
        s_base_zero = sem("base_zero")
        s_x1_out0 = sem("x1_out0")
        s_x1_out1 = sem("x1_out1")
        s_pad_ready = sem("pad_ready")
        s_pad_out = sem("pad_out")
        s_pad_chain = sem("pad_chain")
        s_tab = sem("tab")
        s_table_ready = sem("table_ready")
        s_res_ready = sem("res_ready")
        s_x1b0_in = sem("x1b0_in")
        s_x1b1_in = sem("x1b1_in")
        s_gbb0_in = sem("gbb0_in")
        s_gbb1_in = sem("gbb1_in")
        s_act_mul = sem("act_mul")
        s_shgu_done = sem("shgu_done")
        s_silu_done = sem("silu_done")
        s_a_lo = sem("a_lo")
        s_a_hi = sem("a_hi")
        s_og_ready = sem("og_ready")
        s_shdn_done = sem("shdn_done")
        s_ea_ready = sem("ea_ready")
        s_tile0_in = sem("tile0_in")
        s_tile1_in = sem("tile1_in")
        s_tile2_in = sem("tile2_in")
        s_tile3_in = sem("tile3_in")
        s_tile0_out = sem("tile0_out")
        s_tile1_out = sem("tile1_out")
        s_ext_done = sem("ext_done")
        s_ex_lo = sem("ex_lo")
        s_egu_done = sem("egu_done")
        s_eat_done = sem("eat_done")
        s_ea_lo = sem("ea_lo")
        s_edn_done = sem("edn_done")
        s_ex_hi = sem("ex_hi")
        s_esilu = sem("esilu")
        s_ea_hi = sem("ea_hi")
        s_ey_ready = sem("ey_ready")
        s_esecond = sem("esecond")
        s_emeta = sem("emeta")
        s_est_free = sem("est_free")
        s_est0_in = sem("est0_in")
        s_est1_in = sem("est1_in")
        s_y0_in = sem("y0_in")
        s_y1_in = sem("y1_in")
        s_fin_ready = sem("fin_ready")
        s_stored = sem("stored")
        s_ew_hi = sem("ew_hi")
        s_fin_sum = sem("fin_sum")
        s_fin_mul = sem("fin_mul")

        modrow = nc.dram_tensor("modrow", (B, 5 * D), F32, kind="Internal").ap()
        x1_dram = nc.dram_tensor("x1_dram", (B, S, D), F32, kind="Internal").ap()
        routed_in = nc.dram_tensor("routed_in", (NE * REGION, ROW), F32, kind="Internal").ap()
        routed_out = nc.dram_tensor("routed_out", (2 * T, D), F32, kind="Internal").ap()

        ident = sb("ident", [P, P])
        before = sb("before", [P, P], BF16)
        ones = sb("ones", [P, P], BF16)
        lower = sb("lower", [P, NE, NE])
        token_id = sb("token_id", [P, B * TT])
        eidx = sb("eidx", [P, NE])
        erow = sb("erow", [P, NE])
        step128 = sb("step128", [P, T // P])
        tidx = sb("tidx", [P, NT])
        cols = sb("cols", [P, 3 * KD + 2])
        lw = sb("lw", [P, 4])

        wrt = hilo("wrt", [P, KD, NE])
        wsgu = hilo("wsgu", [P, KD, 2 * FS])
        wsd = hilo("wsd", [P, len(FT), D])
        h2T = hilo("h2T", [P, KD, T])

        sacol = sb("sacol", [P, 2 * KD, B])

        eid_f = sb("eid_f", [P, NT])
        tile_u = sb("tile_u", [1, 2, NT], I32)
        pad_u = sb("pad_u", [1, NE], I32)

        attention_weights = ctx.enter_context(ExitStack())

        def hilo_attention(name, shape):
            return tuple(attention_weights.enter_context(nc.sbuf_tensor(name + x, shape, F32R)) for x in ("_hi", "_lo"))

        wqkv = hilo_attention("wqkv", [P, KD, 3 * D])
        wproj = hilo_attention("wproj", [P, KD, D])

        psum = [ctx.enter_context(nc.psum_tensor(f"bank{i}", [P, 512], F32)) for i in range(8)]

        def parts(t, *idx):
            return t[0][idx], t[1][idx]

        def mm3(pe, out_ap, l, r, start, stop):
            pe.matmul(out_ap, l[1], r[0], start=start, stop=False)
            pe.matmul(out_ap, l[0], r[1], start=False, stop=False)
            return pe.matmul(out_ap, l[0], r[0], start=False, stop=stop)

        with ExitStack() as early:
            def tb(name, shape, dt=F32):
                return early.enter_context(nc.sbuf_tensor(name, shape, dt))

            wmod_s = tb("wmod_s", [P, KD, 6 * D])
            cT = tb("cT", [P, KD, B])
            cS = tb("cS", [P, KD, B])
            stage = tb("stage", [P, 4 * D * KD + KD * NE + KD * 2 * FS + len(FT) * D])
            modS = tb("modS", [B, 6 * D])
            mrow = tb("mrow", [B, 5, D])
            gsgn = tb("gsgn", [B, 2, D])
            bprow = tb("bprow", [B, D])
            at, spans = 0, {}
            for name, n in (("qkv", KD * 3 * D), ("proj", KD * D), ("rt", KD * NE), ("sgu", KD * 2 * FS), ("sd", len(FT) * D)):
                spans[name] = (at, at + n)
                at += n

            def staged(name):
                return stage[:, spans[name][0]:spans[name][1]]

            with nc.Block() as block:
                @block.sync
                def _(sp):
                    sp.dma_start(cT[:], c_t.rearrange("(k p) b -> p k b", p=P)).then_inc(s_c_in, 16)
                    sp.dma_start(wmod_s[:], w_mod.rearrange("(k p) n -> p k n", p=P)).then_inc(s_wmod_in, 16)
                    sp.dma_start(staged("qkv").rearrange("p (k n) -> p k n", k=KD),
                                 w_qkv.rearrange("(k p) n -> p k n", p=P)).then_inc(s_wqkv_in, 16)
                    sp.dma_start(staged("proj").rearrange("p (k n) -> p k n", k=KD),
                                 w_proj.rearrange("(k p) n -> p k n", p=P)).then_inc(s_wproj_in, 16)
                    sp.dma_start(staged("rt").rearrange("p (k n) -> p k n", k=KD),
                                 router_t.rearrange("(k p) n -> p k n", p=P)).then_inc(s_wrt_in, 16)
                    sp.dma_start(staged("sgu").rearrange("p (k n) -> p k n", k=KD),
                                 sh_gu_t.rearrange("(k p) n -> p k n", p=P)).then_inc(s_wsgu_in, 16)
                    for j, (f, m) in enumerate(FT):
                        sp.dma_start(staged("sd").rearrange("p (k n) -> p k n", k=len(FT))[0:m, j, :],
                                     sh_down_t[f:f + m, :]).then_inc(s_wsd_in, 16)
                    sp.wait_ge(s_mrow_ready, 1)
                    sp.dma_start(modrow, mrow[:].rearrange("b j d -> b (j d)")).then_inc(s_modrow_out, 16)
                    sp.wait_ge(s_modrow_out, 16)

                @block.gpsimd
                def _(pool):
                    pool.memset(ident[:], 0.0).then_inc(s_const, 1)
                    pool.memset(before[:], 0.0).then_inc(s_const, 1)
                    pool.wait_ge(s_const, 2)
                    pool.affine_select(out=ident[:], in_=ident[:], compare_op=ALU.not_equal, fill=1.0,
                                       base=0, pattern=[[-1, P]], channel_multiplier=1).then_inc(s_ident_ready, 1)
                    pool.affine_select(out=before[:], in_=before[:], compare_op=ALU.is_ge, fill=1.0,
                                       base=0, pattern=[[-1, P]], channel_multiplier=1).then_inc(s_const, 1)
                    pool.memset(ones[:], 1.0).then_inc(s_const, 1)
                    pool.memset(lower[:], 0.0).then_inc(s_const, 1)
                    pool.wait_ge(s_const, 5)
                    for j in range(1, NE):
                        pool.memset(lower[:, j, 0:j], 1.0).then_inc(s_const, 1)
                    pool.iota(token_id[:], pattern=[[P, B * TT]], base=0, channel_multiplier=1,
                              allow_small_or_imprecise_dtypes=True).then_inc(s_const, 1)
                    for t, step in ((eidx, 1), (erow, REGION), (step128, P), (tidx, 1)):
                        pool.iota(t[:], pattern=[[step, t.shape[1]]], base=0, channel_multiplier=0,
                                  allow_small_or_imprecise_dtypes=True).then_inc(s_const, 1)
                    pool.wait_ge(s_const, 5 + NE - 1 + 5)

                @block.scalar
                def _(act):
                    act.dma_start(cols[:, 0:3 * KD], b_cols).then_inc(s_cols_in, 16)
                    act.dma_start(cols[:, 3 * KD:3 * KD + 1], gate_col).then_inc(s_cols_in, 16)
                    act.dma_start(lw[:, 0:1], cam_w0.partition_broadcast(P)).then_inc(s_cols_in, 16)
                    act.dma_start(lw[:, 1:2], cam_w1.partition_broadcast(P)).then_inc(s_cols_in, 16)
                    act.dma_start(bprow[:], b_proj.partition_broadcast(B)).then_inc(s_cols_in, 16)
                    act.wait_ge(s_c_in, 16)
                    act.activation(cS[:], cT[:], ACT.Exp, scale=-1.0).then_inc(s_c_exp, 1)
                    act.wait_ge(s_lw_sum, 1)
                    act.activation(lw[:, 3:4], lw[:, 2:3], ACT.Exp, scale=-1.0).then_inc(s_lw_exp, 1)
                    act.wait_ge(s_wqkv_in, 16)
                    q3 = staged("qkv").rearrange("p (k n) -> p k n", k=KD)
                    act.activation(wqkv[0][:, :, 0:D], q3[:, :, 0:D], ACT.Copy).then_inc(s_whi, 1)
                    act.wait_ge(s_kscaled, 1)
                    act.activation(wqkv[0][:, :, D:3 * D], q3[:, :, D:3 * D], ACT.Copy).then_inc(s_whi, 1)
                    for src, name, dst in ((s_wproj_in, "proj", wproj), (s_wrt_in, "rt", wrt), (s_wsgu_in, "sgu", wsgu)):
                        act.wait_ge(src, 16)
                        act.activation(dst[0][:], staged(name).rearrange("p (k n) -> p k n", k=KD),
                                       ACT.Copy).then_inc(s_whi, 1)
                    act.wait_ge(s_wsd_in, 16 * len(FT))
                    d3 = staged("sd").rearrange("p (k n) -> p k n", k=len(FT))
                    for j, (f, m) in enumerate(FT):
                        act.activation(wsd[0][0:m, j, :], d3[0:m, j, :], ACT.Copy).then_inc(s_whi, 1)

                @block.vector
                def _(dve):
                    dve.wait_ge(s_c_exp, 1)
                    dve.tensor_scalar(cS[:], cS[:], 1.0, None, ALU.add).then_inc(s_c_chain, 1)
                    dve.wait_ge(s_c_chain, 1)
                    dve.reciprocal(cS[:], cS[:]).then_inc(s_c_chain, 1)
                    dve.wait_ge(s_c_chain, 2)
                    dve.tensor_tensor(cS[:], cS[:], cT[:], ALU.mult).then_inc(s_silu_c, 1)
                    dve.wait_ge(s_cols_in, 16 * 5)
                    dve.scalar_tensor_tensor(lw[:, 2:3], lw[:, 1:2], LAYER_DEPTH, lw[:, 0:1],
                                             ALU.mult, ALU.add).then_inc(s_lw_sum, 1)
                    dve.tensor_scalar(cols[:, KD:2 * KD], cols[:, KD:2 * KD], SCALE, None, ALU.mult).then_inc(s_cols_ready, 1)
                    dve.tensor_tensor(cols[:, 3 * KD + 1:3 * KD + 2], cols[:, 3 * KD:3 * KD + 1],
                                      cols[:, 2 * KD:2 * KD + 1], ALU.mult).then_inc(s_cols_ready, 1)
                    dve.wait_ge(s_lw_exp, 1)
                    dve.tensor_scalar(lw[:, 3:4], lw[:, 3:4], 1.0, None, ALU.add).then_inc(s_c_chain, 1)
                    dve.wait_ge(s_c_chain, 3)
                    dve.reciprocal(lw[:, 3:4], lw[:, 3:4]).then_inc(s_cols_ready, 1)
                    q3 = staged("qkv").rearrange("p (k n) -> p k n", k=KD)
                    dve.wait_ge(s_wqkv_in, 16)
                    dve.tensor_scalar(q3[:, :, D:2 * D], q3[:, :, D:2 * D], SCALE, None, ALU.mult).then_inc(s_kscaled, 1)
                    dve.wait_ge(s_whi, 1)
                    dve.tensor_tensor(wqkv[1][:, :, 0:D], q3[:, :, 0:D], wqkv[0][:, :, 0:D].bitcast(F32),
                                      ALU.subtract).then_inc(s_wlo, 1)
                    dve.wait_ge(s_kscaled, 1)
                    dve.wait_ge(s_whi, 2)
                    dve.tensor_tensor(wqkv[1][:, :, D:3 * D], q3[:, :, D:3 * D], wqkv[0][:, :, D:3 * D].bitcast(F32),
                                      ALU.subtract).then_inc(s_wlo, 1)
                    dve.wait_ge(s_mod_mm, 1)
                    for j in range(3):
                        dve.tensor_copy(modS[:, 512 * j:512 * (j + 1)], psum[j][0:B, :]).then_inc(s_mod_copied, 1)
                    dve.wait_ge(s_mod_copied, 3)
                    for n, g in enumerate((2, 5)):
                        src = modS[:, g * D:(g + 1) * D]
                        dve.tensor_scalar(gsgn[:, n, :], src, 0.0, 2.0, ALU.is_ge, ALU.mult).then_inc(s_guard, 1)
                        dve.scalar_tensor_tensor(mrow[:, 4 * n, :], src, -1.0, src, ALU.mult, ALU.max).then_inc(s_guard, 1)
                    dve.wait_ge(s_guard, 4)
                    for n in range(2):
                        dve.tensor_scalar(mrow[:, 4 * n, :], mrow[:, 4 * n, :], GUARD, None, ALU.max).then_inc(s_guard, 1)
                    dve.wait_ge(s_guard, 6)
                    for n in range(2):
                        dve.scalar_tensor_tensor(mrow[:, 4 * n, :], gsgn[:, n, :], 1.0, mrow[:, 4 * n, :],
                                                 ALU.subtract, ALU.mult).then_inc(s_guard, 1)
                    dve.tensor_scalar(mrow[:, 2, :], modS[:, 4 * D:5 * D], 1.0, None, ALU.add).then_inc(s_guard, 1)
                    dve.tensor_copy(mrow[:, 3, :], modS[:, 3 * D:4 * D]).then_inc(s_guard, 1)
                    dve.wait_ge(s_guard, 10)
                    dve.tensor_tensor(mrow[:, 1, :], mrow[:, 0, :], bprow[:], ALU.mult).then_inc(s_mrow_ready, 1)
                    dve.wait_ge(s_modT, 1)
                    mt = psum[3][:, 0:2 * KD * B].rearrange("p (j b) -> p j b", b=B)
                    dve.tensor_copy(sacol[:, 0:KD, :], mt[:, 0:KD, :]).then_inc(s_sacol_ready, 1)
                    dve.tensor_scalar(sacol[:, KD:2 * KD, :], mt[:, KD:2 * KD, :], 1.0, None, ALU.add).then_inc(s_sacol_ready, 1)
                    for n, (name, dst) in enumerate((("proj", wproj), ("rt", wrt), ("sgu", wsgu))):
                        dve.wait_ge(s_whi, 3 + n)
                        dve.tensor_tensor(dst[1][:], staged(name).rearrange("p (k n) -> p k n", k=KD),
                                          dst[0][:].bitcast(F32), ALU.subtract).then_inc(s_wlo, 1)
                    d3 = staged("sd").rearrange("p (k n) -> p k n", k=len(FT))
                    for j, (f, m) in enumerate(FT):
                        dve.wait_ge(s_whi, 6 + j)
                        dve.tensor_tensor(wsd[1][0:m, j, :], d3[0:m, j, :], wsd[0][0:m, j, :].bitcast(F32),
                                          ALU.subtract).then_inc(s_wlo, 1)

                @block.tensor
                def _(pe):
                    pe.wait_ge(s_silu_c, 1)
                    pe.wait_ge(s_wmod_in, 16)
                    for j in range(3):
                        for k in range(KD):
                            last = pe.matmul(psum[j][0:B, :], cS[:, k, :], wmod_s[:, k, 512 * j:512 * (j + 1)],
                                             start=(k == 0), stop=(k == KD - 1))
                    last.then_inc(s_mod_mm, 1)
                    pe.wait_ge(s_mod_copied, 3)
                    pe.wait_ge(s_ident_ready, 1)
                    for j in range(2 * KD):
                        last = pe.transpose(psum[3][:, j * B:(j + 1) * B], modS[:, j * P:(j + 1) * P], ident[0:B, 0:B])
                    last.then_inc(s_modT, 1)

        with ExitStack() as attention:
            def tb(name, shape, dt=F32):
                return attention.enter_context(nc.sbuf_tensor(name, shape, dt))

            def two(name, shape, dt=F32):
                return [tb(f"{name}{u}", shape, dt) for u in range(2)]

            def two_hilo(name, shape):
                return [(tb(f"{name}{u}_hi", shape, F32R), tb(f"{name}{u}_lo", shape, F32R)) for u in range(2)]

            xa = two("xa", [P, TT, D])
            xr = two("xr", [P, TT, D])
            mb = two("mb", [P, 4, D])
            ht = two("ht", [P, KD, S])
            hT = two_hilo("hT", [P, KD, S])
            QT = two_hilo("QT", [P, KD, S])
            KT = two_hilo("KT", [P, KD, S])
            VV = two_hilo("VV", [P, TT, D])
            qf = two("qf", [P, S])
            th = two("th", [P, S])
            pr = two("pr", [P, TT, S])
            PT = two_hilo("PT", [P, KD, S])
            h2 = two("h2", [P, TT, ROW])
            mv1 = tb("mv1", [P, 2 * TT, 2])
            mv2 = tb("mv2", [P, 2 * TT, 2])
            bst1 = tb("bst1", [P, 2 * TT, 6])
            bst2 = tb("bst2", [P, 2 * TT, 6])
            rs1 = tb("rs1", [P, 2 * TT])
            rs2 = tb("rs2", [P, 2 * TT])
            nt1 = tb("nt1", [P, 2 * TT])
            nm = two("nm", [P, 2, TT])
            ls = two("ls", [P, 2, TT])
            rl = two("rl", [P, 2, TT])
            lg = two("lg", [NE, S])
            NR = 2 * TT
            r_sc = tb("r_sc", [P, NR, NE])
            r_mx = tb("r_mx", [P, NR])
            r_gm = tb("r_gm", [P, NR, NE // 2])
            r_gt = tb("r_gt", [P, NR, NE, NE])
            r_eq = tb("r_eq", [P, NR, NE, NE])
            r_rank = tb("r_rank", [P, NR, NE])
            r_sel = tb("r_sel", [P, 2, NR, NE])
            r_both = tb("r_both", [P, NR, NE], BF16)
            r_pos = tb("r_pos", [P, NR, NE])
            r_base = tb("r_base", [P, NR + 1, NE])
            r_tmp = tb("r_tmp", [P, 2, NR, NE])
            r_slot = tb("r_slot", [P, 2, NR])
            r_w = tb("r_w", [P, 2, NR])
            slot_u = tb("slot_u", [P, 2, NR], U32)
            r_end = tb("r_end", [P, NE, T // P])
            r_tiles = tb("r_tiles", [P, NE])
            r_ends = tb("r_ends", [P, NE])
            r_done = tb("r_done", [P, NT, NE])
            r_tab = tb("r_tab", [P, 4, NT])
            pad = tb("pad", [P, ROW])

            Sb, TR, CO, QK = psum[0:2], psum[2:4], psum[4:6], psum[6:8]

            def bank(t, a=2):
                return t[:, :].rearrange("p (a n) -> p a n", a=a)

            wq_ = lambda k, m: parts(wqkv, slice(None), k, slice(m * P, (m + 1) * P))

            def pe_xt(pe, b, u):
                pe.wait_ge(s_xn_ready, b + 1)
                for d in range(KD):
                    for t in range(TT):
                        last = pe.transpose(TR[u][:, d * S + t * P:d * S + (t + 1) * P],
                                            xa[u][:, t, d * P:(d + 1) * P], ident[:])
                last.then_inc(s_xt_done, 1)

            def pe_qk(pe, b, u):
                pe.wait_ge(s_h_lo, b + 1)
                if u == 1:
                    pe.wait_ge(s_qk_hi, b)
                    pe.wait_ge(s_qk_lo, b)
                for half, dst in enumerate(QK):
                    for m in range(KD):
                        for k in range(KD):
                            last = mm3(pe, dst[:, m * S:(m + 1) * S], wq_(k, half * KD + m),
                                       parts(hT[u], slice(None), k), k == 0, k == KD - 1)
                    last.then_inc(s_qk_done, 1)

            def pe_v(pe, b, u):
                for t in range(TT):
                    for k in range(KD):
                        last = mm3(pe, QK[u][:, t * D:(t + 1) * D],
                                   parts(hT[u], slice(None), k, slice(t * P, (t + 1) * P)),
                                   parts(wqkv, slice(None), k, slice(2 * D, 3 * D)), k == 0, k == KD - 1)
                last.then_inc(s_v_done, 1)

            def pe_scores(pe, b, u, second):
                if second:
                    pe.wait_ge(s_qp_hi, b + 1)
                    pe.wait_ge(s_qp_lo, b + 1)
                else:
                    pe.wait_ge(s_qk_hi, b + 1)
                    pe.wait_ge(s_qk_lo, b + 1)
                ks = KD if second else 1
                for t in range(TT):
                    for k in range(ks):
                        last = mm3(pe, Sb[u][:, t * S:(t + 1) * S],
                                   parts(QT[u], slice(None), k, slice(t * P, (t + 1) * P)),
                                   parts(KT[u], slice(None), k), k == 0, k == ks - 1)
                last.then_inc(s_s2_done if second else s_s1_done, 1)

            def pe_pt(pe, b, u, second):
                pe.wait_ge(s_norm2 if second else s_norm1, b + 1)
                for k in range(TT):
                    for t in range(TT):
                        last = pe.transpose(TR[u][:, k * S + t * P:k * S + (t + 1) * P],
                                            pr[u][:, t, k * P:(k + 1) * P], ident[:])
                last.then_inc(s_pt2_done if second else s_pt1_done, 1)

            def pe_ctx(pe, b, u, second):
                if second:
                    pe.wait_ge(s_pt2_hi, b + 1)
                    pe.wait_ge(s_pt2_lo, b + 1)
                else:
                    pe.wait_ge(s_pt1_hi, b + 1)
                    pe.wait_ge(s_pt1_lo, b + 1)
                    pe.wait_ge(s_v_hi, b + 1)
                    pe.wait_ge(s_v_lo, b + 1)
                for m in range(KD if second else 1):
                    for k in range(TT):
                        last = mm3(pe, CO[u][:, m * S:(m + 1) * S],
                                   parts(VV[u], slice(None), k, slice(m * P, (m + 1) * P)),
                                   parts(PT[u], slice(None), k), k == 0, k == TT - 1)
                last.then_inc(s_c2_done if second else s_c1_done, 1)

            def pe_out(pe, b, u):
                pe.wait_ge(s_ctx_hi, b + 1)
                pe.wait_ge(s_ctx_lo, b + 1)
                for t in range(TT):
                    for m in range(KD):
                        last = mm3(pe, CO[u][:, t * D:(t + 1) * D],
                                   parts(PT[u], slice(None), m, slice(t * P, (t + 1) * P)),
                                   parts(wproj, slice(None), m), m == 0, m == KD - 1)
                last.then_inc(s_o_done, 1)

            def pe_h2t(pe, b, u):
                pe.wait_ge(s_h2_ready, b + 1)
                for d in range(KD):
                    for t in range(TT):
                        last = pe.transpose(TR[u][:, d * S + t * P:d * S + (t + 1) * P],
                                            h2[u][:, t, d * P:(d + 1) * P], ident[:])
                last.then_inc(s_h2t_done, 1)

            def pe_logits(pe, b, u):
                pe.wait_ge(s_h2_hi, b + 1)
                pe.wait_ge(s_h2_lo, b + 1)
                for k in range(KD):
                    last = mm3(pe, CO[u][0:NE, S:2 * S], parts(wrt, slice(None), k),
                               parts(h2T, slice(None), k, ds(b * S, S)), k == 0, k == KD - 1)
                last.then_inc(s_lg_done, 1)

            LOG = CO[0][:, S:S + NR * NE]
            RNK = CO[0][:, S + 64:S + 64 + NR * NE]
            TOT = CO[0][:, S + 128:S + 128 + NR * NE]

            def pe_logits_t(pe, p):
                pe.wait_ge(s_ident_ready, 1)
                pe.wait_ge(s_lg_copied, 2 * p + 2)
                for u in range(2):
                    for t in range(TT):
                        j = u * TT + t
                        last = pe.transpose(LOG[:, j * NE:(j + 1) * NE], lg[u][:, t * P:(t + 1) * P],
                                            ident[0:NE, 0:NE])
                last.then_inc(s_lt_done, 1)

            def pe_rank(pe, p):
                pe.wait_ge(s_both_ready, p + 1)
                rhs = r_both[:].rearrange("p t e -> p (t e)")
                pe.matmul(RNK, before[:], rhs, start=True, stop=True)
                pe.matmul(TOT, ones[:], rhs, start=True, stop=True).then_inc(s_rank_done, 1)

            def act_exp(act, b, u, second):
                act.wait_ge(s_max2 if second else s_max1, b + 1)
                i = int(second)
                for t in range(TT):
                    last = act.activation(pr[u][:, t, :], Sb[u][:, t * S:(t + 1) * S], ACT.Exp,
                                          bias=nm[u][:, i, t:t + 1], accum_out=ls[u][:, i, t:t + 1])
                last.then_inc(s_exp2 if second else s_exp1, 1)

            def act_copy(act, ready, b, dst, src, done):
                act.wait_ge(ready, b + 1)
                act.activation(dst, src, ACT.Copy).then_inc(done, 1)

            def act_h(act, b, u):
                act.wait_ge(s_xt_done, b + 1)
                for d in range(KD):
                    last = act.activation(ht[u][:, d, :], TR[u][:, d * S:(d + 1) * S], ACT.Identity,
                                          scale=sacol[:, KD + d, ds(b, 1)], bias=sacol[:, d, ds(b, 1)])
                last.then_inc(s_ht_ready, 1)

            def act_qk(act, b, u):
                for half, dst in enumerate((QT, KT)):
                    act.wait_ge(s_qk_done, 2 * b + 1 + half)
                    for m in range(KD):
                        last = act.activation(dst[u][0][:, m, :], QK[half][:, m * S:(m + 1) * S], ACT.Identity,
                                              bias=cols[:, half * KD + m:half * KD + m + 1])
                last.then_inc(s_qk_hi, 1)

            def act_tanh(act, b, u):
                act.wait_ge(s_c1_done, b + 1)
                act.activation(th[u][:], CO[u][:, 0:S], ACT.Tanh, scale=cols[:, 3 * KD:3 * KD + 1],
                               bias=cols[:, 3 * KD + 1:3 * KD + 2]).then_inc(s_tanh_done, 1)

            def act_ctx(act, b, u):
                act.wait_ge(s_c2_done, b + 1)
                for m in range(KD):
                    last = act.activation(PT[u][0][:, m, :], CO[u][:, m * S:(m + 1) * S], ACT.Identity,
                                          bias=cols[:, 2 * KD + m:2 * KD + m + 1])
                last.then_inc(s_ctx_hi, 1)

            def dve_max(dve, b, u, second):
                dve.wait_ge(s_s2_done if second else s_s1_done, b + 1)
                dve.tensor_reduce(nm[u][:, int(second), :], bank(Sb[u]), AX.X, ALU.max,
                                  negate=True).then_inc(s_max2 if second else s_max1, 1)

            def dve_norm(dve, b, u, second):
                i = int(second)
                dve.wait_ge(s_exp2 if second else s_exp1, b + 1)
                dve.reciprocal(rl[u][:, i, :], ls[u][:, i, :]).then_inc(s_rl2 if second else s_rl1, 1)
                dve.wait_ge(s_rl2 if second else s_rl1, b + 1)
                for t in range(TT):
                    last = dve.tensor_scalar(pr[u][:, t, :], pr[u][:, t, :], rl[u][:, i, t:t + 1], None, ALU.mult)
                last.then_inc(s_norm2 if second else s_norm1, 1)

            def dve_lo(dve, ready, b, src, hi, lo, done):
                dve.wait_ge(ready, b + 1)
                dve.tensor_tensor(lo, src, hi.bitcast(F32), ALU.subtract).then_inc(done, 1)

            def dve_h(dve, b, u):
                dve.wait_ge(s_ht_ready, b + 1)
                dve.tensor_copy(hT[u][0][:], ht[u][:]).then_inc(s_h_hi, 1)
                dve.wait_ge(s_h_hi, b + 1)
                dve.tensor_tensor(hT[u][1][:], ht[u][:], hT[u][0][:].bitcast(F32), ALU.subtract).then_inc(s_h_lo, 1)

            def biased_lo(dve, dst, src, bias, m):
                return dve.scalar_tensor_tensor(dst[1][:, m, :], src[:, m * S:(m + 1) * S], bias,
                                                dst[0][:, m, :].bitcast(F32), ALU.add, ALU.subtract)

            def dve_qk(dve, b, u):
                dve.wait_ge(s_qk_hi, b + 1)
                dve.tensor_scalar(qf[u][:], QK[0][:, 0:S], cols[:, 0:1], None, ALU.add).then_inc(s_qf_ready, 1)
                for half, dst in enumerate((QT, KT)):
                    for m in range(KD):
                        last = biased_lo(dve, dst[u], QK[half], cols[:, half * KD + m:half * KD + m + 1], m)
                last.then_inc(s_qk_lo, 1)

            def dve_qp(dve, b, u):
                dve.wait_ge(s_tanh_done, b + 1)
                dve.wait_ge(s_qf_ready, b + 1)
                dve.scalar_tensor_tensor(qf[u][:], th[u][:], lw[:, 3:4], qf[u][:], ALU.mult, ALU.add).then_inc(s_qp_ready, 1)

            def dve_ctx(dve, b, u):
                dve.wait_ge(s_ctx_hi, b + 1)
                for m in range(KD):
                    last = biased_lo(dve, PT[u], CO[u], cols[:, 2 * KD + m:2 * KD + m + 1], m)
                last.then_inc(s_ctx_lo, 1)

            def dve_x1(dve, b, u):
                dve.wait_ge(s_o_done, b + 1)
                dve.wait_ge(s_xg_ready, b + 1)
                dve.tensor_tensor(ht[u][:], bank(CO[u]), mb[u][:, 0:1, :].to_broadcast([P, TT, D]),
                                  ALU.mult).then_inc(s_y_ready, 1)
                dve.wait_ge(s_y_ready, b + 1)
                dve.tensor_tensor(xr[u][:], xr[u][:], ht[u][:], ALU.add).then_inc(s_x1_ready, 1)

            def dve_stats(dve, p, which, src, bst, mv, rs, nt, sem_in):
                chain = s_ln1_chain if which == 1 else s_ln2_chain
                n0 = p * 16
                for u in range(2):
                    if sem_in == "x":
                        dve.wait_ge((s_xa0_in, s_xa1_in)[u], 16 * (p + 1))
                    else:
                        dve.wait_ge(s_x1_ready, 2 * p + 1 + u)
                    for t in range(TT):
                        last = dve.bn_stats(bst[:, u * TT + t, :], src[u][:, t, :])
                last.then_inc(chain, 1)
                dve.wait_ge(chain, n0 + 1)
                dve.memset(nt[:], EPS)
                for j in range(2 * TT):
                    last = dve.bn_aggr(mv[:, j, :], bst[:, j, :])
                last.then_inc(chain, 1)
                dve.wait_ge(chain, n0 + 2)
                v = mv[:, :, 1]
                dve.tensor_tensor(v, v, nt[:], ALU.add).then_inc(chain, 1)
                dve.wait_ge(chain, n0 + 3)
                dve.tensor_scalar(rs[:].bitcast(I32), v.bitcast(I32), -0.5, float(0x5F3759DF), ALU.mult, ALU.add).then_inc(chain, 1)
                dve.wait_ge(chain, n0 + 4)
                n = n0 + 4
                for _ in range(3):
                    dve.tensor_tensor(nt[:], rs[:], rs[:], ALU.mult).then_inc(chain, 1)
                    dve.wait_ge(chain, n + 1)
                    dve.tensor_tensor(nt[:], nt[:], v, ALU.mult).then_inc(chain, 1)
                    dve.wait_ge(chain, n + 2)
                    dve.tensor_scalar(nt[:], nt[:], -0.5, 1.5, ALU.mult, ALU.add).then_inc(chain, 1)
                    dve.wait_ge(chain, n + 3)
                    dve.tensor_tensor(rs[:], rs[:], nt[:], ALU.mult).then_inc(chain, 1)
                    dve.wait_ge(chain, n + 4)
                    n += 4

            def dve_ln1(dve, p):
                dve_stats(dve, p, 1, xa, bst1, mv1, rs1, nt1, "x")
                for u in range(2):
                    for t in range(TT):
                        j = u * TT + t
                        last = dve.tensor_scalar(xa[u][:, t, :], xa[u][:, t, :], mv1[:, j, 0:1], rs1[:, j:j + 1],
                                                 ALU.subtract, ALU.mult)
                    last.then_inc(s_xn_ready, 1)

            def dve_ln2(dve, p):
                dve_stats(dve, p, 2, xr, bst2, mv2, rs2, nt1, "x1")
                for u in range(2):
                    for t in range(TT):
                        j = u * TT + t
                        last = dve.tensor_scalar(ht[u][:, t, :], xr[u][:, t, :], mv2[:, j, 0:1], rs2[:, j:j + 1],
                                                 ALU.subtract, ALU.mult)
                    last.then_inc(s_xn2_ready, 1)

            def dve_route_scores(dve, p):
                dve.wait_ge(s_lt_done, p + 1)
                L = LOG.rearrange("p (t e) -> p t e", e=NE)
                dve.tensor_reduce(r_mx[:], L, AX.X, ALU.max).then_inc(s_rt_a, 1)
                dve.wait_ge(s_rt_a, 2 * p + 1)
                dve.tensor_tensor(r_sc[:], L, r_mx[:].unsqueeze(2).to_broadcast([P, NR, NE]), ALU.subtract).then_inc(s_rt_a, 1)

            def act_route(act, p):
                act.wait_ge(s_rt_a, 2 * p + 2)
                act.activation(r_sc[:], r_sc[:], ACT.Exp).then_inc(s_rt_exp, 1)

            NG = NE // 2
            RB = 14

            def dve_route_select(dve, p):
                k = [p * RB]

                def done(ins):
                    ins.then_inc(s_rt_b, 1)
                    k[0] += 1
                    return k[0]

                dve.wait_ge(s_rt_exp, p + 1)
                n = done(dve.tensor_reduce(r_mx[:], r_sc[:], AX.X, ALU.add))
                dve.wait_ge(s_rt_b, n)
                n = done(dve.reciprocal(r_mx[:], r_mx[:]))
                dve.wait_ge(s_rt_b, n)
                n = done(dve.tensor_tensor(r_sc[:], r_sc[:], r_mx[:].unsqueeze(2).to_broadcast([P, NR, NE]), ALU.mult))
                dve.wait_ge(s_rt_b, n)
                pairs = r_sc[:].rearrange("p t (g i) -> p t g i", i=2)
                n = done(dve.tensor_tensor(r_gm[:], pairs[:, :, :, 0], pairs[:, :, :, 1], ALU.max))
                dve.wait_ge(s_rt_b, n)

                def rank(vals, m, out_ap):
                    for t in range(NR):
                        a = vals[:, t, :].unsqueeze(1).to_broadcast([P, m, m])
                        c = vals[:, t, :].unsqueeze(2).to_broadcast([P, m, m])
                        dve.tensor_tensor(r_gt[:, t, 0:m, 0:m], a, c, ALU.is_gt)
                        last = dve.tensor_tensor(r_eq[:, t, 0:m, 0:m], a, c, ALU.is_equal)
                    n = done(last)
                    dve.wait_ge(s_rt_b, n)
                    n = done(dve.tensor_tensor(r_eq[:, :, 0:m, 0:m], r_eq[:, :, 0:m, 0:m],
                                               lower[:, 0:m, 0:m].unsqueeze(1).to_broadcast([P, NR, m, m]), ALU.mult))
                    dve.wait_ge(s_rt_b, n)
                    n = done(dve.tensor_tensor(r_gt[:, :, 0:m, 0:m], r_gt[:, :, 0:m, 0:m], r_eq[:, :, 0:m, 0:m], ALU.add))
                    dve.wait_ge(s_rt_b, n)
                    n = done(dve.tensor_reduce(out_ap, r_gt[:, :, 0:m, 0:m], AX.X, ALU.add))
                    dve.wait_ge(s_rt_b, n)

                rank(r_gm, NG, r_rank[:, :, 0:NG])
                n = done(dve.tensor_scalar(r_gm[:], r_rank[:, :, 0:NG], 2.0, None, ALU.is_lt))
                dve.wait_ge(s_rt_b, n)
                for i in range(2):
                    last = dve.tensor_tensor(pairs[:, :, :, i], pairs[:, :, :, i], r_gm[:], ALU.mult)
                n = done(last)
                dve.wait_ge(s_rt_b, n)
                rank(r_sc, NE, r_rank[:])
                dve.tensor_scalar(r_sel[:, 0], r_rank[:], 0.0, None, ALU.is_equal)
                dve.tensor_scalar(r_sel[:, 1], r_rank[:], 1.0, None, ALU.is_equal)
                dve.tensor_scalar(r_both[:], r_rank[:], 2.0, None, ALU.is_lt).then_inc(s_both_ready, 1)

            RC = NR + 6

            def dve_route_slots(dve, p):
                k = [p * RC]

                def done(ins):
                    ins.then_inc(s_rt_c, 1)
                    k[0] += 1
                    return k[0]

                dve.wait_ge(s_rank_done, p + 1)
                rk = RNK.rearrange("p (t e) -> p t e", e=NE)
                tot = TOT.rearrange("p (t e) -> p t e", e=NE)
                for t in range(NR):
                    n = done(dve.tensor_tensor(r_base[:, t + 1, :], r_base[:, t, :], tot[:, t, :], ALU.add))
                    dve.wait_ge(s_rt_c, n)
                n = done(dve.tensor_tensor(r_pos[:], rk, r_base[:, 0:NR, :], ALU.add))
                dve.wait_ge(s_rt_c, n)
                n = done(dve.tensor_tensor(r_pos[:], r_pos[:], erow[:].unsqueeze(1).to_broadcast([P, NR, NE]), ALU.add))
                dve.tensor_copy(r_base[:, 0, :], r_base[:, NR, :])
                dve.wait_ge(s_rt_c, n)
                for i in range(2):
                    last = dve.tensor_tensor(r_tmp[:, i], r_pos[:], r_sel[:, i], ALU.mult)
                n = done(last)
                dve.wait_ge(s_rt_c, n)
                n = done(dve.tensor_reduce(r_slot[:], r_tmp[:], AX.X, ALU.add))
                dve.wait_ge(s_rt_c, n)
                dve.tensor_copy(slot_u[:], r_slot[:])
                for i in range(2):
                    last = dve.tensor_tensor(r_tmp[:, i], r_sc[:], r_sel[:, i], ALU.mult)
                n = done(last)
                dve.wait_ge(s_rt_c, n)
                n = done(dve.tensor_reduce(r_w[:], r_tmp[:], AX.X, ALU.add))
                dve.tensor_tensor(r_pos[:], r_sel[:, 0], eidx[:].unsqueeze(1).to_broadcast([P, NR, NE]), ALU.mult).then_inc(s_rt_pos, 1)
                dve.wait_ge(s_rt_c, n)
                dve.wait_ge(s_rt_pos, p + 1)
                for u in range(2):
                    js = slice(u * TT, (u + 1) * TT)
                    dve.tensor_copy(h2[u][:, :, D], r_w[:, 0, js])
                    dve.tensor_tensor(h2[u][:, :, D + 1], r_w[:, 1, js], r_w[:, 0, js], ALU.subtract)
                    dve.tensor_reduce(h2[u][:, :, D + 2], r_pos[:, js, :], AX.X, ALU.add)
                    last = dve.tensor_copy(h2[u][:, :, D + 3], token_id[:, ds((p * 2 + u) * TT, TT)])
                last.then_inc(s_slots_ready, 1)

            def pool_xg(pool, b, u):
                pool.wait_ge((s_xr0_in, s_xr1_in)[u], 8 * (b - u + 2))
                pool.wait_ge((s_mb0_in, s_mb1_in)[u], 8 * (b - u + 2))
                pool.tensor_tensor(xr[u][:], xr[u][:], mb[u][:, 1:2, :].to_broadcast([P, TT, D]), ALU.add).then_inc(s_xg_ready, 1)

            def pool_h2(pool, b, u):
                pool.wait_ge(s_xn2_ready, b + 1)
                if not (type(b) is int and b < 2):
                    pool.wait_ge((s_sc0, s_sc1)[u], 16 * TT * (b - u))
                pool.tensor_tensor(h2[u][:, :, 0:D], ht[u][:], mb[u][:, 2:3, :].to_broadcast([P, TT, D]), ALU.mult).then_inc(s_h2_chain, 1)
                pool.wait_ge(s_h2_chain, b + 1)
                pool.tensor_tensor(h2[u][:, :, 0:D], h2[u][:, :, 0:D], mb[u][:, 3:4, :].to_broadcast([P, TT, D]), ALU.add).then_inc(s_h2_ready, 1)

            def pool_scatter(pool, p):
                pool.wait_ge(s_base_zero, 1)
                pool.wait_ge(s_slots_ready, p + 1)
                for u in range(2):
                    for t in range(TT):
                        for i in range(2):
                            j = u * TT + t
                            pool.indirect_dma_start(
                                out=routed_in, out_offset=bass.IndirectOffsetOnAxis(slot_u[:, i, j:j + 1], 0),
                                in_=h2[u][:, t, :], in_offset=None).then_inc((s_sc0, s_sc1)[u], 16)

            def pair_of(p):
                return ((2 * p, 0), (2 * p + 1, 1))

            def pe_front(pe, p):
                for b, u in pair_of(p):
                    pe_xt(pe, b, u)
                for b, u in pair_of(p):
                    pe_qk(pe, b, u)

            def pe_turn(pe, p, post, front):
                for b, u in pair_of(p):
                    pe_scores(pe, b, u, False)
                for b, u in pair_of(p):
                    pe_v(pe, b, u)
                for b, u in pair_of(p):
                    pe_pt(pe, b, u, False)
                for b, u in pair_of(p):
                    pe_ctx(pe, b, u, False)
                if post:
                    pe.wait_ge(s_tanh_done, 2 * p + 2)
                    for b, u in pair_of(p - 1):
                        pe_h2t(pe, b, u)
                    for b, u in pair_of(p - 1):
                        pe_logits(pe, b, u)
                for b, u in pair_of(p):
                    pe_scores(pe, b, u, True)
                if front:
                    for b, u in pair_of(p + 1):
                        pe_xt(pe, b, u)
                if post:
                    pe_logits_t(pe, p - 1)
                if front:
                    pe_qk(pe, 2 * p + 2, 0)
                for b, u in pair_of(p):
                    pe_pt(pe, b, u, True)
                if post:
                    pe_rank(pe, p - 1)
                if front:
                    pe_qk(pe, 2 * p + 3, 1)
                if post:
                    pe.wait_ge(s_slots_ready, p)
                for b, u in pair_of(p):
                    pe_ctx(pe, b, u, True)
                for b, u in pair_of(p):
                    pe_out(pe, b, u)

            def act_turn(act, p, post, front):
                for b, u in pair_of(p):
                    act_exp(act, b, u, False)
                for b, u in pair_of(p):
                    act_copy(act, s_v_done, b, VV[u][0][:], bank(QK[u]), s_v_hi)
                for b, u in pair_of(p):
                    act_copy(act, s_pt1_done, b, PT[u][0][:], bank(TR[u]), s_pt1_hi)
                for b, u in pair_of(p):
                    act_tanh(act, b, u)
                for b, u in pair_of(p):
                    act_copy(act, s_qp_ready, b, QT[u][0][:, 0, :], qf[u][:], s_qp_hi)
                if post:
                    for b, u in pair_of(p - 1):
                        act_copy(act, s_h2t_done, b, h2T[0][:, :, ds(b * S, S)], bank(TR[u]), s_h2_hi)
                    for b, u in pair_of(p - 1):
                        act_copy(act, s_lg_done, b, lg[u][:], CO[u][0:NE, S:2 * S], s_lg_copied)
                for b, u in pair_of(p):
                    act_exp(act, b, u, True)
                if front:
                    for b, u in pair_of(p + 1):
                        act_h(act, b, u)
                if post:
                    act_route(act, p - 1)
                if front:
                    act_qk(act, 2 * p + 2, 0)
                for b, u in pair_of(p):
                    act_copy(act, s_pt2_done, b, PT[u][0][:], bank(TR[u]), s_pt2_hi)
                if front:
                    act_qk(act, 2 * p + 3, 1)
                for b, u in pair_of(p):
                    act_ctx(act, b, u)

            def dve_turn(dve, p, post, front):
                for b, u in pair_of(p):
                    dve_max(dve, b, u, False)
                for b, u in pair_of(p):
                    dve_norm(dve, b, u, False)
                for b, u in pair_of(p):
                    dve_lo(dve, s_v_hi, b, bank(QK[u]), VV[u][0][:], VV[u][1][:], s_v_lo)
                for b, u in pair_of(p):
                    dve_lo(dve, s_pt1_hi, b, bank(TR[u]), PT[u][0][:], PT[u][1][:], s_pt1_lo)
                if front:
                    dve_ln1(dve, p + 1)
                for b, u in pair_of(p):
                    dve_qp(dve, b, u)
                for b, u in pair_of(p):
                    dve_lo(dve, s_qp_hi, b, qf[u][:], QT[u][0][:, 0, :], QT[u][1][:, 0, :], s_qp_lo)
                if post:
                    for b, u in pair_of(p - 1):
                        dve_lo(dve, s_h2_hi, b, bank(TR[u]), h2T[0][:, :, ds(b * S, S)], h2T[1][:, :, ds(b * S, S)], s_h2_lo)
                for b, u in pair_of(p):
                    dve_max(dve, b, u, True)
                if front:
                    for b, u in pair_of(p + 1):
                        dve_h(dve, b, u)
                for b, u in pair_of(p):
                    dve_norm(dve, b, u, True)
                if post:
                    dve_route_scores(dve, p - 1)
                if front:
                    dve_qk(dve, 2 * p + 2, 0)
                for b, u in pair_of(p):
                    dve_lo(dve, s_pt2_hi, b, bank(TR[u]), PT[u][0][:], PT[u][1][:], s_pt2_lo)
                if post:
                    dve_route_select(dve, p - 1)
                if front:
                    dve_qk(dve, 2 * p + 3, 1)
                if post:
                    dve_route_slots(dve, p - 1)
                for b, u in pair_of(p):
                    dve_ctx(dve, b, u)
                for b, u in pair_of(p):
                    dve_x1(dve, b, u)
                dve_ln2(dve, p)

            def pool_turn(pool, p, post, front):
                for b, u in pair_of(p):
                    pool_xg(pool, b, u)
                if post:
                    pool_scatter(pool, p - 1)
                for b, u in pair_of(p):
                    pool_h2(pool, b, u)

            def sp_front(sp, p):
                for b, u in pair_of(p):
                    if not (type(p) is int and p == 0):
                        sp.wait_ge(s_xt_done, b - 1)
                    sp.dma_start(xa[u][:], x_in[ds(b, 1)].rearrange("o (t p) d -> p (o t) d", p=P)).then_inc((s_xa0_in, s_xa1_in)[u], 16)

            def sp_mid(sp, p, first):
                for b, u in pair_of(p):
                    if not first:
                        sp.wait_ge(s_h2_ready, b - 1)
                    sp.dma_start(mb[u][:], modrow[ds(b, 1), 0:4 * D].to_broadcast([P, 4 * D]).rearrange("p (j d) -> p j d", d=D)).then_inc((s_mb0_in, s_mb1_in)[u], 16)
                    if not first:
                        sp.wait_ge((s_x1_out0, s_x1_out1)[u], 8 * (b - u))
                    sp.dma_start(xr[u][:], x_in[ds(b, 1)].rearrange("o (t p) d -> p (o t) d", p=P)).then_inc((s_xr0_in, s_xr1_in)[u], 16)

            def sp_store(sp, p):
                for b, u in pair_of(p):
                    sp.wait_ge(s_x1_ready, b + 1)
                    sp.dma_start(x1_dram[ds(b, 1)].rearrange("o (t p) d -> p (o t) d", p=P), xr[u][:]).then_inc((s_x1_out0, s_x1_out1)[u], 16)

            with nc.Block() as block:
                @block.sync
                def _(sp):
                    sp_front(sp, 0)
                    sp_mid(sp, 0, True)
                    sp_front(sp, 1)
                    sp_store(sp, 0)
                    with sp.Fori(1, NPAIR - 1) as p:
                        sp_mid(sp, p, False)
                        sp_front(sp, p + 1)
                        sp_store(sp, p)
                    sp_mid(sp, NPAIR - 1, False)
                    sp_store(sp, NPAIR - 1)
                    for x in (s_x1_out0, s_x1_out1):
                        sp.wait_ge(x, 16 * NPAIR)
                    sp.wait_ge(s_pad_ready, 1)
                    for e in range(NE):
                        row = sp.value_load(pad_u[0:1, e:e + 1], min_val=0, max_val=NE * REGION - P)
                        sp.dma_start(routed_in[ds(row, P), :], pad[:]).then_inc(s_pad_out, 16)
                    sp.wait_ge(s_pad_out, 16 * NE)

                @block.gpsimd
                def _(pool):
                    pool.memset(pad[:], 0.0).then_inc(s_pad_chain, 1)
                    pool.wait_ge(s_pad_chain, 1)
                    pool.memset(pad[:, D + META - 1:D + META], float(SKIP)).then_inc(s_pad_chain, 1)
                    pool.memset(r_base[:, 0, :], 0.0).then_inc(s_base_zero, 1)
                    pool_turn(pool, 0, False, True)
                    with pool.Fori(1, NPAIR - 1) as p:
                        pool_turn(pool, p, True, True)
                    pool_turn(pool, NPAIR - 1, True, False)
                    pool_scatter(pool, NPAIR - 1)
                    for x in (s_sc0, s_sc1):
                        pool.wait_ge(x, 16 * 2 * TT * NPAIR)

                @block.scalar
                def _(act):
                    for b, u in pair_of(0):
                        act_h(act, b, u)
                    for b, u in pair_of(0):
                        act_qk(act, b, u)
                    act_turn(act, 0, False, True)
                    with act.Fori(1, NPAIR - 1) as p:
                        act_turn(act, p, True, True)
                    act_turn(act, NPAIR - 1, True, False)
                    p = NPAIR - 1
                    for b, u in pair_of(p):
                        act_copy(act, s_h2t_done, b, h2T[0][:, :, ds(b * S, S)], bank(TR[u]), s_h2_hi)
                    for b, u in pair_of(p):
                        act_copy(act, s_lg_done, b, lg[u][:], CO[u][0:NE, S:2 * S], s_lg_copied)
                    act_route(act, p)

                @block.vector
                def _(dve):
                    dve_ln1(dve, 0)
                    for b, u in pair_of(0):
                        dve_h(dve, b, u)
                    for b, u in pair_of(0):
                        dve_qk(dve, b, u)
                    dve.wait_ge(s_base_zero, 1)
                    dve_turn(dve, 0, False, True)
                    with dve.Fori(1, NPAIR - 1) as p:
                        dve_turn(dve, p, True, True)
                    dve_turn(dve, NPAIR - 1, True, False)
                    p = NPAIR - 1
                    for b, u in pair_of(p):
                        dve_lo(dve, s_h2_hi, b, bank(TR[u]), h2T[0][:, :, ds(b * S, S)], h2T[1][:, :, ds(b * S, S)], s_h2_lo)
                    dve_route_scores(dve, p)
                    dve_route_select(dve, p)
                    dve_route_slots(dve, p)
                    dve.wait_ge(s_slots_ready, NPAIR)
                    cnt = r_base[:, NR, :]
                    dve.tensor_tensor(r_end[:], cnt.unsqueeze(2).to_broadcast([P, NE, T // P]),
                                      step128[:].unsqueeze(1).to_broadcast([P, NE, T // P]), ALU.is_gt).then_inc(s_tab, 1)
                    dve.tensor_tensor(r_pos[:, 0, :], cnt, erow[:], ALU.add).then_inc(s_tab, 1)
                    dve.wait_ge(s_tab, 2)
                    dve.tensor_copy(pad_u[:], r_pos[0:1, 0, :]).then_inc(s_pad_ready, 1)
                    dve.tensor_reduce(r_tiles[:], r_end[:], AX.X, ALU.add).then_inc(s_tab, 1)
                    dve.wait_ge(s_tab, 3)
                    dve.tensor_copy(r_ends[:], r_tiles[:]).then_inc(s_tab, 1)
                    dve.wait_ge(s_tab, 4)
                    for e in range(1, NE):
                        dve.tensor_tensor(r_ends[:, e:e + 1], r_ends[:, e - 1:e], r_tiles[:, e:e + 1], ALU.add).then_inc(s_tab, 1)
                        dve.wait_ge(s_tab, 4 + e)
                    n = 4 + NE - 1
                    dve.tensor_tensor(r_done[:], r_ends[:].unsqueeze(1).to_broadcast([P, NT, NE]),
                                      tidx[:].unsqueeze(2).to_broadcast([P, NT, NE]), ALU.is_le).then_inc(s_tab, 1)
                    dve.wait_ge(s_tab, n + 1)
                    dve.tensor_reduce(r_tab[:, 0, :], r_done[:], AX.X, ALU.add).then_inc(s_tab, 1)
                    dve.wait_ge(s_tab, n + 2)
                    dve.tensor_tensor(r_done[:], r_done[:], r_tiles[:].unsqueeze(1).to_broadcast([P, NT, NE]), ALU.mult).then_inc(s_tab, 1)
                    dve.wait_ge(s_tab, n + 3)
                    dve.tensor_reduce(r_tab[:, 1, :], r_done[:], AX.X, ALU.add).then_inc(s_tab, 1)
                    dve.tensor_scalar(eid_f[:], r_tab[:, 0, :], float(NE - 1), None, ALU.min).then_inc(s_tab, 1)
                    dve.wait_ge(s_tab, n + 5)
                    dve.tensor_tensor(r_tab[:, 1, :], tidx[:], r_tab[:, 1, :], ALU.subtract).then_inc(s_tab, 1)
                    dve.tensor_scalar(r_tab[:, 2, :], eid_f[:], float(REGION), None, ALU.mult).then_inc(s_tab, 1)
                    dve.wait_ge(s_tab, n + 7)
                    dve.scalar_tensor_tensor(r_tab[:, 2, :], r_tab[:, 1, :], float(P), r_tab[:, 2, :], ALU.mult, ALU.add).then_inc(s_tab, 1)
                    dve.tensor_scalar(r_tab[:, 3, :], r_tab[:, 0, :], float(NE), None, ALU.is_ge).then_inc(s_tab, 1)
                    dve.wait_ge(s_tab, n + 9)
                    dve.tensor_scalar(r_tab[:, 0, :], r_tab[:, 2, :], r_pos[:, 0, NE - 1:NE], -1.0, ALU.subtract, ALU.mult).then_inc(s_tab, 1)
                    dve.wait_ge(s_tab, n + 10)
                    dve.tensor_tensor(r_tab[:, 0, :], r_tab[:, 0, :], r_tab[:, 3, :], ALU.mult).then_inc(s_tab, 1)
                    dve.wait_ge(s_tab, n + 11)
                    dve.tensor_tensor(r_tab[:, 2, :], r_tab[:, 2, :], r_tab[:, 0, :], ALU.add).then_inc(s_tab, 1)
                    dve.wait_ge(s_tab, n + 12)
                    dve.tensor_copy(tile_u[:, 0, :], eid_f[0:1, :])
                    dve.tensor_copy(tile_u[:, 1, :], r_tab[0:1, 2, :]).then_inc(s_table_ready, 1)

                @block.tensor
                def _(pe):
                    pe_front(pe, 0)
                    pe_turn(pe, 0, False, True)
                    with pe.Fori(1, NPAIR - 1) as p:
                        pe_turn(pe, p, True, True)
                    pe_turn(pe, NPAIR - 1, True, False)
                    p = NPAIR - 1
                    for b, u in pair_of(p):
                        pe_h2t(pe, b, u)
                    for b, u in pair_of(p):
                        pe_logits(pe, b, u)
                    pe_logits_t(pe, p)
                    pe_rank(pe, p)

        attention_weights.close()
        with ExitStack() as ffn:
            def tb(name, shape, dt=F32):
                return ffn.enter_context(nc.sbuf_tensor(name, shape, dt))

            def ring(name, n, shape, dt=F32):
                return [tb(f"{name}{r}", shape, dt) for r in range(n)]

            def ring_hilo(name, n, shape):
                return [(tb(f"{name}{r}_hi", shape, F32R), tb(f"{name}{r}_lo", shape, F32R)) for r in range(n)]

            W1 = KD * 2 * F
            wgu = (tb("wgu_hi", [P, KD, NE * 2 * F], F32R), tb("wgu_lo", [P, KD, NE * 2 * F], F32R))
            wdn = (tb("wdn_hi", [FH, 2, NE * D], F32R), tb("wdn_lo", [FH, 2, NE * D], F32R))
            wstage = ring("wstage", 2, [P, W1 + 2 * D])
            res = tb("res", [P, B, TT, D])
            gbb = ring("gbb", 2, [P, 1, D])
            x1b = ring("x1b", 2, [P, TT, D])
            sact = ring("sact", 2, [P, S])
            aact = ring("aact", 2, [P, S])
            aT = ring_hilo("aT", 2, [P, len(FT), S])
            og = ring("og", 2, [P, TT, D])
            xt_in = ring("xt_in", 4, [P, ROW])
            eT = ring_hilo("eT", 2, [P, KD, P])
            sg = ring("sg", 2, [P, F])
            av = ring("av", 2, [P, F])
            avT = ring_hilo("avT", 2, [FH, 2, P])
            yo = ring("yo", 2, [P, D])
            second = ring("second", 2, [P, 1])
            wt = ring("wt", 2, [P, 1])
            dest = ring("dest", 4, [P, 1], U32)

            def gu_stage(r):
                return wstage[r][:, 0:W1].rearrange("p (k n) -> p k n", k=KD)

            def dn_stage(r):
                return wstage[r][0:FH, W1:].rearrange("p (j n) -> p j n", j=2)

            def bank2(t, n=256):
                return t[:, 0:2 * n].rearrange("p (a n) -> p a n", a=2)

            GUb = [psum[0:3], psum[3:6]]
            DN = psum[6:8]
            XTb, EGU, ATb, EDN = psum[0:2], psum[2:4], psum[4:6], psum[6:8]

            def sp_shared(sp, b, u, first):
                if not first:
                    sp.wait_ge(s_res_ready, b - 1)
                sp.dma_start(x1b[u][:], x1_dram[ds(b, 1)].rearrange("o (t p) d -> p (o t) d", p=P)).then_inc((s_x1b0_in, s_x1b1_in)[u], 16)
                sp.dma_start(gbb[u][:], modrow[ds(b, 1), 4 * D:5 * D].to_broadcast([P, D]).unsqueeze(1)).then_inc((s_gbb0_in, s_gbb1_in)[u], 16)

            def pe_shared_up(pe, b, u, first):
                if not first:
                    pe.wait_ge(s_act_mul, len(FT) * (b - 1))
                for j, (f, m) in enumerate(FT):
                    for g in range(2):
                        for k in range(KD):
                            last = mm3(pe, GUb[u][j][0:m, g * S:(g + 1) * S],
                                       parts(wsgu, slice(None), k, slice(g * FS + f, g * FS + f + m)),
                                       parts(h2T, slice(None), k, ds(b * S, S)), k == 0, k == KD - 1)
                    last.then_inc(s_shgu_done, 1)

            def act_shared(act, b, u):
                for j, (f, m) in enumerate(FT):
                    n = b * len(FT) + j
                    act.wait_ge(s_shgu_done, n + 1)
                    if not (type(n) is int and n < 2):
                        act.wait_ge(s_act_mul, n - 1)
                    act.activation(sact[SJ(u, j)][0:m, :], GUb[u][j][0:m, 0:S], ACT.Silu).then_inc(s_silu_done, 1)

            def SJ(u, j):
                return (u * len(FT) + j) % 2

            def dve_shared(dve, b, u):
                for j, (f, m) in enumerate(FT):
                    n = b * len(FT) + j
                    q = SJ(u, j)
                    dve.wait_ge(s_silu_done, n + 1)
                    if not (type(n) is int and n < 2):
                        dve.wait_ge(s_a_lo, n - 1)
                    dve.tensor_tensor(aact[q][0:m, :], sact[q][0:m, :], GUb[u][j][0:m, S:2 * S], ALU.mult).then_inc(s_act_mul, 1)
                    dve.wait_ge(s_act_mul, n + 1)
                    dve.tensor_copy(aT[u][0][0:m, j, :], aact[q][0:m, :]).then_inc(s_a_hi, 1)
                    dve.wait_ge(s_a_hi, n + 1)
                    dve.tensor_tensor(aT[u][1][0:m, j, :], aact[q][0:m, :], aT[u][0][0:m, j, :].bitcast(F32),
                                      ALU.subtract).then_inc(s_a_lo, 1)

            def pe_shared_down(pe, b, u, first):
                if not first:
                    pe.wait_ge(s_og_ready, b - 1)
                pe.wait_ge(s_a_lo, len(FT) * (b + 1))
                for t in range(TT):
                    for j, (f, m) in enumerate(FT):
                        last = mm3(pe, DN[u][:, t * D:(t + 1) * D],
                                   parts(aT[u], slice(0, m), j, slice(t * P, (t + 1) * P)),
                                   parts(wsd, slice(0, m), j), j == 0, j == len(FT) - 1)
                last.then_inc(s_shdn_done, 1)

            def dve_shared_out(dve, b, u):
                dve.wait_ge(s_shdn_done, b + 1)
                dve.wait_ge((s_gbb0_in, s_gbb1_in)[u], 8 * (b - u + 2))
                dve.wait_ge((s_x1b0_in, s_x1b1_in)[u], 8 * (b - u + 2))
                dve.tensor_tensor(og[u][:], bank2(DN[u]), gbb[u][:].to_broadcast([P, TT, D]), ALU.mult).then_inc(s_og_ready, 1)
                dve.wait_ge(s_og_ready, b + 1)
                dve.tensor_tensor(res[:, ds(b, 1)].rearrange("p o t d -> p (o t) d"), og[u][:], x1b[u][:], ALU.add).then_inc(s_res_ready, 1)

            def sp_tile(sp, t, r, first):
                sp.wait_ge(s_table_ready, 1)
                if not first:
                    sp.wait_ge(s_ea_ready, t - 3)
                row = sp.value_load(tile_u[0:1, 1, ds(t, 1)], min_val=0, max_val=NE * REGION - P)
                sp.dma_start(xt_in[r][:], routed_in[ds(row, P), :]).then_inc(tile_sems[r], 16)

            tile_sems = [s_tile0_in, s_tile1_in, s_tile2_in, s_tile3_in]
            out_sems = [s_tile0_out, s_tile1_out]

            def tile_wait(t, r):
                return 4 * (t - r) + 16

            def pe_tile_in(pe, t, r):
                pe.wait_ge(tile_sems[r], tile_wait(t, r))
                for d in range(KD):
                    last = pe.transpose(XTb[r % 2][:, d * P:(d + 1) * P], xt_in[r][:, d * P:(d + 1) * P], ident[:])
                last.then_inc(s_ext_done, 1)

            def pe_tile_up(pe, t, r):
                pe.wait_ge(s_table_ready, 1)
                pe.wait_ge(s_ex_lo, t + 1)
                e = pe.value_load(tile_u[0:1, 0, ds(t, 1)], min_val=0, max_val=NE - 1)
                for k in range(KD):
                    last = mm3(pe, EGU[r % 2][:, 0:2 * F], parts(eT[r % 2], slice(None), k),
                               parts(wgu, slice(None), k, ds(e * (2 * F), 2 * F)), k == 0, k == KD - 1)
                last.then_inc(s_egu_done, 1)

            def pe_tile_act(pe, t, r):
                pe.wait_ge(s_ea_ready, t + 1)
                for j in range(2):
                    last = pe.transpose(ATb[r % 2][0:FH, j * P:(j + 1) * P], av[r % 2][:, j * FH:(j + 1) * FH], ident[:])
                last.then_inc(s_eat_done, 1)

            def pe_tile_down(pe, t, r):
                pe.wait_ge(s_table_ready, 1)
                pe.wait_ge(s_ea_lo, t + 1)
                e = pe.value_load(tile_u[0:1, 0, ds(t, 1)], min_val=0, max_val=NE - 1)
                for j in range(2):
                    last = mm3(pe, EDN[r % 2][:, 0:D], parts(avT[r % 2], slice(None), j),
                               parts(wdn, slice(None), j, ds(e * D, D)), j == 0, j == 1)
                last.then_inc(s_edn_done, 1)

            def act_tile_in(act, t, r):
                act.wait_ge(s_ext_done, t + 1)
                act.activation(eT[r % 2][0][:], bank2(XTb[r % 2], P), ACT.Copy).then_inc(s_ex_hi, 1)

            def act_tile_silu(act, t, r):
                act.wait_ge(s_egu_done, t + 1)
                act.activation(sg[r % 2][:], EGU[r % 2][:, 0:F], ACT.Silu).then_inc(s_esilu, 1)

            def act_tile_act(act, t, r):
                act.wait_ge(s_eat_done, t + 1)
                act.activation(avT[r % 2][0][:], bank2(ATb[r % 2], P)[0:FH], ACT.Copy).then_inc(s_ea_hi, 1)

            def act_tile_out(act, t, r, first):
                act.wait_ge(s_edn_done, t + 1)
                if not first:
                    act.wait_ge(out_sems[r % 2], 8 * (t - r % 2))
                act.activation(yo[r % 2][:], EDN[r % 2][:, 0:D], ACT.Copy).then_inc(s_ey_ready, 1)

            def dve_tile_in(dve, t, r):
                dve.wait_ge(s_ex_hi, t + 1)
                dve.tensor_tensor(eT[r % 2][1][:], bank2(XTb[r % 2], P), eT[r % 2][0][:].bitcast(F32), ALU.subtract).then_inc(s_ex_lo, 1)

            def dve_tile_meta(dve, t, r):
                q = r % 2
                dve.wait_ge(tile_sems[r], tile_wait(t, r))
                if not (type(t) is int and t < 4):
                    dve.wait_ge(out_sems[q], 8 * (t - q) - 16)
                dve.tensor_tensor(second[q][:], xt_in[r][:, D + 2:D + 3], eid_f[:, ds(t, 1)], ALU.not_equal).then_inc(s_esecond, 1)
                dve.wait_ge(s_esecond, t + 1)
                dve.scalar_tensor_tensor(wt[q][:], xt_in[r][:, D + 1:D + 2], second[q][:, 0:1], xt_in[r][:, D:D + 1],
                                         ALU.mult, ALU.add)
                dve.scalar_tensor_tensor(dest[r][:], second[q][:], float(T), xt_in[r][:, D + 3:D + 4],
                                         ALU.mult, ALU.add).then_inc(s_emeta, 1)

            def dve_tile_act(dve, t, r):
                q = r % 2
                dve.wait_ge(s_emeta, t + 1)
                dve.wait_ge(s_esilu, t + 1)
                dve.scalar_tensor_tensor(av[q][:], sg[q][:], wt[q][:, 0:1], EGU[q][:, F:2 * F],
                                         ALU.mult, ALU.mult).then_inc(s_ea_ready, 1)

            def dve_tile_lo(dve, t, r):
                q = r % 2
                dve.wait_ge(s_ea_hi, t + 1)
                dve.tensor_tensor(avT[q][1][:], bank2(ATb[q], P)[0:FH], avT[q][0][:].bitcast(F32), ALU.subtract).then_inc(s_ea_lo, 1)

            def pool_tile(pool, t, r):
                pool.wait_ge(s_emeta, t + 1)
                pool.wait_ge(s_ey_ready, t + 1)
                pool.indirect_dma_start(out=routed_out, out_offset=bass.IndirectOffsetOnAxis(dest[r][:, 0:1], 0),
                                        in_=yo[r % 2][:], in_offset=None,
                                        bounds_check=2 * T - 1, oob_is_err=False).then_inc(out_sems[r % 2], 16)

            def steps(eng, one):
                for t in range(5):
                    one(t, t % 4, t >= 1, True, True)
                with eng.Fori(1, (NT - 3) // 4) as i:
                    for v in range(4):
                        one(4 * i + 1 + v, (1 + v) % 4, True, True, True)
                one(NT - 2, (NT - 2) % 4, True, True, False)
                one(NT - 1, (NT - 1) % 4, True, False, False)

            LASTT = NT - 1

            with nc.Block() as block:
                @block.sync
                def _(sp):
                    for e in range(NE):
                        r = e % 2
                        if e >= 2:
                            sp.wait_ge(s_est_free, 2 * (e - 1))
                        sp.dma_start(gu_stage(r), gu_t[:, e, :].rearrange("(k p) n -> p k n", p=P)).then_inc((s_est0_in, s_est1_in)[r], 16)
                        sp.dma_start(dn_stage(r), down_t[e].rearrange("(j p) n -> p j n", p=FH)).then_inc((s_est0_in, s_est1_in)[r], 16)
                    for b in range(2):
                        sp_shared(sp, b, b, True)
                    with sp.Fori(1, NPAIR) as p:
                        for u in range(2):
                            sp_shared(sp, 2 * p + u, u, False)
                    for t in range(4):
                        sp_tile(sp, t, t, True)
                    with sp.Fori(1, (NT - 3) // 4) as i:
                        for v in range(4):
                            sp_tile(sp, 4 * i + v, v, False)
                    for t in range(NT - 3, NT):
                        sp_tile(sp, t, t % 4, False)
                    sp.wait_ge(s_tile0_out, 16 * ((NT + 1) // 2))
                    sp.wait_ge(s_tile1_out, 16 * (NT // 2))

                    def fin_in(b, u):
                        for i in range(2):
                            sp.dma_start((x1b, og)[i][u][:], routed_out[ds(b * S + i * T, S), :].rearrange("(t p) d -> p t d", p=P)).then_inc((s_y0_in, s_y1_in)[u], 16)
                        sp.dma_start(gbb[u][:], modrow[ds(b, 1), 4 * D:5 * D].to_broadcast([P, D]).unsqueeze(1)).then_inc((s_y0_in, s_y1_in)[u], 16)

                    def fin_out(b, u):
                        sp.wait_ge(s_fin_ready, b + 1)
                        sp.dma_start(out[ds(b, 1)].rearrange("o (t p) d -> p (o t) d", p=P), res[:, ds(b, 1)].rearrange("p o t d -> p (o t) d")).then_inc(s_stored, 16)

                    for b in range(2):
                        fin_in(b, b)
                    with sp.Fori(0, NPAIR - 1) as p:
                        for u in range(2):
                            fin_out(2 * p + u, u)
                            fin_in(2 * p + 2 + u, u)
                    for u in range(2):
                        fin_out(B - 2 + u, u)
                    sp.wait_ge(s_stored, 16 * B)

                @block.gpsimd
                def _(pool):
                    for t in range(NT):
                        pool_tile(pool, t, t % 4)

                @block.scalar
                def _(act):
                    for e in range(NE):
                        r = e % 2
                        act.wait_ge((s_est0_in, s_est1_in)[r], 32 * (e // 2 + 1))
                        act.activation(wgu[0][:, :, e * 2 * F:(e + 1) * 2 * F], gu_stage(r), ACT.Copy)
                        act.activation(wdn[0][:, :, e * D:(e + 1) * D], dn_stage(r), ACT.Copy).then_inc(s_ew_hi, 1)
                    for b in range(2):
                        act_shared(act, b, b)
                    with act.Fori(1, NPAIR) as p:
                        for u in range(2):
                            act_shared(act, 2 * p + u, u)

                    def one(t, r, back, up, ahead):
                        if up:
                            act_tile_silu(act, t + 1, (r + 1) % 4)
                        act_tile_act(act, t, r)
                        if back:
                            act_tile_out(act, t - 1, (r - 1) % 4, type(t) is int and t < 3)
                        if ahead:
                            act_tile_in(act, t + 2, (r + 2) % 4)

                    act_tile_in(act, 0, 0)
                    act_tile_in(act, 1, 1)
                    act_tile_silu(act, 0, 0)
                    steps(act, one)
                    act_tile_out(act, LASTT, LASTT % 4, False)

                @block.vector
                def _(dve):
                    for e in range(NE):
                        r = e % 2
                        dve.wait_ge(s_ew_hi, e + 1)
                        dve.tensor_tensor(wgu[1][:, :, e * 2 * F:(e + 1) * 2 * F], gu_stage(r),
                                          wgu[0][:, :, e * 2 * F:(e + 1) * 2 * F].bitcast(F32), ALU.subtract).then_inc(s_est_free, 1)
                        dve.tensor_tensor(wdn[1][:, :, e * D:(e + 1) * D], dn_stage(r),
                                          wdn[0][:, :, e * D:(e + 1) * D].bitcast(F32), ALU.subtract).then_inc(s_est_free, 1)

                    dve_shared(dve, 0, 0)
                    with dve.Fori(0, NPAIR - 1) as p:
                        for u in range(2):
                            dve_shared(dve, 2 * p + 1 + u, 1 - u)
                            dve_shared_out(dve, 2 * p + u, u)
                    dve_shared(dve, B - 1, 1)
                    dve_shared_out(dve, B - 2, 0)
                    dve_shared_out(dve, B - 1, 1)

                    def one(t, r, back, up, ahead):
                        if up:
                            dve_tile_meta(dve, t + 1, (r + 1) % 4)
                            dve_tile_act(dve, t + 1, (r + 1) % 4)
                        dve_tile_lo(dve, t, r)
                        if ahead:
                            dve_tile_in(dve, t + 2, (r + 2) % 4)

                    dve_tile_in(dve, 0, 0)
                    dve_tile_in(dve, 1, 1)
                    dve_tile_meta(dve, 0, 0)
                    dve_tile_act(dve, 0, 0)
                    steps(dve, one)

                    def fin(b, u):
                        dve.wait_ge((s_y0_in, s_y1_in)[u], 24 * (b - u + 2))
                        dve.tensor_tensor(x1b[u][:], x1b[u][:], og[u][:], ALU.add).then_inc(s_fin_sum, 1)
                        dve.wait_ge(s_fin_sum, b + 1)
                        dve.tensor_tensor(x1b[u][:], x1b[u][:], gbb[u][:].to_broadcast([P, TT, D]), ALU.mult).then_inc(s_fin_mul, 1)
                        dve.wait_ge(s_fin_mul, b + 1)
                        r_ = res[:, ds(b, 1)].rearrange("p o t d -> p (o t) d")
                        dve.tensor_tensor(r_, r_, x1b[u][:], ALU.add).then_inc(s_fin_ready, 1)
                    with dve.Fori(0, NPAIR) as p:
                        for u in range(2):
                            fin(2 * p + u, u)

                @block.tensor
                def _(pe):
                    pe_shared_up(pe, 0, 0, True)
                    pe_shared_up(pe, 1, 1, True)
                    pe_shared_down(pe, 0, 0, True)
                    pe_shared_up(pe, 2, 0, False)
                    pe_shared_down(pe, 1, 1, True)
                    with pe.Fori(1, NPAIR - 1) as p:
                        for u in range(2):
                            pe_shared_up(pe, 2 * p + 1 + u, 1 - u, False)
                            pe_shared_down(pe, 2 * p + u, u, False)
                    pe_shared_up(pe, B - 1, 1, False)
                    pe_shared_down(pe, B - 2, 0, False)
                    pe_shared_down(pe, B - 1, 1, False)

                    def one(t, r, back, up, ahead):
                        if up:
                            pe_tile_up(pe, t + 1, (r + 1) % 4)
                        pe_tile_act(pe, t, r)
                        if back:
                            pe_tile_down(pe, t - 1, (r - 1) % 4)
                        if ahead:
                            pe_tile_in(pe, t + 2, (r + 2) % 4)

                    pe.wait_ge(s_est_free, 2 * NE)
                    pe.wait_ge(s_og_ready, B)
                    pe_tile_in(pe, 0, 0)
                    pe_tile_in(pe, 1, 1)
                    pe_tile_up(pe, 0, 0)
                    steps(pe, one)
                    pe_tile_down(pe, LASTT, LASTT % 4)


def kernel(L0_attn_hidden_states, L0_attn_c_attn_w, L0_attn_c_attn_b, L0_attn_c_proj_w, L0_attn_c_proj_b,
           L0_attn_cam_gate, L0_attn_cam_w0, L0_attn_cam_w1, L0_ffn_gate_weight, L0_ffn_gate_w, L0_ffn_up_w,
           L0_ffn_down_w, L0_ffn_sh_gate_w, L0_ffn_sh_up_w, L0_ffn_sh_down_w, L0_c, L0_wmod):
    import concourse.bacc as bacc
    from concourse.bass_utils import run_bass_kernel_spmd

    def lay(a):
        return np.ascontiguousarray(a)

    gate_w, up_w = np.asarray(L0_ffn_gate_w), np.asarray(L0_ffn_up_w)
    arrays = {
        "x": lay(L0_attn_hidden_states),
        "w_qkv": lay(L0_attn_c_attn_w),
        "b_cols": lay(np.asarray(L0_attn_c_attn_b).reshape(-1, P).T),
        "w_proj": lay(L0_attn_c_proj_w),
        "b_proj": lay(L0_attn_c_proj_b),
        "gate_col": lay(np.asarray(L0_attn_cam_gate).reshape(P, 1)),
        "cam_w0": lay(L0_attn_cam_w0),
        "cam_w1": lay(L0_attn_cam_w1),
        "router_t": lay(np.asarray(L0_ffn_gate_weight).T),
        "gu_t": lay(np.concatenate([gate_w, up_w], axis=1).transpose(2, 0, 1)),
        "down_t": lay(np.asarray(L0_ffn_down_w).transpose(0, 2, 1)),
        "sh_gu_t": lay(np.concatenate([np.asarray(L0_ffn_sh_gate_w), np.asarray(L0_ffn_sh_up_w)], axis=0).T),
        "sh_down_t": lay(np.asarray(L0_ffn_sh_down_w).T),
        "c_t": lay(np.asarray(L0_c).T),
        "w_mod": lay(L0_wmod),
    }
    nc = bacc.Bacc("TRN2", target_bir_lowering=False, num_devices=1)
    args = [nc.dram_tensor(n, a.shape, mybir.dt.from_np(a.dtype), kind="ExternalInput").ap() for n, a in arrays.items()]
    out = nc.dram_tensor("out", arrays["x"].shape, F32, kind="ExternalOutput").ap()
    adaln_block(nc, *args, out)
    r = run_bass_kernel_spmd(nc, [arrays], core_ids=[0])
    return r.results[0]["out"]
```

```python
from contextlib import ExitStack

import numpy as np

import concourse.bass as bass
from concourse import mybir

ALU = mybir.AluOpType
ACT = mybir.ActivationFunctionType
F32 = mybir.dt.float32
F32R = mybir.dt.float32r
BF16 = mybir.dt.bfloat16
U32 = mybir.dt.uint32
I32 = mybir.dt.int32
AX = mybir.AxisListType
ds = bass.ds

P = 128
EPS = 1e-5
GUARD = 0.25
HEAD_DIM = 16
SCALE = float(HEAD_DIM) ** -0.5
LAYER_DEPTH = 0.5
META = 4
SKIP = 1 << 20


def adaln_block(nc, x_in, w_qkv, b_cols, w_proj, b_proj, gate_col, cam_w0, cam_w1,
                router_t, gu_t, down_t, sh_gu_t, sh_down_t, c_t, w_mod, out):
    B, S, D = x_in.shape
    NE = router_t.shape[1]
    F = down_t.shape[1]
    FS = sh_down_t.shape[0]
    KD = D // P
    TT = S // P
    T = B * S
    NPAIR = B // 2
    NT = (2 * T + NE * (P - 1)) // P
    REGION = T + P
    ROW = D + META
    FH = F // 2
    FT = [(f, min(P, FS - f)) for f in range(0, FS, P)]
    UNR = 3
    assert D == KD * P == 256 and S == TT * P == 256 and NT % UNR == 0 and F <= 256

    with ExitStack() as ctx:
        def sb(name, shape, dt=F32):
            return ctx.enter_context(nc.sbuf_tensor(name, shape, dt))

        def hilo(name, shape):
            return sb(name + "_hi", shape, F32R), sb(name + "_lo", shape, F32R)

        def sem(name):
            return ctx.enter_context(nc.semaphore(name))

        s_c_in = sem("c_in")
        s_wmod_in = sem("wmod_in")
        s_wqkv_in = sem("wqkv_in")
        s_wproj_in = sem("wproj_in")
        s_wrt_in = sem("wrt_in")
        s_wsgu_in = sem("wsgu_in")
        s_wsd_in = sem("wsd_in")
        s_mrow_ready = sem("mrow_ready")
        s_modrow_out = sem("modrow_out")
        s_const = sem("const")
        s_ident_ready = sem("ident_ready")
        s_cols_in = sem("cols_in")
        s_c_exp = sem("c_exp")
        s_lw_sum = sem("lw_sum")
        s_lw_exp = sem("lw_exp")
        s_whi = sem("whi")
        s_kscaled = sem("kscaled")
        s_bvrep_ready = sem("bvrep_ready")
        s_c_chain = sem("c_chain")
        s_silu_c = sem("silu_c")
        s_cols_ready = sem("cols_ready")
        s_wlo = sem("wlo")
        s_mod_mm = sem("mod_mm")
        s_mod_copied = sem("mod_copied")
        s_guard = sem("guard")
        s_bvp_done = sem("bvp_done")
        s_bp_ready = sem("bp_ready")
        s_modT = sem("modT")
        s_sacol_ready = sem("sacol_ready")
        s_xn_ready = sem("xn_ready")
        s_xt_done = sem("xt_done")
        s_h_lo = sem("h_lo")
        s_qk_hi = sem("qk_hi")
        s_qk_lo = sem("qk_lo")
        s_qk_done = sem("qk_done")
        s_v_done = sem("v_done")
        s_qp_hi = sem("qp_hi")
        s_qp_lo = sem("qp_lo")
        s_s2_done = sem("s2_done")
        s_s1_done = sem("s1_done")
        s_exp2 = sem("exp2")
        s_norm1 = sem("norm1")
        s_pt2_done = sem("pt2_done")
        s_pt1_done = sem("pt1_done")
        s_pt2_hi = sem("pt2_hi")
        s_pt2_lo = sem("pt2_lo")
        s_pt1_hi = sem("pt1_hi")
        s_pt1_lo = sem("pt1_lo")
        s_v_hi = sem("v_hi")
        s_v_lo = sem("v_lo")
        s_c2_done = sem("c2_done")
        s_c1_done = sem("c1_done")
        s_ctx_hi = sem("ctx_hi")
        s_ctx_lo = sem("ctx_lo")
        s_o_done = sem("o_done")
        s_h2_ready = sem("h2_ready")
        s_h2t_done = sem("h2t_done")
        s_h2_hi = sem("h2_hi")
        s_h2_lo = sem("h2_lo")
        s_lg_done = sem("lg_done")
        s_max2 = sem("max2")
        s_max1 = sem("max1")
        s_exp1 = sem("exp1")
        s_rl1 = sem("rl1")
        s_ht_ready = sem("ht_ready")
        s_tanh_done = sem("tanh_done")
        s_rl2 = sem("rl2")
        s_h_hi = sem("h_hi")
        s_qf_ready = sem("qf_ready")
        s_qp_ready = sem("qp_ready")
        s_mb0_in = sem("mb0_in")
        s_mb1_in = sem("mb1_in")
        s_y_ready = sem("y_ready")
        s_stats1 = sem("stats1")
        s_var1 = sem("var1")
        s_xa0_in = sem("xa0_in")
        s_xa1_in = sem("xa1_in")
        s_stats2 = sem("stats2")
        s_var2 = sem("var2")
        s_x1_ready = sem("x1_ready")
        s_xr0_in = sem("xr0_in")
        s_xr1_in = sem("xr1_in")
        s_xg_ready = sem("xg_ready")
        s_xn2_ready = sem("xn2_ready")
        s_h2c0 = sem("h2c0")
        s_h2c1 = sem("h2c1")
        s_h2_chain = sem("h2_chain")
        s_lg_copied = sem("lg_copied")
        s_rstd1 = sem("rstd1")
        s_rstd2 = sem("rstd2")
        s_x1_out0 = sem("x1_out0")
        s_x1_out1 = sem("x1_out1")
        s_lt_done = sem("lt_done")
        s_both_ready = sem("both_ready")
        s_rank_done = sem("rank_done")
        s_rt_a = sem("rt_a")
        s_rt_exp = sem("rt_exp")
        s_rt_b = sem("rt_b")
        s_sel_ready = sem("sel_ready")
        s_rt_c = sem("rt_c")
        s_tab = sem("tab")
        s_slots_ready = sem("slots_ready")
        s_pad_ready = sem("pad_ready")
        s_table_ready = sem("table_ready")
        s_scattered = sem("scattered")
        s_est_free = sem("est_free")
        s_est0_in = sem("est0_in")
        s_est1_in = sem("est1_in")
        s_ew_hi = sem("ew_hi")
        s_res_ready = sem("res_ready")
        s_x1b0_in = sem("x1b0_in")
        s_x1b1_in = sem("x1b1_in")
        s_gbb0_in = sem("gbb0_in")
        s_gbb1_in = sem("gbb1_in")
        s_act_mul = sem("act_mul")
        s_shgu_done = sem("shgu_done")
        s_a_hi = sem("a_hi")
        s_silu_done = sem("silu_done")
        s_a_lo = sem("a_lo")
        s_og_ready = sem("og_ready")
        s_shdn_done = sem("shdn_done")
        s_ea_ready = sem("ea_ready")
        s_tile0_in = sem("tile0_in")
        s_tile1_in = sem("tile1_in")
        s_tile2_in = sem("tile2_in")
        s_tile3_in = sem("tile3_in")
        s_tile0_out = sem("tile0_out")
        s_tile1_out = sem("tile1_out")
        s_tile2_out = sem("tile2_out")
        s_tile3_out = sem("tile3_out")
        s_ext_done = sem("ext_done")
        s_ex_lo = sem("ex_lo")
        s_egu_done = sem("egu_done")
        s_eat_done = sem("eat_done")
        s_ea_lo = sem("ea_lo")
        s_edn_done = sem("edn_done")
        s_ex_hi = sem("ex_hi")
        s_esilu = sem("esilu")
        s_ea_hi = sem("ea_hi")
        s_ey_ready = sem("ey_ready")
        s_esecond = sem("esecond")
        s_emeta = sem("emeta")
        s_pad_written = sem("pad_written")
        s_pad_out = sem("pad_out")
        s_y0_in = sem("y0_in")
        s_y1_in = sem("y1_in")
        s_fin_ready = sem("fin_ready")
        s_stored = sem("stored")
        s_fin_sum = sem("fin_sum")
        s_fin_mul = sem("fin_mul")

        modrow = nc.dram_tensor("modrow", (B, 5 * D), F32, kind="Internal").ap()
        x1_dram = nc.dram_tensor("x1_dram", (B, S, D), F32, kind="Internal").ap()
        routed_in = nc.dram_tensor("routed_in", (NE * REGION, ROW), F32, kind="Internal").ap()
        routed_out = nc.dram_tensor("routed_out", (2 * T, D), F32, kind="Internal").ap()

        ident = sb("ident", [P, P])
        before = sb("before", [P, P], BF16)
        ones = sb("ones", [P, P], BF16)
        lower = sb("lower", [P, NE, NE])
        token_id = sb("token_id", [P, B * TT])
        eidx = sb("eidx", [P, NE])
        erow = sb("erow", [P, NE])
        step128 = sb("step128", [P, T // P])
        tidx = sb("tidx", [P, NT])
        cols = sb("cols", [P, 3 * KD + 2])
        lw = sb("lw", [P, 4])

        wrt = hilo("wrt", [P, KD, NE])
        wsgu = hilo("wsgu", [P, KD, 2 * FS])
        wsd = hilo("wsd", [P, len(FT), D])
        h2T = hilo("h2T", [P, KD, T])

        sacol = sb("sacol", [P, 2 * KD, B])

        h2all = sb("h2all", [P, B * TT, ROW])
        lgall = sb("lgall", [P, T])
        eps_t = sb("eps_t", [P, 2 * TT])
        minus_half = sb("minus_half", [P, 2 * TT])

        eid_f = sb("eid_f", [P, NT])
        tile_u = sb("tile_u", [1, 2, NT], I32)
        pad_u = sb("pad_u", [1, NE], I32)

        attention_weights = ctx.enter_context(ExitStack())

        def hilo_attention(name, shape):
            return tuple(attention_weights.enter_context(nc.sbuf_tensor(name + x, shape, F32R)) for x in ("_hi", "_lo"))

        wqkv = hilo_attention("wqkv", [P, KD, 3 * D])
        wproj = hilo_attention("wproj", [P, KD, D])

        psum = [ctx.enter_context(nc.psum_tensor(f"bank{i}", [P, 512], F32)) for i in range(8)]

        def parts(t, *idx):
            return t[0][idx], t[1][idx]

        def mm3(pe, out_ap, l, r, start, stop):
            pe.matmul(out_ap, l[1], r[0], start=start, stop=False)
            pe.matmul(out_ap, l[0], r[1], start=False, stop=False)
            return pe.matmul(out_ap, l[0], r[0], start=False, stop=stop)

        with ExitStack() as early:
            def tb(name, shape, dt=F32):
                return early.enter_context(nc.sbuf_tensor(name, shape, dt))

            wmod_s = tb("wmod_s", [P, KD, 6 * D])
            cT = tb("cT", [P, KD, B])
            cS = tb("cS", [P, KD, B])
            stage = tb("stage", [P, 4 * D * KD + KD * NE + KD * 2 * FS + len(FT) * D])
            modS = tb("modS", [B, 6 * D])
            mrow = tb("mrow", [B, 5, D])
            bvrep = tb("bvrep", [P, KD, B])
            gsgn = tb("gsgn", [B, 2, D])
            bprow = tb("bprow", [B, D])
            at, spans = 0, {}
            for name, n in (("qkv", KD * 3 * D), ("proj", KD * D), ("rt", KD * NE), ("sgu", KD * 2 * FS), ("sd", len(FT) * D)):
                spans[name] = (at, at + n)
                at += n

            def staged(name):
                return stage[:, spans[name][0]:spans[name][1]]

            with nc.Block() as block:
                @block.sync
                def _(sp):
                    sp.dma_start(cT[:], c_t.rearrange("(k p) b -> p k b", p=P)).then_inc(s_c_in, 16)
                    sp.dma_start(wmod_s[:], w_mod.rearrange("(k p) n -> p k n", p=P)).then_inc(s_wmod_in, 16)
                    sp.dma_start(staged("qkv").rearrange("p (k n) -> p k n", k=KD),
                                 w_qkv.rearrange("(k p) n -> p k n", p=P)).then_inc(s_wqkv_in, 16)
                    sp.dma_start(staged("proj").rearrange("p (k n) -> p k n", k=KD),
                                 w_proj.rearrange("(k p) n -> p k n", p=P)).then_inc(s_wproj_in, 16)
                    sp.dma_start(staged("rt").rearrange("p (k n) -> p k n", k=KD),
                                 router_t.rearrange("(k p) n -> p k n", p=P)).then_inc(s_wrt_in, 16)
                    sp.dma_start(staged("sgu").rearrange("p (k n) -> p k n", k=KD),
                                 sh_gu_t.rearrange("(k p) n -> p k n", p=P)).then_inc(s_wsgu_in, 16)
                    for j, (f, m) in enumerate(FT):
                        sp.dma_start(staged("sd").rearrange("p (k n) -> p k n", k=len(FT))[0:m, j, :],
                                     sh_down_t[f:f + m, :]).then_inc(s_wsd_in, 16)
                    sp.wait_ge(s_mrow_ready, 1)
                    sp.dma_start(modrow, mrow[:].rearrange("b j d -> b (j d)")).then_inc(s_modrow_out, 16)
                    sp.wait_ge(s_modrow_out, 16)

                @block.gpsimd
                def _(pool):
                    pool.memset(ident[:], 0.0).then_inc(s_const, 1)
                    pool.memset(before[:], 0.0).then_inc(s_const, 1)
                    pool.wait_ge(s_const, 2)
                    pool.affine_select(out=ident[:], in_=ident[:], compare_op=ALU.not_equal, fill=1.0,
                                       base=0, pattern=[[-1, P]], channel_multiplier=1).then_inc(s_ident_ready, 1)
                    pool.affine_select(out=before[:], in_=before[:], compare_op=ALU.is_ge, fill=1.0,
                                       base=0, pattern=[[-1, P]], channel_multiplier=1).then_inc(s_const, 1)
                    pool.memset(ones[:], 1.0).then_inc(s_const, 1)
                    pool.memset(lower[:], 0.0).then_inc(s_const, 1)
                    pool.wait_ge(s_const, 5)
                    for j in range(1, NE):
                        pool.memset(lower[:, j, 0:j], 1.0).then_inc(s_const, 1)
                    pool.iota(token_id[:], pattern=[[P, B * TT]], base=0, channel_multiplier=1,
                              allow_small_or_imprecise_dtypes=True).then_inc(s_const, 1)
                    pool.memset(minus_half[:], -0.5).then_inc(s_const, 1)
                    pool.memset(eps_t[:], EPS).then_inc(s_const, 1)
                    for t, step in ((eidx, 1), (erow, REGION), (step128, P), (tidx, 1)):
                        pool.iota(t[:], pattern=[[step, t.shape[1]]], base=0, channel_multiplier=0,
                                  allow_small_or_imprecise_dtypes=True).then_inc(s_const, 1)
                    pool.wait_ge(s_const, 5 + NE - 1 + 7)

                @block.scalar
                def _(act):
                    act.dma_start(cols[:, 0:3 * KD], b_cols).then_inc(s_cols_in, 16)
                    act.dma_start(cols[:, 3 * KD:3 * KD + 1], gate_col).then_inc(s_cols_in, 16)
                    act.dma_start(lw[:, 0:1], cam_w0.partition_broadcast(P)).then_inc(s_cols_in, 16)
                    act.dma_start(lw[:, 1:2], cam_w1.partition_broadcast(P)).then_inc(s_cols_in, 16)
                    act.dma_start(bprow[:], b_proj.partition_broadcast(B)).then_inc(s_cols_in, 16)
                    act.wait_ge(s_c_in, 16)
                    act.activation(cS[:], cT[:], ACT.Exp, scale=-1.0).then_inc(s_c_exp, 1)
                    act.wait_ge(s_lw_sum, 1)
                    act.activation(lw[:, 3:4], lw[:, 2:3], ACT.Exp, scale=-1.0).then_inc(s_lw_exp, 1)
                    act.wait_ge(s_wqkv_in, 16)
                    q3 = staged("qkv").rearrange("p (k n) -> p k n", k=KD)
                    act.activation(wqkv[0][:, :, 0:D], q3[:, :, 0:D], ACT.Copy).then_inc(s_whi, 1)
                    act.wait_ge(s_kscaled, 1)
                    act.activation(wqkv[0][:, :, D:3 * D], q3[:, :, D:3 * D], ACT.Copy).then_inc(s_whi, 1)
                    for src, name, dst in ((s_wproj_in, "proj", wproj), (s_wrt_in, "rt", wrt), (s_wsgu_in, "sgu", wsgu)):
                        act.wait_ge(src, 16)
                        act.activation(dst[0][:], staged(name).rearrange("p (k n) -> p k n", k=KD),
                                       ACT.Copy).then_inc(s_whi, 1)
                    act.wait_ge(s_wsd_in, 16 * len(FT))
                    d3 = staged("sd").rearrange("p (k n) -> p k n", k=len(FT))
                    for j, (f, m) in enumerate(FT):
                        act.activation(wsd[0][0:m, j, :], d3[0:m, j, :], ACT.Copy).then_inc(s_whi, 1)

                @block.vector
                def _(dve):
                    dve.wait_ge(s_cols_in, 16 * 5)
                    dve.tensor_copy(bvrep[:], cols[:, 2 * KD:3 * KD].unsqueeze(2).to_broadcast([P, KD, B])).then_inc(s_bvrep_ready, 1)
                    dve.wait_ge(s_c_exp, 1)
                    dve.tensor_scalar(cS[:], cS[:], 1.0, None, ALU.add).then_inc(s_c_chain, 1)
                    dve.wait_ge(s_c_chain, 1)
                    dve.reciprocal(cS[:], cS[:]).then_inc(s_c_chain, 1)
                    dve.wait_ge(s_c_chain, 2)
                    dve.tensor_tensor(cS[:], cS[:], cT[:], ALU.mult).then_inc(s_silu_c, 1)
                    dve.scalar_tensor_tensor(lw[:, 2:3], lw[:, 1:2], LAYER_DEPTH, lw[:, 0:1],
                                             ALU.mult, ALU.add).then_inc(s_lw_sum, 1)
                    dve.tensor_scalar(cols[:, KD:2 * KD], cols[:, KD:2 * KD], SCALE, None, ALU.mult).then_inc(s_cols_ready, 1)
                    dve.tensor_tensor(cols[:, 3 * KD + 1:3 * KD + 2], cols[:, 3 * KD:3 * KD + 1],
                                      cols[:, 2 * KD:2 * KD + 1], ALU.mult).then_inc(s_cols_ready, 1)
                    dve.wait_ge(s_lw_exp, 1)
                    dve.tensor_scalar(lw[:, 3:4], lw[:, 3:4], 1.0, None, ALU.add).then_inc(s_c_chain, 1)
                    dve.wait_ge(s_c_chain, 3)
                    dve.reciprocal(lw[:, 3:4], lw[:, 3:4]).then_inc(s_cols_ready, 1)
                    q3 = staged("qkv").rearrange("p (k n) -> p k n", k=KD)
                    dve.wait_ge(s_wqkv_in, 16)
                    dve.tensor_scalar(q3[:, :, D:2 * D], q3[:, :, D:2 * D], SCALE, None, ALU.mult).then_inc(s_kscaled, 1)
                    dve.wait_ge(s_whi, 1)
                    dve.tensor_tensor(wqkv[1][:, :, 0:D], q3[:, :, 0:D], wqkv[0][:, :, 0:D].bitcast(F32),
                                      ALU.subtract).then_inc(s_wlo, 1)
                    dve.wait_ge(s_kscaled, 1)
                    dve.wait_ge(s_whi, 2)
                    dve.tensor_tensor(wqkv[1][:, :, D:3 * D], q3[:, :, D:3 * D], wqkv[0][:, :, D:3 * D].bitcast(F32),
                                      ALU.subtract).then_inc(s_wlo, 1)
                    dve.wait_ge(s_mod_mm, 1)
                    for j in range(3):
                        dve.tensor_copy(modS[:, 512 * j:512 * (j + 1)], psum[j][0:B, :]).then_inc(s_mod_copied, 1)
                    dve.wait_ge(s_mod_copied, 3)
                    for n, g in enumerate((2, 5)):
                        src = modS[:, g * D:(g + 1) * D]
                        dve.tensor_scalar(gsgn[:, n, :], src, 0.0, 2.0, ALU.is_ge, ALU.mult).then_inc(s_guard, 1)
                        dve.scalar_tensor_tensor(mrow[:, 4 * n, :], src, -1.0, src, ALU.mult, ALU.max).then_inc(s_guard, 1)
                    dve.wait_ge(s_guard, 4)
                    for n in range(2):
                        dve.tensor_scalar(mrow[:, 4 * n, :], mrow[:, 4 * n, :], GUARD, None, ALU.max).then_inc(s_guard, 1)
                    dve.wait_ge(s_guard, 6)
                    for n in range(2):
                        dve.scalar_tensor_tensor(mrow[:, 4 * n, :], gsgn[:, n, :], 1.0, mrow[:, 4 * n, :],
                                                 ALU.subtract, ALU.mult).then_inc(s_guard, 1)
                    dve.tensor_scalar(mrow[:, 2, :], modS[:, 4 * D:5 * D], 1.0, None, ALU.add).then_inc(s_guard, 1)
                    dve.tensor_copy(mrow[:, 3, :], modS[:, 3 * D:4 * D]).then_inc(s_guard, 1)
                    dve.wait_ge(s_guard, 10)
                    dve.wait_ge(s_bvp_done, 1)
                    dve.tensor_tensor(bprow[:], bprow[:], psum[4][0:B, 0:D], ALU.add).then_inc(s_bp_ready, 1)
                    dve.wait_ge(s_bp_ready, 1)
                    dve.tensor_tensor(mrow[:, 1, :], mrow[:, 0, :], bprow[:], ALU.mult).then_inc(s_mrow_ready, 1)
                    dve.wait_ge(s_modT, 1)
                    mt = psum[3][:, 0:2 * KD * B].rearrange("p (j b) -> p j b", b=B)
                    dve.tensor_copy(sacol[:, 0:KD, :], mt[:, 0:KD, :]).then_inc(s_sacol_ready, 1)
                    dve.tensor_scalar(sacol[:, KD:2 * KD, :], mt[:, KD:2 * KD, :], 1.0, None, ALU.add).then_inc(s_sacol_ready, 1)
                    for n, (name, dst) in enumerate((("proj", wproj), ("rt", wrt), ("sgu", wsgu))):
                        dve.wait_ge(s_whi, 3 + n)
                        dve.tensor_tensor(dst[1][:], staged(name).rearrange("p (k n) -> p k n", k=KD),
                                          dst[0][:].bitcast(F32), ALU.subtract).then_inc(s_wlo, 1)
                    d3 = staged("sd").rearrange("p (k n) -> p k n", k=len(FT))
                    for j, (f, m) in enumerate(FT):
                        dve.wait_ge(s_whi, 6 + j)
                        dve.tensor_tensor(wsd[1][0:m, j, :], d3[0:m, j, :], wsd[0][0:m, j, :].bitcast(F32),
                                          ALU.subtract).then_inc(s_wlo, 1)

                @block.tensor
                def _(pe):
                    pe.wait_ge(s_silu_c, 1)
                    pe.wait_ge(s_wmod_in, 16)
                    for j in range(3):
                        for k in range(KD):
                            last = pe.matmul(psum[j][0:B, :], cS[:, k, :], wmod_s[:, k, 512 * j:512 * (j + 1)],
                                             start=(k == 0), stop=(k == KD - 1))
                    last.then_inc(s_mod_mm, 1)
                    pe.wait_ge(s_bvrep_ready, 1)
                    pe.wait_ge(s_wproj_in, 16)
                    wp3 = staged("proj").rearrange("p (k n) -> p k n", k=KD)
                    for k in range(KD):
                        last = pe.matmul(psum[4][0:B, 0:D], bvrep[:, k, :], wp3[:, k, :], start=(k == 0), stop=(k == KD - 1))
                    last.then_inc(s_bvp_done, 1)
                    pe.wait_ge(s_mod_copied, 3)
                    pe.wait_ge(s_ident_ready, 1)
                    for j in range(2 * KD):
                        last = pe.transpose(psum[3][:, j * B:(j + 1) * B], modS[:, j * P:(j + 1) * P], ident[0:B, 0:B])
                    last.then_inc(s_modT, 1)

        with ExitStack() as attention:
            def tb(name, shape, dt=F32):
                return attention.enter_context(nc.sbuf_tensor(name, shape, dt))

            def two(name, shape, dt=F32):
                return [tb(f"{name}{u}", shape, dt) for u in range(2)]

            def two_hilo(name, shape):
                return [(tb(f"{name}{u}_hi", shape, F32R), tb(f"{name}{u}_lo", shape, F32R)) for u in range(2)]

            xa = two("xa", [P, TT, D])
            xr = two("xr", [P, TT, D])
            mb = two("mb", [P, 4, D])
            ht = two("ht", [P, KD, S])
            hT = two_hilo("hT", [P, KD, S])
            QT = two_hilo("QT", [P, KD, S])
            KT = two_hilo("KT", [P, KD, S])
            VV = two_hilo("VV", [P, TT, D])
            qf = two("qf", [P, S])
            th = two("th", [P, S])
            pr = two("pr", [P, TT, S])
            PT = two_hilo("PT", [P, KD, S])
            h2 = two("h2", [P, TT, D])
            yb = two("yb", [P, TT, D])
            bst1 = tb("bst1", [P, 2 * TT, 6])
            bst2 = tb("bst2", [P, 2 * TT, 6])
            mv1 = tb("mv1", [P, 2 * TT, 2])
            mv2 = tb("mv2", [P, 2 * TT, 2])
            spare1 = tb("spare1", [P, 1])
            spare2 = tb("spare2", [P, 1])
            rs1 = tb("rs1", [P, 2 * TT])
            rs2 = tb("rs2", [P, 2 * TT])
            nm = two("nm", [P, 2, TT])
            ls = two("ls", [P, 2, TT])
            rl = two("rl", [P, 2, TT])
            Sb, TR, CO, QK = psum[0:2], psum[2:4], psum[4:6], psum[6:8]

            def bank(t, a=2):
                return t[:, :].rearrange("p (a n) -> p a n", a=a)

            wq_ = lambda k, m: parts(wqkv, slice(None), k, slice(m * P, (m + 1) * P))

            def pe_xt(pe, b, u):
                pe.wait_ge(s_xn_ready, b + 1)
                for d in range(KD):
                    for t in range(TT):
                        last = pe.transpose(TR[u][:, d * S + t * P:d * S + (t + 1) * P],
                                            xa[u][:, t, d * P:(d + 1) * P], ident[:])
                last.then_inc(s_xt_done, 1)

            def pe_qk(pe, b, u):
                pe.wait_ge(s_h_lo, b + 1)
                if u == 1:
                    pe.wait_ge(s_qk_hi, b)
                    pe.wait_ge(s_qk_lo, b)
                for half, dst in enumerate(QK):
                    for m in range(KD):
                        for k in range(KD):
                            last = mm3(pe, dst[:, m * S:(m + 1) * S], wq_(k, half * KD + m),
                                       parts(hT[u], slice(None), k), k == 0, k == KD - 1)
                    last.then_inc(s_qk_done, 1)

            def pe_v(pe, b, u):
                for t in range(TT):
                    for k in range(KD):
                        last = mm3(pe, QK[u][:, t * D:(t + 1) * D],
                                   parts(hT[u], slice(None), k, slice(t * P, (t + 1) * P)),
                                   parts(wqkv, slice(None), k, slice(2 * D, 3 * D)), k == 0, k == KD - 1)
                last.then_inc(s_v_done, 1)

            def pe_scores(pe, b, u, second):
                if second:
                    pe.wait_ge(s_qp_hi, b + 1)
                    pe.wait_ge(s_qp_lo, b + 1)
                else:
                    pe.wait_ge(s_qk_hi, b + 1)
                    pe.wait_ge(s_qk_lo, b + 1)
                ks = KD if second else 1
                for t in range(TT):
                    for k in range(ks):
                        last = mm3(pe, Sb[u][:, t * S:(t + 1) * S],
                                   parts(QT[u], slice(None), k, slice(t * P, (t + 1) * P)),
                                   parts(KT[u], slice(None), k), k == 0, k == ks - 1)
                last.then_inc(s_s2_done if second else s_s1_done, 1)

            def pe_pt(pe, b, u, second):
                pe.wait_ge(s_exp2 if second else s_norm1, b + 1)
                for k in range(TT):
                    for t in range(TT):
                        last = pe.transpose(TR[u][:, k * S + t * P:k * S + (t + 1) * P],
                                            pr[u][:, t, k * P:(k + 1) * P], ident[:])
                last.then_inc(s_pt2_done if second else s_pt1_done, 1)

            def pe_ctx(pe, b, u, second):
                if second:
                    pe.wait_ge(s_pt2_hi, b + 1)
                    pe.wait_ge(s_pt2_lo, b + 1)
                else:
                    pe.wait_ge(s_pt1_hi, b + 1)
                    pe.wait_ge(s_pt1_lo, b + 1)
                    pe.wait_ge(s_v_hi, b + 1)
                    pe.wait_ge(s_v_lo, b + 1)
                for m in range(KD if second else 1):
                    for k in range(TT):
                        last = mm3(pe, CO[u][:, m * S:(m + 1) * S],
                                   parts(VV[u], slice(None), k, slice(m * P, (m + 1) * P)),
                                   parts(PT[u], slice(None), k), k == 0, k == TT - 1)
                last.then_inc(s_c2_done if second else s_c1_done, 1)

            def pe_out(pe, b, u):
                pe.wait_ge(s_ctx_hi, b + 1)
                pe.wait_ge(s_ctx_lo, b + 1)
                for t in range(TT):
                    for m in range(KD):
                        last = mm3(pe, CO[u][:, t * D:(t + 1) * D],
                                   parts(PT[u], slice(None), m, slice(t * P, (t + 1) * P)),
                                   parts(wproj, slice(None), m), m == 0, m == KD - 1)
                last.then_inc(s_o_done, 1)

            def pe_h2t(pe, b, u):
                pe.wait_ge(s_h2_ready, b + 1)
                for d in range(KD):
                    for t in range(TT):
                        last = pe.transpose(TR[u][:, d * S + t * P:d * S + (t + 1) * P],
                                            h2[u][:, t, d * P:(d + 1) * P], ident[:])
                last.then_inc(s_h2t_done, 1)

            def pe_logits(pe, b, u):
                pe.wait_ge(s_h2_hi, b + 1)
                pe.wait_ge(s_h2_lo, b + 1)
                for k in range(KD):
                    last = mm3(pe, Sb[u][0:NE, 0:S], parts(wrt, slice(None), k),
                               parts(h2T, slice(None), k, ds(b * S, S)), k == 0, k == KD - 1)
                last.then_inc(s_lg_done, 1)

            def act_exp(act, b, u, second):
                act.wait_ge(s_max2 if second else s_max1, b + 1)
                i = int(second)
                for t in range(TT):
                    last = act.activation(pr[u][:, t, :], Sb[u][:, t * S:(t + 1) * S], ACT.Exp,
                                          bias=nm[u][:, i, t:t + 1], accum_out=ls[u][:, i, t:t + 1])
                last.then_inc(s_exp2 if second else s_exp1, 1)

            def act_norm(act, b, u):
                act.wait_ge(s_rl1, b + 1)
                for t in range(TT):
                    last = act.activation(pr[u][:, t, :], pr[u][:, t, :], ACT.Copy, scale=rl[u][:, 0, t:t + 1])
                last.then_inc(s_norm1, 1)

            def act_copy(act, ready, b, dst, src, done):
                act.wait_ge(ready, b + 1)
                act.activation(dst, src, ACT.Copy).then_inc(done, 1)

            def act_h(act, b, u):
                act.wait_ge(s_xt_done, b + 1)
                for d in range(KD):
                    last = act.activation(ht[u][:, d, :], TR[u][:, d * S:(d + 1) * S], ACT.Identity,
                                          scale=sacol[:, KD + d, ds(b, 1)], bias=sacol[:, d, ds(b, 1)])
                last.then_inc(s_ht_ready, 1)

            def act_qk(act, b, u):
                for half, dst in enumerate((QT, KT)):
                    act.wait_ge(s_qk_done, 2 * b + 1 + half)
                    for m in range(KD):
                        last = act.activation(dst[u][0][:, m, :], QK[half][:, m * S:(m + 1) * S], ACT.Identity,
                                              bias=cols[:, half * KD + m:half * KD + m + 1])
                last.then_inc(s_qk_hi, 1)

            def act_tanh(act, b, u):
                act.wait_ge(s_c1_done, b + 1)
                act.activation(th[u][:], CO[u][:, 0:S], ACT.Tanh, scale=cols[:, 3 * KD:3 * KD + 1],
                               bias=cols[:, 3 * KD + 1:3 * KD + 2]).then_inc(s_tanh_done, 1)

            def act_ctx(act, b, u):
                act.wait_ge(s_c2_done, b + 1)
                act.activation(PT[u][0][:], bank(CO[u]), ACT.Copy).then_inc(s_ctx_hi, 1)

            def dve_max(dve, b, u, second):
                dve.wait_ge(s_s2_done if second else s_s1_done, b + 1)
                dve.tensor_reduce(nm[u][:, int(second), :], bank(Sb[u]), AX.X, ALU.max,
                                  negate=True).then_inc(s_max2 if second else s_max1, 1)

            def dve_rl(dve, b, u, second):
                i = int(second)
                dve.wait_ge(s_exp2 if second else s_exp1, b + 1)
                dve.reciprocal(rl[u][:, i, :], ls[u][:, i, :]).then_inc(s_rl2 if second else s_rl1, 1)

            def dve_lo(dve, ready, b, src, hi, lo, done):
                dve.wait_ge(ready, b + 1)
                dve.tensor_tensor(lo, src, hi.bitcast(F32), ALU.subtract).then_inc(done, 1)

            def dve_h(dve, b, u):
                dve.wait_ge(s_ht_ready, b + 1)
                dve.tensor_copy(hT[u][0][:], ht[u][:]).then_inc(s_h_hi, 1)
                dve.wait_ge(s_h_hi, b + 1)
                dve.tensor_tensor(hT[u][1][:], ht[u][:], hT[u][0][:].bitcast(F32), ALU.subtract).then_inc(s_h_lo, 1)

            def biased_lo(dve, dst, src, bias, m):
                return dve.scalar_tensor_tensor(dst[1][:, m, :], src[:, m * S:(m + 1) * S], bias,
                                                dst[0][:, m, :].bitcast(F32), ALU.add, ALU.subtract)

            def dve_qk(dve, b, u):
                dve.wait_ge(s_qk_hi, b + 1)
                for half, dst in enumerate((QT, KT)):
                    for m in range(KD):
                        last = biased_lo(dve, dst[u], QK[half], cols[:, half * KD + m:half * KD + m + 1], m)
                last.then_inc(s_qk_lo, 1)

            def dve_qp(dve, b, u):
                dve.wait_ge(s_tanh_done, b + 1)
                dve.wait_ge(s_qf_ready, b + 1)
                dve.scalar_tensor_tensor(qf[u][:], th[u][:], lw[:, 3:4], qf[u][:], ALU.mult, ALU.add).then_inc(s_qp_ready, 1)

            def dve_x1(dve, b, u):
                dve.wait_ge(s_o_done, b + 1)
                dve.wait_ge(s_rl2, b + 1)
                dve.wait_ge((s_mb0_in, s_mb1_in)[u], 8 * (b - u + 2))
                for t in range(TT):
                    last = dve.scalar_tensor_tensor(yb[u][:, t, :], CO[u][:, t * D:(t + 1) * D], rl[u][:, 1, t:t + 1],
                                                    mb[u][:, 0, :], ALU.mult, ALU.mult)
                last.then_inc(s_y_ready, 1)

            def dve_stats(dve, p, src, bst, mv, spare, stats, var, ready):
                for u in range(2):
                    dve.wait_ge(*ready(u))
                    for t in range(TT):
                        last = dve.bn_stats(bst[:, u * TT + t, :], src[u][:, t, :])
                last.then_inc(stats, 1)
                dve.wait_ge(stats, 2 * p + 1)
                dve.memset(spare[:], 0.0).then_inc(stats, 1)
                for j in range(2 * TT):
                    last = dve.bn_aggr(mv[:, j, :], bst[:, j, :])
                last.then_inc(var, 1)

            def dve_ln1_stats(dve, p):
                dve_stats(dve, p, xa, bst1, mv1, spare1, s_stats1, s_var1, lambda u: ((s_xa0_in, s_xa1_in)[u], 16 * (p + 1)))

            def dve_ln2_stats(dve, p):
                dve_stats(dve, p, xr, bst2, mv2, spare2, s_stats2, s_var2, lambda u: (s_x1_ready, 2 * p + 1 + u))

            def dve_normalise(dve, p, rstd, src, dst, mv, rs, done):
                dve.wait_ge(rstd, 2 * p + 2)
                for u in range(2):
                    for t in range(TT):
                        j = u * TT + t
                        last = dve.tensor_scalar(dst[u][:, t, :], src[u][:, t, :], mv[:, j, 0:1], rs[:, j:j + 1],
                                                 ALU.subtract, ALU.mult)
                    last.then_inc(done, 1)

            def pool_xg(pool, b, u):
                pool.wait_ge((s_xr0_in, s_xr1_in)[u], 8 * (b - u + 2))
                pool.wait_ge((s_mb0_in, s_mb1_in)[u], 8 * (b - u + 2))
                pool.tensor_tensor(xr[u][:], xr[u][:], mb[u][:, 1:2, :].to_broadcast([P, TT, D]), ALU.add).then_inc(s_xg_ready, 1)

            def pool_rstd(pool, p, var, mv, rs, rstd):
                pool.wait_ge(var, p + 1)
                pool.tensor_tensor(rs[:], mv[:, :, 1], eps_t[:], ALU.add).then_inc(rstd, 1)
                pool.wait_ge(rstd, 2 * p + 1)
                pool.tensor_tensor(rs[:], rs[:], minus_half[:], ALU.pow).then_inc(rstd, 1)

            def pool_qf(pool, b, u):
                pool.wait_ge(s_qk_lo, b + 1)
                pool.tensor_tensor(qf[u][:], QT[u][0][:, 0, :].bitcast(F32), QT[u][1][:, 0, :].bitcast(F32),
                                   ALU.add).then_inc(s_qf_ready, 1)

            def pool_x1(pool, b, u):
                pool.wait_ge(s_xg_ready, b + 1)
                pool.wait_ge(s_y_ready, b + 1)
                pool.tensor_tensor(xr[u][:], xr[u][:], yb[u][:], ALU.add).then_inc(s_x1_ready, 1)

            def pool_h2(pool, b, u):
                pool.wait_ge(s_xn2_ready, b + 1)
                if not (type(b) is int and b < 2):
                    pool.wait_ge((s_h2c0, s_h2c1)[u], 8 * (b - u))
                pool.tensor_tensor(h2[u][:], yb[u][:], mb[u][:, 2:3, :].to_broadcast([P, TT, D]), ALU.mult).then_inc(s_h2_chain, 1)
                pool.wait_ge(s_h2_chain, b + 1)
                pool.tensor_tensor(h2[u][:], h2[u][:], mb[u][:, 3:4, :].to_broadcast([P, TT, D]), ALU.add).then_inc(s_h2_ready, 1)

            def pair_of(p):
                return ((2 * p, 0), (2 * p + 1, 1))

            def pe_front(pe, p):
                for b, u in pair_of(p):
                    pe_xt(pe, b, u)
                for b, u in pair_of(p):
                    pe_qk(pe, b, u)

            def pe_turn(pe, p, post, front):
                for b, u in pair_of(p):
                    pe_scores(pe, b, u, False)
                for b, u in pair_of(p):
                    pe_v(pe, b, u)
                for b, u in pair_of(p):
                    pe_pt(pe, b, u, False)
                for b, u in pair_of(p):
                    pe_ctx(pe, b, u, False)
                if front:
                    for b, u in pair_of(p + 1):
                        pe_xt(pe, b, u)
                for b, u in pair_of(p):
                    pe_scores(pe, b, u, True)
                if front:
                    pe_qk(pe, 2 * p + 2, 0)
                for b, u in pair_of(p):
                    pe_pt(pe, b, u, True)
                if front:
                    pe_qk(pe, 2 * p + 3, 1)
                for b, u in pair_of(p):
                    pe_ctx(pe, b, u, True)
                if post:
                    for b, u in pair_of(p - 1):
                        pe_h2t(pe, b, u)
                for b, u in pair_of(p):
                    pe_out(pe, b, u)
                    if post:
                        pe_logits(pe, b - 2, u)
                if post:
                    pe.wait_ge(s_lg_copied, 2 * p)

            def act_turn(act, p, post, front):
                for b, u in pair_of(p):
                    act_exp(act, b, u, False)
                for b, u in pair_of(p):
                    act_norm(act, b, u)
                for b, u in pair_of(p):
                    act_copy(act, s_v_done, b, VV[u][0][:], bank(QK[u]), s_v_hi)
                for b, u in pair_of(p):
                    act_copy(act, s_pt1_done, b, PT[u][0][:], bank(TR[u]), s_pt1_hi)
                for b, u in pair_of(p):
                    act_tanh(act, b, u)
                if front:
                    act_h(act, 2 * p + 2, 0)
                for b, u in pair_of(p):
                    act_copy(act, s_qp_ready, b, QT[u][0][:, 0, :], qf[u][:], s_qp_hi)
                if front:
                    act_h(act, 2 * p + 3, 1)
                for b, u in pair_of(p):
                    act_exp(act, b, u, True)
                if front:
                    act_qk(act, 2 * p + 2, 0)
                for b, u in pair_of(p):
                    act_copy(act, s_pt2_done, b, PT[u][0][:], bank(TR[u]), s_pt2_hi)
                if front:
                    act_qk(act, 2 * p + 3, 1)
                for b, u in pair_of(p):
                    act_ctx(act, b, u)
                if post:
                    act_post(act, p - 1)

            def act_post(act, p):
                for b, u in pair_of(p):
                    act_copy(act, s_h2t_done, b, h2T[0][:, :, ds(b * S, S)], bank(TR[u]), s_h2_hi)
                for b, u in pair_of(p):
                    act_copy(act, s_lg_done, b, lgall[0:NE, ds(b * S, S)], Sb[u][0:NE, 0:S], s_lg_copied)

            def dve_turn(dve, p, post, front):
                for b, u in pair_of(p):
                    dve_max(dve, b, u, False)
                if front:
                    dve_ln1_stats(dve, p + 1)
                for b, u in pair_of(p):
                    dve_rl(dve, b, u, False)
                for b, u in pair_of(p):
                    dve_lo(dve, s_v_hi, b, bank(QK[u]), VV[u][0][:], VV[u][1][:], s_v_lo)
                if front:
                    dve_normalise(dve, p + 1, s_rstd1, xa, xa, mv1, rs1, s_xn_ready)
                for b, u in pair_of(p):
                    dve_lo(dve, s_pt1_hi, b, bank(TR[u]), PT[u][0][:], PT[u][1][:], s_pt1_lo)
                if post:
                    dve_ln2_stats(dve, p - 1)
                for b, u in pair_of(p):
                    dve_qp(dve, b, u)
                for b, u in pair_of(p):
                    dve_lo(dve, s_qp_hi, b, qf[u][:], QT[u][0][:, 0, :], QT[u][1][:, 0, :], s_qp_lo)
                if front:
                    dve_h(dve, 2 * p + 2, 0)
                dve_max(dve, 2 * p, 0, True)
                if front:
                    dve_h(dve, 2 * p + 3, 1)
                dve_max(dve, 2 * p + 1, 1, True)
                if post:
                    dve_normalise(dve, p - 1, s_rstd2, xr, yb, mv2, rs2, s_xn2_ready)
                for b, u in pair_of(p):
                    dve_rl(dve, b, u, True)
                if front:
                    dve_qk(dve, 2 * p + 2, 0)
                for b, u in pair_of(p):
                    dve_lo(dve, s_pt2_hi, b, bank(TR[u]), PT[u][0][:], PT[u][1][:], s_pt2_lo)
                if front:
                    dve_qk(dve, 2 * p + 3, 1)
                for b, u in pair_of(p):
                    dve_lo(dve, s_ctx_hi, b, bank(CO[u]), PT[u][0][:], PT[u][1][:], s_ctx_lo)
                if post:
                    dve_h2_lo(dve, p - 1)
                for b, u in pair_of(p):
                    dve_x1(dve, b, u)

            def dve_h2_lo(dve, p):
                for b, u in pair_of(p):
                    dve_lo(dve, s_h2_hi, b, bank(TR[u]), h2T[0][:, :, ds(b * S, S)], h2T[1][:, :, ds(b * S, S)], s_h2_lo)

            def pool_turn(pool, p, post, front):
                if front:
                    pool_rstd(pool, p + 1, s_var1, mv1, rs1, s_rstd1)
                if post:
                    pool_rstd(pool, p - 1, s_var2, mv2, rs2, s_rstd2)
                    for b, u in pair_of(p - 1):
                        pool_h2(pool, b, u)
                if front:
                    pool_qf(pool, 2 * p + 2, 0)
                    pool_qf(pool, 2 * p + 3, 1)
                for b, u in pair_of(p):
                    pool_xg(pool, b, u)
                for b, u in pair_of(p):
                    pool_x1(pool, b, u)

            def sp_front(sp, p):
                for b, u in pair_of(p):
                    if not (type(p) is int and p == 0):
                        sp.wait_ge(s_xt_done, b - 1)
                    sp.dma_start(xa[u][:], x_in[ds(b, 1)].rearrange("o (t p) d -> p (o t) d", p=P)).then_inc((s_xa0_in, s_xa1_in)[u], 16)

            def sp_mid(sp, p, first):
                for b, u in pair_of(p):
                    if not first:
                        sp.wait_ge(s_h2_ready, b - 1)
                    sp.dma_start(mb[u][:], modrow[ds(b, 1), 0:4 * D].to_broadcast([P, 4 * D]).rearrange("p (j d) -> p j d", d=D)).then_inc((s_mb0_in, s_mb1_in)[u], 16)
                    if not first:
                        sp.wait_ge((s_x1_out0, s_x1_out1)[u], 8 * (b - u))
                    sp.dma_start(xr[u][:], x_in[ds(b, 1)].rearrange("o (t p) d -> p (o t) d", p=P)).then_inc((s_xr0_in, s_xr1_in)[u], 16)

            def sp_store(sp, p):
                for b, u in pair_of(p):
                    sp.wait_ge(s_x1_ready, b + 1)
                    sp.dma_start(x1_dram[ds(b, 1)].rearrange("o (t p) d -> p (o t) d", p=P), xr[u][:]).then_inc((s_x1_out0, s_x1_out1)[u], 16)

            def sp_keep(sp, p):
                for b, u in pair_of(p):
                    sp.wait_ge(s_h2_ready, b + 1)
                    sp.dma_start(h2all[:, ds(b * TT, TT), 0:D], h2[u][:]).then_inc((s_h2c0, s_h2c1)[u], 16)

            with nc.Block() as block:
                @block.sync
                def _(sp):
                    sp_front(sp, 0)
                    sp_front(sp, 1)
                    sp_mid(sp, 0, True)
                    with sp.Fori(1, NPAIR - 1) as p:
                        sp_front(sp, p + 1)
                        sp_store(sp, p - 1)
                        sp_mid(sp, p, False)
                        sp_keep(sp, p - 1)
                    p = NPAIR - 1
                    sp_store(sp, p - 1)
                    sp_mid(sp, p, False)
                    sp_keep(sp, p - 1)
                    sp_store(sp, p)
                    sp_keep(sp, p)
                    for x in (s_x1_out0, s_x1_out1, s_h2c0, s_h2c1):
                        sp.wait_ge(x, 16 * NPAIR)

                @block.gpsimd
                def _(pool):
                    pool_rstd(pool, 0, s_var1, mv1, rs1, s_rstd1)
                    for b, u in pair_of(0):
                        pool_qf(pool, b, u)
                    pool_turn(pool, 0, False, True)
                    with pool.Fori(1, NPAIR - 1) as p:
                        pool_turn(pool, p, True, True)
                    p = NPAIR - 1
                    pool_turn(pool, p, True, False)
                    pool_rstd(pool, p, s_var2, mv2, rs2, s_rstd2)
                    for b, u in pair_of(p):
                        pool_h2(pool, b, u)

                @block.scalar
                def _(act):
                    for b, u in pair_of(0):
                        act_h(act, b, u)
                    for b, u in pair_of(0):
                        act_qk(act, b, u)
                    act_turn(act, 0, False, True)
                    with act.Fori(1, NPAIR - 1) as p:
                        act_turn(act, p, True, True)
                    act_turn(act, NPAIR - 1, True, False)
                    act_post(act, NPAIR - 1)

                @block.vector
                def _(dve):
                    dve_ln1_stats(dve, 0)
                    dve_normalise(dve, 0, s_rstd1, xa, xa, mv1, rs1, s_xn_ready)
                    for b, u in pair_of(0):
                        dve_h(dve, b, u)
                    for b, u in pair_of(0):
                        dve_qk(dve, b, u)
                    dve_turn(dve, 0, False, True)
                    with dve.Fori(1, NPAIR - 1) as p:
                        dve_turn(dve, p, True, True)
                    dve_turn(dve, NPAIR - 1, True, False)
                    p = NPAIR - 1
                    dve_ln2_stats(dve, p)
                    dve_normalise(dve, p, s_rstd2, xr, yb, mv2, rs2, s_xn2_ready)
                    dve_h2_lo(dve, p)

                @block.tensor
                def _(pe):
                    pe_front(pe, 0)
                    pe_turn(pe, 0, False, True)
                    with pe.Fori(1, NPAIR - 1) as p:
                        pe_turn(pe, p, True, True)
                    pe_turn(pe, NPAIR - 1, True, False)
                    p = NPAIR - 1
                    for b, u in pair_of(p):
                        pe_h2t(pe, b, u)
                    for b, u in pair_of(p):
                        pe_logits(pe, b, u)

        attention_weights.close()
        with ExitStack() as ffn:
            def tb(name, shape, dt=F32):
                return ffn.enter_context(nc.sbuf_tensor(name, shape, dt))

            def ring(name, n, shape, dt=F32):
                return [tb(f"{name}{r}", shape, dt) for r in range(n)]

            def ring_hilo(name, n, shape):
                return [(tb(f"{name}{r}_hi", shape, F32R), tb(f"{name}{r}_lo", shape, F32R)) for r in range(n)]

            W1 = KD * 2 * F
            wgu = (tb("wgu_hi", [P, KD, NE * 2 * F], F32R), tb("wgu_lo", [P, KD, NE * 2 * F], F32R))
            wdn = (tb("wdn_hi", [FH, 2, NE * D], F32R), tb("wdn_lo", [FH, 2, NE * D], F32R))
            wstage = ring("wstage", 2, [P, W1 + 2 * D])
            res = tb("res", [P, B, TT, D])
            gbb = ring("gbb", 2, [P, 1, D])
            x1b = ring("x1b", 2, [P, TT, D])
            sact = ring("sact", 2, [P, S])
            aact = ring("aact", 2, [P, S])
            aT = ring_hilo("aT", 2, [P, len(FT), S])
            og = ring("og", 2, [P, TT, D])
            xt_in = ring("xt_in", 4, [P, ROW])
            eT = [tuple(h[:, 0, q * S:(q + 1) * S].rearrange("p (k n) -> p k n", k=KD) for h in h2T) for q in range(2)]
            avT = [tuple(h[0:FH, 1, q * S:(q + 1) * S].rearrange("p (k n) -> p k n", k=2) for h in h2T) for q in range(2)]
            sg = [wstage[q][:, 0:F] for q in range(2)]
            av = [wstage[q][:, F:2 * F] for q in range(2)]
            yo = [wstage[q % 2][:, 2 * F + q // 2 * D:2 * F + (q // 2 + 1) * D] for q in range(4)]
            second = ring("second", 2, [P, 1])
            wt = ring("wt", 2, [P, 1])
            dest = ring("dest", 4, [P, 1], U32)

            NR = T // P
            NG = NE // 2
            taken = [0]

            def scratch(*shape):
                n = int(np.prod(shape))
                at = B // 2 * TT * D + taken[0]
                taken[0] += n
                flat = res[:].rearrange("p b t d -> p (b t d)")[:, at:at + n]
                names = "abc"[:len(shape)]
                return flat.rearrange(f"p ({' '.join(names)}) -> p {' '.join(names)}", **dict(zip(names, shape)))

            r_sc = scratch(NR, NE)
            r_mx = scratch(NR)
            r_gm = scratch(NR, NG)
            r_gt, r_eq = (lgall[:, i * NR * NE * NE:(i + 1) * NR * NE * NE].rearrange("p (t j i) -> p t j i", j=NE, i=NE)
                          for i in range(2))
            r_grank = scratch(NR, NG)
            r_rank = scratch(NR, NE)
            r_sel = scratch(2, NR, NE)
            r_both = scratch(NR, NE // 2).bitcast(BF16)
            r_pos = scratch(NR, NE)
            r_tmp = scratch(2, NR, NE)
            r_slot = scratch(2, NR)
            slot_u = tb("slot_u", [P, 2, NR], U32)
            r_w = scratch(2, NR)
            r_cnt = scratch(NE)
            r_last = scratch(NE)
            r_end = scratch(NE, T // P)
            r_tiles = scratch(NE)
            r_ends = scratch(NE)
            r_done = scratch(NT, NE)
            r_tab = scratch(4, NT)
            pad = h2all[:, 0, :]

            def gu_stage(r):
                return wstage[r][:, 0:W1].rearrange("p (k n) -> p k n", k=KD)

            def dn_stage(r):
                return wstage[r][0:FH, W1:].rearrange("p (j n) -> p j n", j=2)

            def bank2(t, n=256):
                return t[:, 0:2 * n].rearrange("p (a n) -> p a n", a=2)

            GUb = [psum[0:3], psum[3:6]]
            DN = psum[6:8]
            XTb, EGU, ATb, EDN = psum[0:2], psum[2:4], psum[4:6], psum[6:8]

            LOG = psum[6][:, 0:NR * NE]
            RNK = psum[7][:, 0:NR * NE]
            TOT = psum[6][:, 0:NE]

            def pe_logits_t(pe):
                for j in range(NR):
                    last = pe.transpose(LOG[:, j * NE:(j + 1) * NE], lgall[0:NE, j * P:(j + 1) * P], ident[0:NE, 0:NE])
                last.then_inc(s_lt_done, 1)

            def pe_rank(pe):
                pe.wait_ge(s_both_ready, 1)
                pe.matmul(RNK, before[:], r_both.rearrange("p t e -> p (t e)"), start=True, stop=False)
                for j in range(NR - 1):
                    pe.matmul(RNK[:, (j + 1) * NE:].rearrange("p (t e) -> p t e", e=NE), ones[:],
                              r_both[:, j:j + 1, :].to_broadcast([P, NR - 1 - j, NE]), start=False, stop=(j == NR - 2))
                for j in range(NR):
                    last = pe.matmul(TOT, ones[:], r_both[:, j, :], start=(j == 0), stop=(j == NR - 1))
                last.then_inc(s_rank_done, 1)

            def dve_route_scores(dve):
                dve.wait_ge(s_lt_done, 1)
                L = LOG.rearrange("p (t e) -> p t e", e=NE)
                dve.tensor_reduce(r_mx, L, AX.X, ALU.max).then_inc(s_rt_a, 1)
                dve.wait_ge(s_rt_a, 1)
                dve.tensor_tensor(r_sc, L, r_mx.unsqueeze(2).to_broadcast([P, NR, NE]), ALU.subtract).then_inc(s_rt_a, 1)

            def act_route(act):
                act.wait_ge(s_rt_a, 2)
                act.activation(r_sc, r_sc, ACT.Exp).then_inc(s_rt_exp, 1)

            def dve_route_select(dve):
                k = [0]

                def done(ins):
                    ins.then_inc(s_rt_b, 1)
                    k[0] += 1
                    return k[0]

                dve.wait_ge(s_rt_exp, 1)
                n = done(dve.tensor_reduce(r_mx, r_sc, AX.X, ALU.add))
                dve.wait_ge(s_rt_b, n)
                n = done(dve.reciprocal(r_mx, r_mx))
                dve.wait_ge(s_rt_b, n)
                n = done(dve.tensor_tensor(r_sc, r_sc, r_mx.unsqueeze(2).to_broadcast([P, NR, NE]), ALU.mult))
                dve.wait_ge(s_rt_b, n)
                pairs = r_sc.rearrange("p t (g i) -> p t g i", i=2)
                n = done(dve.tensor_tensor(r_gm, pairs[:, :, :, 0], pairs[:, :, :, 1], ALU.max))
                dve.wait_ge(s_rt_b, n)

                def rank(vals, m, out_ap):
                    a = vals[:].unsqueeze(2).to_broadcast([P, NR, m, m])
                    c = vals[:].unsqueeze(3).to_broadcast([P, NR, m, m])
                    dve.tensor_tensor(r_gt[:, :, 0:m, 0:m], a, c, ALU.is_gt)
                    n = done(dve.tensor_tensor(r_eq[:, :, 0:m, 0:m], a, c, ALU.is_equal))
                    dve.wait_ge(s_rt_b, n)
                    n = done(dve.tensor_tensor(r_eq[:, :, 0:m, 0:m], r_eq[:, :, 0:m, 0:m],
                                               lower[:, 0:m, 0:m].unsqueeze(1).to_broadcast([P, NR, m, m]), ALU.mult))
                    dve.wait_ge(s_rt_b, n)
                    n = done(dve.tensor_tensor(r_gt[:, :, 0:m, 0:m], r_gt[:, :, 0:m, 0:m], r_eq[:, :, 0:m, 0:m], ALU.add))
                    dve.wait_ge(s_rt_b, n)
                    n = done(dve.tensor_reduce(out_ap, r_gt[:, :, 0:m, 0:m], AX.X, ALU.add))
                    dve.wait_ge(s_rt_b, n)

                rank(r_gm, NG, r_grank)
                n = done(dve.tensor_scalar(r_gm, r_grank, 2.0, None, ALU.is_lt))
                dve.wait_ge(s_rt_b, n)
                for i in range(2):
                    last = dve.tensor_tensor(pairs[:, :, :, i], pairs[:, :, :, i], r_gm, ALU.mult)
                n = done(last)
                dve.wait_ge(s_rt_b, n)
                rank(r_sc, NE, r_rank)
                dve.tensor_scalar(r_both, r_rank, 2.0, None, ALU.is_lt).then_inc(s_both_ready, 1)
                dve.tensor_scalar(r_sel[:, 0], r_rank, 0.0, None, ALU.is_equal)
                dve.tensor_scalar(r_sel[:, 1], r_rank, 1.0, None, ALU.is_equal).then_inc(s_sel_ready, 1)

            def dve_route_slots(dve):
                k = [0]

                def done(ins):
                    ins.then_inc(s_rt_c, 1)
                    k[0] += 1
                    return k[0]

                dve.wait_ge(s_sel_ready, 1)
                for i in range(2):
                    dve.tensor_tensor(r_tmp[:, i], r_sc, r_sel[:, i], ALU.mult)
                dve.tensor_copy(h2all[:, :, D + 3], token_id[:])
                n = done(dve.tensor_tensor(r_pos, r_sel[:, 0], eidx[:].unsqueeze(1).to_broadcast([P, NR, NE]), ALU.mult))
                dve.wait_ge(s_rt_c, n)
                dve.tensor_reduce(h2all[:, :, D + 2], r_pos, AX.X, ALU.add)
                n = done(dve.tensor_reduce(r_w, r_tmp, AX.X, ALU.add))
                dve.wait_ge(s_rt_c, n)
                dve.tensor_copy(h2all[:, :, D], r_w[:, 0, :])
                n = done(dve.tensor_tensor(h2all[:, :, D + 1], r_w[:, 1, :], r_w[:, 0, :], ALU.subtract))
                dve.wait_ge(s_rank_done, 1)
                dve.wait_ge(s_rt_c, n)
                rk = RNK.rearrange("p (t e) -> p t e", e=NE)
                dve.tensor_copy(r_cnt, TOT).then_inc(s_tab, 1)
                n = done(dve.tensor_tensor(r_pos, rk, erow[:].unsqueeze(1).to_broadcast([P, NR, NE]), ALU.add))
                dve.wait_ge(s_rt_c, n)
                for i in range(2):
                    last = dve.tensor_tensor(r_tmp[:, i], r_pos, r_sel[:, i], ALU.mult)
                n = done(last)
                dve.wait_ge(s_rt_c, n)
                n = done(dve.tensor_reduce(r_slot, r_tmp, AX.X, ALU.add))
                dve.wait_ge(s_rt_c, n)
                dve.tensor_copy(slot_u[:], r_slot).then_inc(s_slots_ready, 1)

            def dve_tables(dve):
                k = [1]

                def done(ins):
                    ins.then_inc(s_tab, 1)
                    k[0] += 1
                    return k[0]

                dve.wait_ge(s_tab, 1)
                dve.tensor_tensor(r_end, r_cnt.unsqueeze(2).to_broadcast([P, NE, T // P]),
                                  step128[:].unsqueeze(1).to_broadcast([P, NE, T // P]), ALU.is_gt)
                n = done(dve.tensor_tensor(r_last, r_cnt, erow[:], ALU.add))
                dve.wait_ge(s_tab, n)
                dve.tensor_copy(pad_u[:], r_last[0:1, :]).then_inc(s_pad_ready, 1)
                n = done(dve.tensor_reduce(r_tiles, r_end, AX.X, ALU.add))
                dve.wait_ge(s_tab, n)
                n = done(dve.tensor_copy(r_ends, r_tiles))
                dve.wait_ge(s_tab, n)
                for e in range(1, NE):
                    n = done(dve.tensor_tensor(r_ends[:, e:e + 1], r_ends[:, e - 1:e], r_tiles[:, e:e + 1], ALU.add))
                    dve.wait_ge(s_tab, n)
                n = done(dve.tensor_tensor(r_done, r_ends.unsqueeze(1).to_broadcast([P, NT, NE]),
                                           tidx[:].unsqueeze(2).to_broadcast([P, NT, NE]), ALU.is_le))
                dve.wait_ge(s_tab, n)
                n = done(dve.tensor_reduce(r_tab[:, 0, :], r_done, AX.X, ALU.add))
                dve.wait_ge(s_tab, n)
                n = done(dve.tensor_tensor(r_done, r_done, r_tiles.unsqueeze(1).to_broadcast([P, NT, NE]), ALU.mult))
                dve.wait_ge(s_tab, n)
                dve.tensor_scalar(eid_f[:], r_tab[:, 0, :], float(NE - 1), None, ALU.min)
                n = done(dve.tensor_reduce(r_tab[:, 1, :], r_done, AX.X, ALU.add))
                dve.wait_ge(s_tab, n)
                dve.tensor_tensor(r_tab[:, 1, :], tidx[:], r_tab[:, 1, :], ALU.subtract)
                dve.tensor_scalar(r_tab[:, 2, :], eid_f[:], float(REGION), None, ALU.mult)
                n = done(dve.tensor_scalar(r_tab[:, 3, :], r_tab[:, 0, :], float(NE), None, ALU.is_ge))
                dve.wait_ge(s_tab, n)
                n = done(dve.scalar_tensor_tensor(r_tab[:, 2, :], r_tab[:, 1, :], float(P), r_tab[:, 2, :], ALU.mult, ALU.add))
                dve.wait_ge(s_tab, n)
                n = done(dve.tensor_scalar(r_tab[:, 0, :], r_tab[:, 2, :], r_last[:, NE - 1:NE], -1.0, ALU.subtract, ALU.mult))
                dve.wait_ge(s_tab, n)
                n = done(dve.tensor_tensor(r_tab[:, 0, :], r_tab[:, 0, :], r_tab[:, 3, :], ALU.mult))
                dve.wait_ge(s_tab, n)
                n = done(dve.tensor_tensor(r_tab[:, 2, :], r_tab[:, 2, :], r_tab[:, 0, :], ALU.add))
                dve.wait_ge(s_tab, n)
                dve.tensor_copy(tile_u[:, 0, :], eid_f[0:1, :])
                dve.tensor_copy(tile_u[:, 1, :], r_tab[0:1, 2, :]).then_inc(s_table_ready, 1)

            def pool_scatter(pool):
                pool.wait_ge(s_slots_ready, 1)
                for j in range(NR):
                    for i in range(2):
                        pool.indirect_dma_start(
                            out=routed_in, out_offset=bass.IndirectOffsetOnAxis(slot_u[:, i, j:j + 1], 0),
                            in_=h2all[:, j, :], in_offset=None).then_inc(s_scattered, 16)

            def sp_weights(sp, e, r, first):
                if not first:
                    sp.wait_ge(s_est_free, e - 1)
                sp.dma_start(gu_stage(r), gu_t[:, ds(e, 1), :].rearrange("(k p) o n -> p k (o n)", p=P)).then_inc((s_est0_in, s_est1_in)[r], 16)
                sp.dma_start(dn_stage(r), down_t[ds(e, 1)].rearrange("o (j p) n -> p (o j) n", p=FH)).then_inc((s_est0_in, s_est1_in)[r], 16)

            def act_weights(act, e, r):
                act.wait_ge((s_est0_in, s_est1_in)[r], 16 * (e - r) + 32)
                act.activation(wgu[0][:, :, ds(e * (2 * F), 2 * F)], gu_stage(r), ACT.Copy)
                act.activation(wdn[0][:, :, ds(e * D, D)], dn_stage(r), ACT.Copy).then_inc(s_ew_hi, 1)

            def dve_weights(dve, e, r):
                dve.wait_ge(s_ew_hi, e + 1)
                dve.tensor_tensor(wgu[1][:, :, ds(e * (2 * F), 2 * F)], gu_stage(r),
                                  wgu[0][:, :, ds(e * (2 * F), 2 * F)].bitcast(F32), ALU.subtract)
                dve.tensor_tensor(wdn[1][:, :, ds(e * D, D)], dn_stage(r),
                                  wdn[0][:, :, ds(e * D, D)].bitcast(F32), ALU.subtract).then_inc(s_est_free, 1)

            def sp_shared(sp, b, u, first):
                if not first:
                    sp.wait_ge(s_res_ready, b - 1)
                sp.dma_start(x1b[u][:], x1_dram[ds(b, 1)].rearrange("o (t p) d -> p (o t) d", p=P)).then_inc((s_x1b0_in, s_x1b1_in)[u], 16)
                sp.dma_start(gbb[u][:], modrow[ds(b, 1), 4 * D:5 * D].to_broadcast([P, D]).unsqueeze(1)).then_inc((s_gbb0_in, s_gbb1_in)[u], 16)

            def pe_shared_up(pe, b, u, first):
                if not first:
                    pe.wait_ge(s_act_mul, len(FT) * (b - 1))
                for j, (f, m) in enumerate(FT):
                    for g in range(2):
                        for k in range(KD):
                            last = mm3(pe, GUb[u][j][0:m, g * S:(g + 1) * S],
                                       parts(wsgu, slice(None), k, slice(g * FS + f, g * FS + f + m)),
                                       parts(h2T, slice(None), k, ds(b * S, S)), k == 0, k == KD - 1)
                    last.then_inc(s_shgu_done, 1)

            def SJ(u, j):
                return (u * len(FT) + j) % 2

            def act_shared(act, b, u):
                def hi(j):
                    f, m = FT[j]
                    act.wait_ge(s_act_mul, b * len(FT) + j + 1)
                    act.activation(aT[u][0][0:m, j, :], aact[SJ(u, j)][0:m, :], ACT.Copy).then_inc(s_a_hi, 1)

                for j, (f, m) in enumerate(FT):
                    n = b * len(FT) + j
                    act.wait_ge(s_shgu_done, n + 1)
                    if not (type(n) is int and n < 2):
                        act.wait_ge(s_act_mul, n - 1)
                    act.activation(sact[SJ(u, j)][0:m, :], GUb[u][j][0:m, 0:S], ACT.Silu).then_inc(s_silu_done, 1)
                    if j:
                        hi(j - 1)
                hi(len(FT) - 1)

            def dve_shared(dve, b, u):
                def lo(j):
                    f, m = FT[j]
                    dve.wait_ge(s_a_hi, b * len(FT) + j + 1)
                    dve.tensor_tensor(aT[u][1][0:m, j, :], aact[SJ(u, j)][0:m, :], aT[u][0][0:m, j, :].bitcast(F32),
                                      ALU.subtract).then_inc(s_a_lo, 1)

                for j, (f, m) in enumerate(FT):
                    n = b * len(FT) + j
                    q = SJ(u, j)
                    dve.wait_ge(s_silu_done, n + 1)
                    if not (type(n) is int and n < 2):
                        dve.wait_ge(s_a_lo, n - 1)
                    dve.tensor_tensor(aact[q][0:m, :], sact[q][0:m, :], GUb[u][j][0:m, S:2 * S], ALU.mult).then_inc(s_act_mul, 1)
                    if j:
                        lo(j - 1)
                lo(len(FT) - 1)

            def pe_shared_down(pe, b, u, first):
                if not first:
                    pe.wait_ge(s_og_ready, b - 1)
                pe.wait_ge(s_a_lo, len(FT) * (b + 1))
                for t in range(TT):
                    for j, (f, m) in enumerate(FT):
                        last = mm3(pe, DN[u][:, t * D:(t + 1) * D],
                                   parts(aT[u], slice(0, m), j, slice(t * P, (t + 1) * P)),
                                   parts(wsd, slice(0, m), j), j == 0, j == len(FT) - 1)
                last.then_inc(s_shdn_done, 1)

            def dve_shared_out(dve, b, u):
                dve.wait_ge(s_shdn_done, b + 1)
                dve.wait_ge((s_gbb0_in, s_gbb1_in)[u], 8 * (b - u + 2))
                dve.wait_ge((s_x1b0_in, s_x1b1_in)[u], 8 * (b - u + 2))
                dve.tensor_tensor(og[u][:], bank2(DN[u]), gbb[u][:].to_broadcast([P, TT, D]), ALU.mult).then_inc(s_og_ready, 1)
                dve.wait_ge(s_og_ready, b + 1)
                dve.tensor_tensor(res[:, ds(b, 1)].rearrange("p o t d -> p (o t) d"), og[u][:], x1b[u][:], ALU.add).then_inc(s_res_ready, 1)

            def sp_tile(sp, t, r, first):
                sp.wait_ge(s_table_ready, 1)
                if not first:
                    sp.wait_ge(s_ea_ready, t - 3)
                row = sp.value_load(tile_u[0:1, 1, ds(t, 1)], min_val=0, max_val=NE * REGION - P)
                sp.dma_start(xt_in[r][:], routed_in[ds(row, P), :]).then_inc(tile_sems[r], 16)

            tile_sems = [s_tile0_in, s_tile1_in, s_tile2_in, s_tile3_in]
            out_sems = [s_tile0_out, s_tile1_out, s_tile2_out, s_tile3_out]

            def tile_wait(t, r):
                return 4 * (t - r) + 16

            def pe_tile_in(pe, t, r):
                pe.wait_ge(tile_sems[r], tile_wait(t, r))
                for d in range(KD):
                    last = pe.transpose(XTb[r % 2][:, d * P:(d + 1) * P], xt_in[r][:, d * P:(d + 1) * P], ident[:])
                last.then_inc(s_ext_done, 1)

            def pe_tile_up(pe, t, r):
                pe.wait_ge(s_table_ready, 1)
                e = pe.value_load(tile_u[0:1, 0, ds(t, 1)], min_val=0, max_val=NE - 1)
                pe.wait_ge(s_ex_lo, t + 1)
                for k in range(KD):
                    last = mm3(pe, EGU[r % 2][:, 0:2 * F], parts(eT[r % 2], slice(None), k),
                               parts(wgu, slice(None), k, ds(e * (2 * F), 2 * F)), k == 0, k == KD - 1)
                last.then_inc(s_egu_done, 1)

            def pe_tile_act(pe, t, r):
                pe.wait_ge(s_ea_ready, t + 1)
                for j in range(2):
                    last = pe.transpose(ATb[r % 2][0:FH, j * P:(j + 1) * P], av[r % 2][:, j * FH:(j + 1) * FH], ident[:])
                last.then_inc(s_eat_done, 1)

            def pe_tile_down(pe, t, r):
                pe.wait_ge(s_table_ready, 1)
                e = pe.value_load(tile_u[0:1, 0, ds(t, 1)], min_val=0, max_val=NE - 1)
                pe.wait_ge(s_ea_lo, t + 1)
                for j in range(2):
                    last = mm3(pe, EDN[r % 2][:, 0:D], parts(avT[r % 2], slice(None), j),
                               parts(wdn, slice(None), j, ds(e * D, D)), j == 0, j == 1)
                last.then_inc(s_edn_done, 1)

            def act_tile_in(act, t, r):
                act.wait_ge(s_ext_done, t + 1)
                act.activation(eT[r % 2][0], bank2(XTb[r % 2], P), ACT.Copy).then_inc(s_ex_hi, 1)

            def act_tile_silu(act, t, r):
                act.wait_ge(s_egu_done, t + 1)
                act.activation(sg[r % 2], EGU[r % 2][:, 0:F], ACT.Silu).then_inc(s_esilu, 1)

            def act_tile_act(act, t, r):
                act.wait_ge(s_eat_done, t + 1)
                act.activation(avT[r % 2][0], bank2(ATb[r % 2], P)[0:FH], ACT.Copy).then_inc(s_ea_hi, 1)

            def act_tile_out(act, t, r, first):
                act.wait_ge(s_edn_done, t + 1)
                if not first:
                    act.wait_ge(out_sems[r], 4 * (t - r))
                act.activation(yo[r], EDN[r % 2][:, 0:D], ACT.Copy).then_inc(s_ey_ready, 1)

            def dve_tile_in(dve, t, r):
                dve.wait_ge(s_ex_hi, t + 1)
                dve.tensor_tensor(eT[r % 2][1], bank2(XTb[r % 2], P), eT[r % 2][0].bitcast(F32), ALU.subtract).then_inc(s_ex_lo, 1)

            def dve_tile_meta(dve, t, r):
                q = r % 2
                dve.wait_ge(tile_sems[r], tile_wait(t, r))
                if not (type(t) is int and t < 4):
                    dve.wait_ge(out_sems[r], 4 * (t - r))
                dve.tensor_tensor(second[q][:], xt_in[r][:, D + 2:D + 3], eid_f[:, ds(t, 1)], ALU.not_equal).then_inc(s_esecond, 1)
                dve.wait_ge(s_esecond, t + 1)
                dve.scalar_tensor_tensor(wt[q][:], xt_in[r][:, D + 1:D + 2], second[q][:, 0:1], xt_in[r][:, D:D + 1],
                                         ALU.mult, ALU.add)
                dve.scalar_tensor_tensor(dest[r][:], second[q][:], float(T), xt_in[r][:, D + 3:D + 4],
                                         ALU.mult, ALU.add).then_inc(s_emeta, 1)

            def dve_tile_act(dve, t, r):
                q = r % 2
                dve.wait_ge(s_emeta, t + 1)
                dve.wait_ge(s_esilu, t + 1)
                dve.scalar_tensor_tensor(av[q], sg[q], wt[q][:, 0:1], EGU[q][:, F:2 * F],
                                         ALU.mult, ALU.mult).then_inc(s_ea_ready, 1)

            def dve_tile_lo(dve, t, r):
                q = r % 2
                dve.wait_ge(s_ea_hi, t + 1)
                dve.tensor_tensor(avT[q][1], bank2(ATb[q], P)[0:FH], avT[q][0].bitcast(F32), ALU.subtract).then_inc(s_ea_lo, 1)

            def pool_tile(pool, t, r):
                pool.wait_ge(s_emeta, t + 1)
                pool.wait_ge(s_ey_ready, t + 1)
                pool.indirect_dma_start(out=routed_out, out_offset=bass.IndirectOffsetOnAxis(dest[r][:, 0:1], 0),
                                        in_=yo[r], in_offset=None,
                                        bounds_check=2 * T - 1, oob_is_err=False).then_inc(out_sems[r], 16)

            def steps(eng, one):
                for t in range(5):
                    one(t, t % 4, t >= 1, True, True)
                with eng.Fori(1, (NT - 3) // 4) as i:
                    for v in range(4):
                        one(4 * i + 1 + v, (1 + v) % 4, True, True, True)
                one(NT - 2, (NT - 2) % 4, True, True, False)
                one(NT - 1, (NT - 1) % 4, True, False, False)

            LASTT = NT - 1

            with nc.Block() as block:
                @block.sync
                def _(sp):
                    for b in range(2):
                        sp_weights(sp, b, b, True)
                        sp_shared(sp, b, b, True)
                    with sp.Fori(1, NPAIR) as p:
                        for u in range(2):
                            sp_weights(sp, 2 * p + u, u, False)
                            sp_shared(sp, 2 * p + u, u, False)
                    sp.wait_ge(s_pad_written, 2)
                    sp.wait_ge(s_pad_ready, 1)
                    for e in range(NE):
                        row = sp.value_load(pad_u[0:1, e:e + 1], min_val=0, max_val=NE * REGION - P)
                        sp.dma_start(routed_in[ds(row, P), :], pad).then_inc(s_pad_out, 16)
                    sp.wait_ge(s_pad_out, 16 * NE)
                    for t in range(4):
                        sp_tile(sp, t, t, True)
                    with sp.Fori(1, (NT - 3) // 4) as i:
                        for v in range(4):
                            sp_tile(sp, 4 * i + v, v, False)
                    for t in range(NT - 3, NT):
                        sp_tile(sp, t, t % 4, False)
                    for r in range(4):
                        sp.wait_ge(out_sems[r], 16 * ((NT + 3 - r) // 4))

                    def fin_in(b, u):
                        for i in range(2):
                            sp.dma_start((x1b, og)[i][u][:], routed_out[ds(b * S + i * T, S), :].rearrange("(t p) d -> p t d", p=P)).then_inc((s_y0_in, s_y1_in)[u], 16)
                        sp.dma_start(gbb[u][:], modrow[ds(b, 1), 4 * D:5 * D].to_broadcast([P, D]).unsqueeze(1)).then_inc((s_y0_in, s_y1_in)[u], 16)

                    def fin_out(b, u):
                        sp.wait_ge(s_fin_ready, b + 1)
                        sp.dma_start(out[ds(b, 1)].rearrange("o (t p) d -> p (o t) d", p=P), res[:, ds(b, 1)].rearrange("p o t d -> p (o t) d")).then_inc(s_stored, 16)

                    for b in range(2):
                        fin_in(b, b)
                    with sp.Fori(0, NPAIR - 1) as p:
                        for u in range(2):
                            fin_out(2 * p + u, u)
                            fin_in(2 * p + 2 + u, u)
                    for u in range(2):
                        fin_out(B - 2 + u, u)
                    sp.wait_ge(s_stored, 16 * B)

                @block.gpsimd
                def _(pool):
                    pool_scatter(pool)
                    pool.wait_ge(s_scattered, 32 * NR)
                    pool.memset(pad, 0.0).then_inc(s_pad_written, 1)
                    pool.wait_ge(s_pad_written, 1)
                    pool.memset(pad[:, D + META - 1:D + META], float(SKIP)).then_inc(s_pad_written, 1)
                    for t in range(NT):
                        pool_tile(pool, t, t % 4)

                @block.scalar
                def _(act):
                    act_route(act)
                    for u in range(2):
                        act_weights(act, u, u)
                        act_shared(act, u, u)
                    with act.Fori(1, NPAIR) as p:
                        for u in range(2):
                            act_weights(act, 2 * p + u, u)
                            act_shared(act, 2 * p + u, u)

                    def one(t, r, back, up, ahead):
                        if up:
                            act_tile_silu(act, t + 1, (r + 1) % 4)
                        if ahead:
                            act_tile_in(act, t + 2, (r + 2) % 4)
                        act_tile_act(act, t, r)
                        if back:
                            act_tile_out(act, t - 1, (r - 1) % 4, type(t) is int and t < 5)

                    act_tile_in(act, 0, 0)
                    act_tile_in(act, 1, 1)
                    act_tile_silu(act, 0, 0)
                    steps(act, one)
                    act_tile_out(act, LASTT, LASTT % 4, False)

                @block.vector
                def _(dve):
                    dve_route_scores(dve)
                    dve_route_select(dve)
                    dve_weights(dve, 0, 0)
                    dve_route_slots(dve)
                    dve_shared(dve, 0, 0)
                    dve_tables(dve)
                    with dve.Fori(0, NPAIR - 1) as p:
                        for u in range(2):
                            dve_weights(dve, 2 * p + 1 + u, 1 - u)
                            dve_shared(dve, 2 * p + 1 + u, 1 - u)
                            dve_shared_out(dve, 2 * p + u, u)
                    dve_weights(dve, B - 1, 1)
                    dve_shared(dve, B - 1, 1)
                    dve_shared_out(dve, B - 2, 0)
                    dve_shared_out(dve, B - 1, 1)

                    def one(t, r, back, up, ahead):
                        if up:
                            dve_tile_meta(dve, t + 1, (r + 1) % 4)
                            dve_tile_act(dve, t + 1, (r + 1) % 4)
                        if ahead:
                            dve_tile_in(dve, t + 2, (r + 2) % 4)
                        dve_tile_lo(dve, t, r)

                    dve_tile_in(dve, 0, 0)
                    dve_tile_in(dve, 1, 1)
                    dve_tile_meta(dve, 0, 0)
                    dve_tile_act(dve, 0, 0)
                    steps(dve, one)

                    def fin(b, u):
                        dve.wait_ge((s_y0_in, s_y1_in)[u], 24 * (b - u + 2))
                        dve.tensor_tensor(x1b[u][:], x1b[u][:], og[u][:], ALU.add).then_inc(s_fin_sum, 1)
                        dve.wait_ge(s_fin_sum, b + 1)
                        dve.tensor_tensor(x1b[u][:], x1b[u][:], gbb[u][:].to_broadcast([P, TT, D]), ALU.mult).then_inc(s_fin_mul, 1)
                        dve.wait_ge(s_fin_mul, b + 1)
                        r_ = res[:, ds(b, 1)].rearrange("p o t d -> p (o t) d")
                        dve.tensor_tensor(r_, r_, x1b[u][:], ALU.add).then_inc(s_fin_ready, 1)
                    with dve.Fori(0, NPAIR) as p:
                        for u in range(2):
                            fin(2 * p + u, u)

                @block.tensor
                def _(pe):
                    pe_logits_t(pe)
                    pe_shared_up(pe, 0, 0, True)
                    pe_rank(pe)
                    pe_shared_up(pe, 1, 1, True)
                    pe_shared_down(pe, 0, 0, True)
                    pe_shared_up(pe, 2, 0, False)
                    pe_shared_down(pe, 1, 1, True)
                    with pe.Fori(1, NPAIR - 1) as p:
                        for u in range(2):
                            pe_shared_up(pe, 2 * p + 1 + u, 1 - u, False)
                            pe_shared_down(pe, 2 * p + u, u, False)
                    pe_shared_up(pe, B - 1, 1, False)
                    pe_shared_down(pe, B - 2, 0, False)
                    pe_shared_down(pe, B - 1, 1, False)

                    def one(t, r, back, up, ahead):
                        if up:
                            pe_tile_up(pe, t + 1, (r + 1) % 4)
                        if ahead:
                            pe_tile_in(pe, t + 2, (r + 2) % 4)
                        pe_tile_act(pe, t, r)
                        if back:
                            pe_tile_down(pe, t - 1, (r - 1) % 4)

                    pe.wait_ge(s_est_free, NE)
                    pe.wait_ge(s_og_ready, B)
                    pe_tile_in(pe, 0, 0)
                    pe_tile_in(pe, 1, 1)
                    pe_tile_up(pe, 0, 0)
                    steps(pe, one)
                    pe_tile_down(pe, LASTT, LASTT % 4)


def kernel(L0_attn_hidden_states, L0_attn_c_attn_w, L0_attn_c_attn_b, L0_attn_c_proj_w, L0_attn_c_proj_b,
           L0_attn_cam_gate, L0_attn_cam_w0, L0_attn_cam_w1, L0_ffn_gate_weight, L0_ffn_gate_w, L0_ffn_up_w,
           L0_ffn_down_w, L0_ffn_sh_gate_w, L0_ffn_sh_up_w, L0_ffn_sh_down_w, L0_c, L0_wmod):
    import concourse.bacc as bacc
    from concourse.bass_utils import run_bass_kernel_spmd

    def lay(a):
        return np.ascontiguousarray(a)

    gate_w, up_w = np.asarray(L0_ffn_gate_w), np.asarray(L0_ffn_up_w)
    arrays = {
        "x": lay(L0_attn_hidden_states),
        "w_qkv": lay(L0_attn_c_attn_w),
        "b_cols": lay(np.asarray(L0_attn_c_attn_b).reshape(-1, P).T),
        "w_proj": lay(L0_attn_c_proj_w),
        "b_proj": lay(L0_attn_c_proj_b),
        "gate_col": lay(np.asarray(L0_attn_cam_gate).reshape(P, 1)),
        "cam_w0": lay(L0_attn_cam_w0),
        "cam_w1": lay(L0_attn_cam_w1),
        "router_t": lay(np.asarray(L0_ffn_gate_weight).T),
        "gu_t": lay(np.concatenate([gate_w, up_w], axis=1).transpose(2, 0, 1)),
        "down_t": lay(np.asarray(L0_ffn_down_w).transpose(0, 2, 1)),
        "sh_gu_t": lay(np.concatenate([np.asarray(L0_ffn_sh_gate_w), np.asarray(L0_ffn_sh_up_w)], axis=0).T),
        "sh_down_t": lay(np.asarray(L0_ffn_sh_down_w).T),
        "c_t": lay(np.asarray(L0_c).T),
        "w_mod": lay(L0_wmod),
    }
    nc = bacc.Bacc("TRN2", target_bir_lowering=False, num_devices=1)
    args = [nc.dram_tensor(n, a.shape, mybir.dt.from_np(a.dtype), kind="ExternalInput").ap() for n, a in arrays.items()]
    out = nc.dram_tensor("out", arrays["x"].shape, F32, kind="ExternalOutput").ap()
    adaln_block(nc, *args, out)
    r = run_bass_kernel_spmd(nc, [arrays], core_ids=[0])
    return r.results[0]["out"]
```

```python
from contextlib import ExitStack

import numpy as np

import concourse.bass as bass
from concourse import mybir

ALU = mybir.AluOpType
ACT = mybir.ActivationFunctionType
F32 = mybir.dt.float32
F32R = mybir.dt.float32r
BF16 = mybir.dt.bfloat16
U32 = mybir.dt.uint32
I32 = mybir.dt.int32
AX = mybir.AxisListType
ds = bass.ds

P = 128
EPS = 1e-5
GUARD = 0.25
HEAD_DIM = 16
SCALE = float(HEAD_DIM) ** -0.5
LAYER_DEPTH = 0.5
META = 4
SKIP = 1 << 20


def adaln_block(nc, x_in, w_qkv, b_cols, w_proj, b_proj, gate_col, cam_w0, cam_w1,
                router_t, gu_t, down_t, sh_gu_t, sh_down_t, c_t, w_mod, out):
    B, S, D = x_in.shape
    NE = router_t.shape[1]
    F = down_t.shape[1]
    FS = sh_down_t.shape[0]
    KD = D // P
    TT = S // P
    T = B * S
    NPAIR = B // 2
    NT = (2 * T + NE * (P - 1)) // P
    REGION = T + P
    ROW = D + META
    FH = F // 2
    FT = [(f, min(P, FS - f)) for f in range(0, FS, P)]
    UNR = 3
    assert D == KD * P == 256 and S == TT * P == 256 and NT % UNR == 0 and F <= 256

    with ExitStack() as ctx:
        def sb(name, shape, dt=F32):
            return ctx.enter_context(nc.sbuf_tensor(name, shape, dt))

        def hilo(name, shape):
            return sb(name + "_hi", shape, F32R), sb(name + "_lo", shape, F32R)

        def sem(name):
            return ctx.enter_context(nc.semaphore(name))

        s_wmod0_in = sem("wmod0_in")
        s_wmod_in = sem("wmod_in")
        s_wqkv_in = sem("wqkv_in")
        s_wproj_in = sem("wproj_in")
        s_wrt_in = sem("wrt_in")
        s_wsgu_in = sem("wsgu_in")
        s_wsd_in = sem("wsd_in")
        s_mrow_ready = sem("mrow_ready")
        s_guard_pool = sem("guard_pool")
        s_modrow_out = sem("modrow_out")
        s_const = sem("const")
        s_ident_ready = sem("ident_ready")
        s_c_in = sem("c_in")
        s_cols_in = sem("cols_in")
        s_c_exp = sem("c_exp")
        s_whi = sem("whi")
        s_kscaled = sem("kscaled")
        s_lw_sum = sem("lw_sum")
        s_lw_exp = sem("lw_exp")
        s_c_chain = sem("c_chain")
        s_silu_c = sem("silu_c")
        s_modT = sem("modT")
        s_sacol_ready = sem("sacol_ready")
        s_wlo = sem("wlo")
        s_cols_ready = sem("cols_ready")
        s_mod_mm = sem("mod_mm")
        s_mod_copied = sem("mod_copied")
        s_bvp_done = sem("bvp_done")
        s_bp_ready = sem("bp_ready")
        s_guard = sem("guard")
        s_xn_ready = sem("xn_ready")
        s_xt_done = sem("xt_done")
        s_h_lo = sem("h_lo")
        s_qk_hi = sem("qk_hi")
        s_qk_lo = sem("qk_lo")
        s_qk_done = sem("qk_done")
        s_v_done = sem("v_done")
        s_qp_hi = sem("qp_hi")
        s_qp_lo = sem("qp_lo")
        s_s2_done = sem("s2_done")
        s_s1_done = sem("s1_done")
        s_exp2 = sem("exp2")
        s_norm1 = sem("norm1")
        s_pt2_done = sem("pt2_done")
        s_pt1_done = sem("pt1_done")
        s_pt2_hi = sem("pt2_hi")
        s_pt2_lo = sem("pt2_lo")
        s_pt1_hi = sem("pt1_hi")
        s_pt1_lo = sem("pt1_lo")
        s_v_hi = sem("v_hi")
        s_v_lo = sem("v_lo")
        s_c2_done = sem("c2_done")
        s_c1_done = sem("c1_done")
        s_ctx_hi = sem("ctx_hi")
        s_ctx_lo = sem("ctx_lo")
        s_o_done = sem("o_done")
        s_h2_ready = sem("h2_ready")
        s_h2t_done = sem("h2t_done")
        s_h2_hi = sem("h2_hi")
        s_h2_lo = sem("h2_lo")
        s_lg_done = sem("lg_done")
        s_max2 = sem("max2")
        s_max1 = sem("max1")
        s_exp1 = sem("exp1")
        s_rl1 = sem("rl1")
        s_ht_ready = sem("ht_ready")
        s_tanh_done = sem("tanh_done")
        s_rl2 = sem("rl2")
        s_h_hi = sem("h_hi")
        s_qf_ready = sem("qf_ready")
        s_qp_ready = sem("qp_ready")
        s_mx0_in = sem("mx0_in")
        s_mx1_in = sem("mx1_in")
        s_y_ready = sem("y_ready")
        s_stats1 = sem("stats1")
        s_var1 = sem("var1")
        s_xa0_in = sem("xa0_in")
        s_xa1_in = sem("xa1_in")
        s_stats2 = sem("stats2")
        s_var2 = sem("var2")
        s_x1_ready = sem("x1_ready")
        s_xr0_in = sem("xr0_in")
        s_xr1_in = sem("xr1_in")
        s_xg_ready = sem("xg_ready")
        s_mh0_in = sem("mh0_in")
        s_mh1_in = sem("mh1_in")
        s_xn2_ready = sem("xn2_ready")
        s_h2c0 = sem("h2c0")
        s_h2c1 = sem("h2c1")
        s_h2_chain = sem("h2_chain")
        s_lg_copied = sem("lg_copied")
        s_rstd1 = sem("rstd1")
        s_rstd2 = sem("rstd2")
        s_x1_out0 = sem("x1_out0")
        s_x1_out1 = sem("x1_out1")
        s_lt_done = sem("lt_done")
        s_both_ready = sem("both_ready")
        s_rank_done = sem("rank_done")
        s_rt_a = sem("rt_a")
        s_rt_exp = sem("rt_exp")
        s_rt_b = sem("rt_b")
        s_rt_c = sem("rt_c")
        s_tab = sem("tab")
        s_slots_ready = sem("slots_ready")
        s_pad_ready = sem("pad_ready")
        s_table_ready = sem("table_ready")
        s_scattered = sem("scattered")
        s_split_pool = sem("split_pool")
        s_split_dve = sem("split_dve")
        s_est0_in = sem("est0_in")
        s_est1_in = sem("est1_in")
        s_ew_hi = sem("ew_hi")
        s_res_ready = sem("res_ready")
        s_x1b0_in = sem("x1b0_in")
        s_x1b1_in = sem("x1b1_in")
        s_act_mul = sem("act_mul")
        s_shgu_done = sem("shgu_done")
        s_a_hi = sem("a_hi")
        s_silu_done = sem("silu_done")
        s_a_lo = sem("a_lo")
        s_og_ready = sem("og_ready")
        s_shdn_done = sem("shdn_done")
        s_gb_in = sem("gb_in")
        s_pad_out = sem("pad_out")
        s_ea_ready = sem("ea_ready")
        s_tile0_in = sem("tile0_in")
        s_tile1_in = sem("tile1_in")
        s_tile2_in = sem("tile2_in")
        s_tile3_in = sem("tile3_in")
        s_tile0_out = sem("tile0_out")
        s_tile1_out = sem("tile1_out")
        s_tile2_out = sem("tile2_out")
        s_tile3_out = sem("tile3_out")
        s_ext_done = sem("ext_done")
        s_ex_lo = sem("ex_lo")
        s_egu_done = sem("egu_done")
        s_eat_done = sem("eat_done")
        s_ea_lo = sem("ea_lo")
        s_edn_done = sem("edn_done")
        s_ex_hi = sem("ex_hi")
        s_esilu = sem("esilu")
        s_ea_hi = sem("ea_hi")
        s_ey_ready = sem("ey_ready")
        s_esecond = sem("esecond")
        s_emeta = sem("emeta")
        s_y0_in = sem("y0_in")
        s_y1_in = sem("y1_in")
        s_y2_in = sem("y2_in")
        s_y3_in = sem("y3_in")
        s_y4_in = sem("y4_in")
        s_y5_in = sem("y5_in")
        s_y6_in = sem("y6_in")
        s_y7_in = sem("y7_in")
        s_pad_written = sem("pad_written")
        s_fin_pool = sem("fin_pool")
        s_fin_dve = sem("fin_dve")
        s_stored = sem("stored")

        modrow = nc.dram_tensor("modrow", (B, 5 * D), F32, kind="Internal").ap()
        x1_dram = nc.dram_tensor("x1_dram", (B, S, D), F32, kind="Internal").ap()
        routed_in = nc.dram_tensor("routed_in", (NE * REGION, ROW), F32, kind="Internal").ap()
        routed_out = nc.dram_tensor("routed_out", (2 * T, D), F32, kind="Internal").ap()

        ident = sb("ident", [P, P])
        before = sb("before", [P, P], BF16)
        ones = sb("ones", [P, P], BF16)
        lower = sb("lower", [P, NE, NE])
        token_id = sb("token_id", [P, B * TT])
        eidx = sb("eidx", [P, NE])
        erow = sb("erow", [P, NE])
        step128 = sb("step128", [P, T // P])
        tidx = sb("tidx", [P, NT])
        cols = sb("cols", [P, 3 * KD + 2])
        lw = sb("lw", [P, 4])

        wrt = hilo("wrt", [P, KD, NE])
        wsgu = hilo("wsgu", [P, KD, 2 * FS])
        wsd = hilo("wsd", [P, len(FT), D])
        h2T = hilo("h2T", [P, KD, T])

        sacol = sb("sacol", [P, 2 * KD, B])

        h2all = sb("h2all", [P, B * TT, ROW])
        lgall = sb("lgall", [P, T])
        eps_t = sb("eps_t", [P, 2 * TT])
        minus_half = sb("minus_half", [P, 2 * TT])

        eid_f = sb("eid_f", [P, NT])
        tile_u = sb("tile_u", [1, 2, NT], I32)
        pad_u = sb("pad_u", [1, NE], I32)

        attention_weights = ctx.enter_context(ExitStack())

        def hilo_attention(name, shape):
            return tuple(attention_weights.enter_context(nc.sbuf_tensor(name + x, shape, F32R)) for x in ("_hi", "_lo"))

        wqkv = hilo_attention("wqkv", [P, KD, 3 * D])
        wproj = hilo_attention("wproj", [P, KD, D])

        psum = [ctx.enter_context(nc.psum_tensor(f"bank{i}", [P, 512], F32)) for i in range(8)]

        def parts(t, *idx):
            return t[0][idx], t[1][idx]

        def mm3(pe, out_ap, l, r, start, stop):
            pe.matmul(out_ap, l[1], r[0], start=start, stop=False)
            pe.matmul(out_ap, l[0], r[1], start=False, stop=False)
            return pe.matmul(out_ap, l[0], r[0], start=False, stop=stop)

        with ExitStack() as early:
            def tb(name, shape, dt=F32):
                return early.enter_context(nc.sbuf_tensor(name, shape, dt))

            wmod_s = h2all[:].rearrange("p t d -> p (t d)")[:, 0:KD * 6 * D].rearrange("p (k n) -> p k n", k=KD)
            cT = tb("cT", [P, KD, B])
            cS = tb("cS", [P, KD, B])
            stage = tb("stage", [P, 4 * D * KD + KD * NE + KD * 2 * FS + len(FT) * D])
            modS = tb("modS", [B, 4 * D])
            mrow = tb("mrow", [B, 5, D])
            bvrep = tb("bvrep", [P, KD, B])
            gsgn = tb("gsgn", [B, 2, D])
            bprow = tb("bprow", [B, D])
            MCH = 3

            def ms(j):
                return slice(j * 6 * D // MCH, (j + 1) * 6 * D // MCH)

            at, spans = 0, {}
            for name, n in (("qkv", KD * 3 * D), ("proj", KD * D), ("rt", KD * NE), ("sgu", KD * 2 * FS), ("sd", len(FT) * D)):
                spans[name] = (at, at + n)
                at += n

            def staged(name):
                return stage[:, spans[name][0]:spans[name][1]]

            def two(name, shape, dt=F32):
                return [tb(f"{name}{u}", shape, dt) for u in range(2)]

            def two_hilo(name, shape):
                return [(tb(f"{name}{u}_hi", shape, F32R), tb(f"{name}{u}_lo", shape, F32R)) for u in range(2)]

            xa = two("xa", [P, TT, D])
            xr = two("xr", [P, TT, D])
            mx = two("mx", [P, 2, D])
            mh = two("mh", [P, 2, D])
            ht = two("ht", [P, KD, S])
            hT = two_hilo("hT", [P, KD, S])
            QT = two_hilo("QT", [P, KD, S])
            KT = two_hilo("KT", [P, KD, S])
            VV = two_hilo("VV", [P, TT, D])
            qf = two("qf", [P, S])
            th = two("th", [P, S])
            pr = two("pr", [P, TT, S])
            PT = two_hilo("PT", [P, KD, S])
            h2 = two("h2", [P, TT, D])
            yb = two("yb", [P, TT, D])
            bst1 = tb("bst1", [P, 2 * TT, 6])
            bst2 = tb("bst2", [P, 2 * TT, 6])
            mv1 = tb("mv1", [P, 2 * TT, 2])
            mv2 = tb("mv2", [P, 2 * TT, 2])
            spare1 = tb("spare1", [P, 1])
            spare2 = tb("spare2", [P, 1])
            rs1 = tb("rs1", [P, 2 * TT])
            rs2 = tb("rs2", [P, 2 * TT])
            nm = two("nm", [P, 2, TT])
            ls = two("ls", [P, 2, TT])
            rl = two("rl", [P, 2, TT])
            Sb, TR, CO, QK = psum[0:2], psum[2:4], psum[4:6], psum[6:8]

            def bank(t, a=2):
                return t[:, :].rearrange("p (a n) -> p a n", a=a)

            wq_ = lambda k, m: parts(wqkv, slice(None), k, slice(m * P, (m + 1) * P))

            q3 = staged("qkv").rearrange("p (k n) -> p k n", k=KD)
            d3 = staged("sd").rearrange("p (k n) -> p k n", k=len(FT))
            later = (("rt", wrt), ("sgu", wsgu))

            def sp_setup(sp):
                for j in range(MCH):
                    sp.dma_start(wmod_s[:, :, ms(j)], w_mod[:, ms(j)].rearrange("(k p) n -> p k n", p=P)).then_inc((s_wmod0_in, s_wmod_in, s_wmod_in)[j], 16)
                    if j == 0:
                        sp.dma_start(staged("qkv").rearrange("p (k n) -> p k n", k=KD),
                                     w_qkv.rearrange("(k p) n -> p k n", p=P)).then_inc(s_wqkv_in, 16)
                sp.dma_start(staged("proj").rearrange("p (k n) -> p k n", k=KD),
                             w_proj.rearrange("(k p) n -> p k n", p=P)).then_inc(s_wproj_in, 16)

            def sp_later(sp):
                sp.dma_start(staged("rt").rearrange("p (k n) -> p k n", k=KD),
                             router_t.rearrange("(k p) n -> p k n", p=P)).then_inc(s_wrt_in, 16)
                sp.dma_start(staged("sgu").rearrange("p (k n) -> p k n", k=KD),
                             sh_gu_t.rearrange("(k p) n -> p k n", p=P)).then_inc(s_wsgu_in, 16)
                for j, (f, m) in enumerate(FT):
                    sp.dma_start(staged("sd").rearrange("p (k n) -> p k n", k=len(FT))[0:m, j, :],
                                 sh_down_t[f:f + m, :]).then_inc(s_wsd_in, 16)

            def sp_modrow(sp):
                sp.wait_ge(s_mrow_ready, 1)
                sp.wait_ge(s_guard_pool, 2)
                sp.dma_start(modrow, mrow[:].rearrange("b j d -> b (j d)")).then_inc(s_modrow_out, 16)
                sp.wait_ge(s_modrow_out, 16)

            def pool_setup(pool):
                pool.memset(minus_half[:], -0.5).then_inc(s_const, 1)
                pool.memset(eps_t[:], EPS).then_inc(s_const, 1)
                pool.memset(ident[:], 0.0).then_inc(s_const, 1)
                pool.memset(before[:], 0.0).then_inc(s_const, 1)
                pool.wait_ge(s_const, 4)
                pool.affine_select(out=ident[:], in_=ident[:], compare_op=ALU.not_equal, fill=1.0,
                                   base=0, pattern=[[-1, P]], channel_multiplier=1).then_inc(s_ident_ready, 1)
                pool.affine_select(out=before[:], in_=before[:], compare_op=ALU.is_ge, fill=1.0,
                                   base=0, pattern=[[-1, P]], channel_multiplier=1).then_inc(s_const, 1)
                pool.memset(ones[:], 1.0).then_inc(s_const, 1)
                pool.memset(lower[:], 0.0).then_inc(s_const, 1)
                pool.wait_ge(s_const, 7)
                for j in range(1, NE):
                    pool.memset(lower[:, j, 0:j], 1.0).then_inc(s_const, 1)
                pool.iota(token_id[:], pattern=[[P, B * TT]], base=0, channel_multiplier=1,
                          allow_small_or_imprecise_dtypes=True).then_inc(s_const, 1)
                for t, step in ((eidx, 1), (erow, REGION), (step128, P), (tidx, 1)):
                    pool.iota(t[:], pattern=[[step, t.shape[1]]], base=0, channel_multiplier=0,
                              allow_small_or_imprecise_dtypes=True).then_inc(s_const, 1)
                pool.wait_ge(s_const, 7 + NE - 1 + 5)

            def act_setup(act):
                act.dma_start(cT[:], c_t.rearrange("(k p) b -> p k b", p=P)).then_inc(s_c_in, 16)
                act.dma_start(cols[:, 0:3 * KD], b_cols).then_inc(s_cols_in, 16)
                act.dma_start(cols[:, 3 * KD:3 * KD + 1], gate_col).then_inc(s_cols_in, 16)
                act.dma_start(lw[:, 0:1], cam_w0.partition_broadcast(P)).then_inc(s_cols_in, 16)
                act.dma_start(lw[:, 1:2], cam_w1.partition_broadcast(P)).then_inc(s_cols_in, 16)
                act.dma_start(bprow[:], b_proj.partition_broadcast(B)).then_inc(s_cols_in, 16)
                act.wait_ge(s_c_in, 16)
                act.activation(cS[:], cT[:], ACT.Exp, scale=-1.0).then_inc(s_c_exp, 1)
                act.wait_ge(s_wqkv_in, 16)
                act.activation(wqkv[0][:, :, 0:D], q3[:, :, 0:D], ACT.Copy).then_inc(s_whi, 1)
                act.wait_ge(s_kscaled, 1)
                act.activation(wqkv[0][:, :, D:3 * D], q3[:, :, D:3 * D], ACT.Copy).then_inc(s_whi, 1)
                act.wait_ge(s_lw_sum, 1)
                act.activation(lw[:, 3:4], lw[:, 2:3], ACT.Exp, scale=-1.0).then_inc(s_lw_exp, 1)

            def act_wproj(act):
                act.wait_ge(s_wproj_in, 16)
                act.activation(wproj[0][:], staged("proj").rearrange("p (k n) -> p k n", k=KD), ACT.Copy).then_inc(s_whi, 1)

            def act_later(act):
                for src, (name, dst) in zip((s_wrt_in, s_wsgu_in), later):
                    act.wait_ge(src, 16)
                    act.activation(dst[0][:], staged(name).rearrange("p (k n) -> p k n", k=KD), ACT.Copy).then_inc(s_whi, 1)
                act.wait_ge(s_wsd_in, 16 * len(FT))
                for j, (f, m) in enumerate(FT):
                    act.activation(wsd[0][0:m, j, :], d3[0:m, j, :], ACT.Copy).then_inc(s_whi, 1)

            def dve_silu(dve):
                dve.wait_ge(s_c_exp, 1)
                dve.tensor_scalar(cS[:], cS[:], 1.0, None, ALU.add).then_inc(s_c_chain, 1)
                dve.wait_ge(s_c_chain, 1)
                dve.reciprocal(cS[:], cS[:]).then_inc(s_c_chain, 1)
                dve.wait_ge(s_c_chain, 2)
                dve.tensor_tensor(cS[:], cS[:], cT[:], ALU.mult).then_inc(s_silu_c, 1)

            def dve_kscale(dve):
                dve.wait_ge(s_wqkv_in, 16)
                dve.tensor_scalar(q3[:, :, D:2 * D], q3[:, :, D:2 * D], SCALE, None, ALU.mult).then_inc(s_kscaled, 1)

            def dve_sacol(dve):
                dve.wait_ge(s_modT, 1)
                mt = psum[0][:, 0:2 * KD * B].rearrange("p (j b) -> p j b", b=B)
                dve.tensor_copy(sacol[:, 0:KD, :], mt[:, 0:KD, :]).then_inc(s_sacol_ready, 1)
                dve.tensor_scalar(sacol[:, KD:2 * KD, :], mt[:, KD:2 * KD, :], 1.0, None, ALU.add).then_inc(s_sacol_ready, 1)

            def dve_wqkv(dve):
                dve.wait_ge(s_whi, 1)
                dve.tensor_tensor(wqkv[1][:, :, 0:D], q3[:, :, 0:D], wqkv[0][:, :, 0:D].bitcast(F32),
                                  ALU.subtract).then_inc(s_wlo, 1)
                dve.wait_ge(s_kscaled, 1)
                dve.wait_ge(s_whi, 2)
                dve.tensor_tensor(wqkv[1][:, :, D:3 * D], q3[:, :, D:3 * D], wqkv[0][:, :, D:3 * D].bitcast(F32),
                                  ALU.subtract).then_inc(s_wlo, 1)

            def dve_cols(dve):
                dve.wait_ge(s_cols_in, 16 * 5)
                dve.scalar_tensor_tensor(lw[:, 2:3], lw[:, 1:2], LAYER_DEPTH, lw[:, 0:1],
                                         ALU.mult, ALU.add).then_inc(s_lw_sum, 1)
                dve.tensor_copy(bvrep[:], cols[:, 2 * KD:3 * KD].unsqueeze(2).to_broadcast([P, KD, B])).then_inc(s_cols_ready, 1)
                dve.tensor_scalar(cols[:, KD:2 * KD], cols[:, KD:2 * KD], SCALE, None, ALU.mult).then_inc(s_cols_ready, 1)
                dve.tensor_tensor(cols[:, 3 * KD + 1:3 * KD + 2], cols[:, 3 * KD:3 * KD + 1],
                                  cols[:, 2 * KD:2 * KD + 1], ALU.mult).then_inc(s_cols_ready, 1)

            def dve_lw(dve):
                dve.wait_ge(s_lw_exp, 1)
                dve.tensor_scalar(lw[:, 3:4], lw[:, 3:4], 1.0, None, ALU.add).then_inc(s_c_chain, 1)
                dve.wait_ge(s_c_chain, 3)
                dve.reciprocal(lw[:, 3:4], lw[:, 3:4]).then_inc(s_cols_ready, 1)

            def dve_wproj(dve):
                dve.wait_ge(s_whi, 3)
                dve.tensor_tensor(wproj[1][:], staged("proj").rearrange("p (k n) -> p k n", k=KD),
                                  wproj[0][:].bitcast(F32), ALU.subtract).then_inc(s_wlo, 1)

            def dve_rows(dve):
                dve.wait_ge(s_mod_mm, 1)
                for j in range(2):
                    dve.tensor_copy(modS[:, 512 * j:512 * (j + 1)], psum[4 + j][0:B, :]).then_inc(s_mod_copied, 1)
                dve.wait_ge(s_bvp_done, 1)
                dve.tensor_tensor(bprow[:], bprow[:], psum[2][0:B, 0:D], ALU.add).then_inc(s_bp_ready, 1)

            def pool_rows(pool):
                pool.wait_ge(s_mod_copied, 2)
                pool.tensor_scalar(mrow[:, 2, :], modS[:, 2 * D:3 * D], 1.0, None, ALU.add).then_inc(s_guard_pool, 1)
                pool.tensor_copy(mrow[:, 3, :], modS[:, D:2 * D]).then_inc(s_guard_pool, 1)

            def dve_guard(dve):
                dve.wait_ge(s_mod_copied, 2)
                raw = modS[:].rearrange("b (g d) -> b g d", d=D)[:, 0:4:3, :]
                kept = mrow[:, 0:5:4, :]
                dve.tensor_scalar(gsgn[:], raw, 0.0, 2.0, ALU.is_ge, ALU.mult)
                dve.scalar_tensor_tensor(kept, raw, -1.0, raw, ALU.mult, ALU.max).then_inc(s_guard, 1)
                dve.wait_ge(s_guard, 1)
                dve.tensor_scalar(kept, kept, GUARD, None, ALU.max).then_inc(s_guard, 1)
                dve.wait_ge(s_guard, 2)
                dve.scalar_tensor_tensor(kept, gsgn[:], 1.0, kept, ALU.subtract, ALU.mult).then_inc(s_guard, 1)
                dve.wait_ge(s_guard, 3)
                dve.wait_ge(s_bp_ready, 1)
                dve.tensor_tensor(mrow[:, 1, :], mrow[:, 0, :], bprow[:], ALU.mult).then_inc(s_mrow_ready, 1)

            def dve_later(dve):
                for n, (name, dst) in enumerate(later):
                    dve.wait_ge(s_whi, 4 + n)
                    dve.tensor_tensor(dst[1][:], staged(name).rearrange("p (k n) -> p k n", k=KD),
                                      dst[0][:].bitcast(F32), ALU.subtract).then_inc(s_wlo, 1)

            def dve_between(dve):
                for j, (f, m) in enumerate(FT):
                    dve.wait_ge(s_whi, 6 + j)
                    dve.tensor_tensor(wsd[1][0:m, j, :], d3[0:m, j, :], wsd[0][0:m, j, :].bitcast(F32),
                                      ALU.subtract).then_inc(s_wlo, 1)

            def pe_modcol(pe):
                pe.wait_ge(s_silu_c, 1)
                pe.wait_ge(s_wmod0_in, 16)
                for j in range(2 * KD):
                    for k in range(KD):
                        last = pe.matmul(psum[0][:, j * B:(j + 1) * B], wmod_s[:, k, j * P:(j + 1) * P], cS[:, k, :],
                                         start=(k == 0), stop=(k == KD - 1))
                last.then_inc(s_modT, 1)

            def pe_modrow(pe):
                pe.wait_ge(s_wmod_in, 32)
                for j in range(2):
                    for k in range(KD):
                        last = pe.matmul(psum[4 + j][0:B, :], cS[:, k, :], wmod_s[:, k, ms(1 + j)],
                                         start=(k == 0), stop=(k == KD - 1))
                last.then_inc(s_mod_mm, 1)
                pe.wait_ge(s_cols_ready, 3)
                pe.wait_ge(s_wproj_in, 16)
                wp3 = staged("proj").rearrange("p (k n) -> p k n", k=KD)
                for k in range(KD):
                    last = pe.matmul(psum[2][0:B, 0:D], bvrep[:, k, :], wp3[:, k, :], start=(k == 0), stop=(k == KD - 1))
                last.then_inc(s_bvp_done, 1)

            def pe_xt(pe, b, u):
                pe.wait_ge(s_xn_ready, b + 1)
                for d in range(KD):
                    for t in range(TT):
                        last = pe.transpose(TR[u][:, d * S + t * P:d * S + (t + 1) * P],
                                            xa[u][:, t, d * P:(d + 1) * P], ident[:])
                last.then_inc(s_xt_done, 1)

            def pe_qk(pe, b, u):
                pe.wait_ge(s_h_lo, b + 1)
                if u == 1:
                    pe.wait_ge(s_qk_hi, b)
                    pe.wait_ge(s_qk_lo, b)
                for half, dst in enumerate(QK):
                    for m in range(KD):
                        for k in range(KD):
                            last = mm3(pe, dst[:, m * S:(m + 1) * S], wq_(k, half * KD + m),
                                       parts(hT[u], slice(None), k), k == 0, k == KD - 1)
                    last.then_inc(s_qk_done, 1)

            def pe_v(pe, b, u):
                for t in range(TT):
                    for k in range(KD):
                        last = mm3(pe, QK[u][:, t * D:(t + 1) * D],
                                   parts(hT[u], slice(None), k, slice(t * P, (t + 1) * P)),
                                   parts(wqkv, slice(None), k, slice(2 * D, 3 * D)), k == 0, k == KD - 1)
                last.then_inc(s_v_done, 1)

            def pe_scores(pe, b, u, second):
                if second:
                    pe.wait_ge(s_qp_hi, b + 1)
                    pe.wait_ge(s_qp_lo, b + 1)
                else:
                    pe.wait_ge(s_qk_hi, b + 1)
                    pe.wait_ge(s_qk_lo, b + 1)
                ks = KD if second else 1
                for t in range(TT):
                    for k in range(ks):
                        last = mm3(pe, Sb[u][:, t * S:(t + 1) * S],
                                   parts(QT[u], slice(None), k, slice(t * P, (t + 1) * P)),
                                   parts(KT[u], slice(None), k), k == 0, k == ks - 1)
                last.then_inc(s_s2_done if second else s_s1_done, 1)

            def pe_pt(pe, b, u, second):
                pe.wait_ge(s_exp2 if second else s_norm1, b + 1)
                for k in range(TT):
                    for t in range(TT):
                        last = pe.transpose(TR[u][:, k * S + t * P:k * S + (t + 1) * P],
                                            pr[u][:, t, k * P:(k + 1) * P], ident[:])
                last.then_inc(s_pt2_done if second else s_pt1_done, 1)

            def pe_ctx(pe, b, u, second):
                if second:
                    pe.wait_ge(s_pt2_hi, b + 1)
                    pe.wait_ge(s_pt2_lo, b + 1)
                else:
                    pe.wait_ge(s_pt1_hi, b + 1)
                    pe.wait_ge(s_pt1_lo, b + 1)
                    pe.wait_ge(s_v_hi, b + 1)
                    pe.wait_ge(s_v_lo, b + 1)
                for m in range(KD if second else 1):
                    for k in range(TT):
                        last = mm3(pe, CO[u][:, m * S:(m + 1) * S],
                                   parts(VV[u], slice(None), k, slice(m * P, (m + 1) * P)),
                                   parts(PT[u], slice(None), k), k == 0, k == TT - 1)
                last.then_inc(s_c2_done if second else s_c1_done, 1)

            def pe_out(pe, b, u):
                pe.wait_ge(s_wlo, 3)
                pe.wait_ge(s_ctx_hi, b + 1)
                pe.wait_ge(s_ctx_lo, b + 1)
                for t in range(TT):
                    for m in range(KD):
                        last = mm3(pe, CO[u][:, t * D:(t + 1) * D],
                                   parts(PT[u], slice(None), m, slice(t * P, (t + 1) * P)),
                                   parts(wproj, slice(None), m), m == 0, m == KD - 1)
                last.then_inc(s_o_done, 1)

            def pe_h2t(pe, b, u):
                pe.wait_ge(s_h2_ready, b + 1)
                for d in range(KD):
                    for t in range(TT):
                        last = pe.transpose(TR[u][:, d * S + t * P:d * S + (t + 1) * P],
                                            h2[u][:, t, d * P:(d + 1) * P], ident[:])
                last.then_inc(s_h2t_done, 1)

            def pe_logits(pe, b, u):
                pe.wait_ge(s_wlo, 4)
                pe.wait_ge(s_h2_hi, b + 1)
                pe.wait_ge(s_h2_lo, b + 1)
                for k in range(KD):
                    last = mm3(pe, TR[u][0:NE, 0:S], parts(wrt, slice(None), k),
                               parts(h2T, slice(None), k, ds(b * S, S)), k == 0, k == KD - 1)
                last.then_inc(s_lg_done, 1)

            def act_exp(act, b, u, second):
                act.wait_ge(s_max2 if second else s_max1, b + 1)
                i = int(second)
                for t in range(TT):
                    last = act.activation(pr[u][:, t, :], Sb[u][:, t * S:(t + 1) * S], ACT.Exp,
                                          bias=nm[u][:, i, t:t + 1], accum_out=ls[u][:, i, t:t + 1])
                last.then_inc(s_exp2 if second else s_exp1, 1)

            def act_norm(act, b, u):
                act.wait_ge(s_rl1, b + 1)
                for t in range(TT):
                    last = act.activation(pr[u][:, t, :], pr[u][:, t, :], ACT.Copy, scale=rl[u][:, 0, t:t + 1])
                last.then_inc(s_norm1, 1)

            def act_copy(act, ready, b, dst, src, done):
                act.wait_ge(ready, b + 1)
                act.activation(dst, src, ACT.Copy).then_inc(done, 1)

            def act_h(act, b, u):
                act.wait_ge(s_xt_done, b + 1)
                for d in range(KD):
                    last = act.activation(ht[u][:, d, :], TR[u][:, d * S:(d + 1) * S], ACT.Identity,
                                          scale=sacol[:, KD + d, ds(b, 1)], bias=sacol[:, d, ds(b, 1)])
                last.then_inc(s_ht_ready, 1)

            def act_qk(act, b, u):
                for half, dst in enumerate((QT, KT)):
                    act.wait_ge(s_qk_done, 2 * b + 1 + half)
                    for m in range(KD):
                        last = act.activation(dst[u][0][:, m, :], QK[half][:, m * S:(m + 1) * S], ACT.Identity,
                                              bias=cols[:, half * KD + m:half * KD + m + 1])
                last.then_inc(s_qk_hi, 1)

            def act_tanh(act, b, u):
                act.wait_ge(s_c1_done, b + 1)
                act.activation(th[u][:], CO[u][:, 0:S], ACT.Tanh, scale=cols[:, 3 * KD:3 * KD + 1],
                               bias=cols[:, 3 * KD + 1:3 * KD + 2]).then_inc(s_tanh_done, 1)

            def act_ctx(act, b, u):
                act.wait_ge(s_c2_done, b + 1)
                act.activation(PT[u][0][:], bank(CO[u]), ACT.Copy).then_inc(s_ctx_hi, 1)

            def dve_max(dve, b, u, second):
                dve.wait_ge(s_s2_done if second else s_s1_done, b + 1)
                dve.tensor_reduce(nm[u][:, int(second), :], bank(Sb[u]), AX.X, ALU.max,
                                  negate=True).then_inc(s_max2 if second else s_max1, 1)

            def dve_rl(dve, b, u, second):
                i = int(second)
                dve.wait_ge(s_exp2 if second else s_exp1, b + 1)
                dve.reciprocal(rl[u][:, i, :], ls[u][:, i, :]).then_inc(s_rl2 if second else s_rl1, 1)

            def dve_lo(dve, ready, b, src, hi, lo, done):
                dve.wait_ge(ready, b + 1)
                dve.tensor_tensor(lo, src, hi.bitcast(F32), ALU.subtract).then_inc(done, 1)

            def dve_h(dve, b, u):
                dve.wait_ge(s_ht_ready, b + 1)
                dve.tensor_copy(hT[u][0][:], ht[u][:]).then_inc(s_h_hi, 1)
                dve.wait_ge(s_h_hi, b + 1)
                dve.tensor_tensor(hT[u][1][:], ht[u][:], hT[u][0][:].bitcast(F32), ALU.subtract).then_inc(s_h_lo, 1)

            def biased_lo(dve, dst, src, bias, m):
                return dve.scalar_tensor_tensor(dst[1][:, m, :], src[:, m * S:(m + 1) * S], bias,
                                                dst[0][:, m, :].bitcast(F32), ALU.add, ALU.subtract)

            def dve_qk(dve, b, u):
                dve.wait_ge(s_qk_hi, b + 1)
                for half, dst in enumerate((QT, KT)):
                    for m in range(KD):
                        last = biased_lo(dve, dst[u], QK[half], cols[:, half * KD + m:half * KD + m + 1], m)
                last.then_inc(s_qk_lo, 1)

            def dve_qp(dve, b, u):
                dve.wait_ge(s_tanh_done, b + 1)
                dve.wait_ge(s_qf_ready, b + 1)
                dve.scalar_tensor_tensor(qf[u][:], th[u][:], lw[:, 3:4], qf[u][:], ALU.mult, ALU.add).then_inc(s_qp_ready, 1)

            def dve_x1(dve, b, u):
                dve.wait_ge(s_o_done, b + 1)
                dve.wait_ge(s_rl2, b + 1)
                dve.wait_ge((s_mx0_in, s_mx1_in)[u], 8 * (b - u + 2))
                for t in range(TT):
                    last = dve.scalar_tensor_tensor(yb[u][:, t, :], CO[u][:, t * D:(t + 1) * D], rl[u][:, 1, t:t + 1],
                                                    mx[u][:, 0, :], ALU.mult, ALU.mult)
                last.then_inc(s_y_ready, 1)

            def dve_stats(dve, p, src, bst, mv, spare, stats, var, ready):
                for u in range(2):
                    dve.wait_ge(*ready(u))
                    for t in range(TT):
                        last = dve.bn_stats(bst[:, u * TT + t, :], src[u][:, t, :])
                last.then_inc(stats, 1)
                dve.wait_ge(stats, 2 * p + 1)
                dve.memset(spare[:], 0.0).then_inc(stats, 1)
                for j in range(2 * TT):
                    last = dve.bn_aggr(mv[:, j, :], bst[:, j, :])
                last.then_inc(var, 1)

            def dve_ln1_stats(dve, p):
                dve_stats(dve, p, xa, bst1, mv1, spare1, s_stats1, s_var1, lambda u: ((s_xa0_in, s_xa1_in)[u], 16 * (p + 1)))

            def dve_ln2_stats(dve, p):
                dve_stats(dve, p, xr, bst2, mv2, spare2, s_stats2, s_var2, lambda u: (s_x1_ready, 2 * p + 1 + u))

            def dve_normalise(dve, p, rstd, src, dst, mv, rs, done):
                dve.wait_ge(rstd, 2 * p + 2)
                for u in range(2):
                    for t in range(TT):
                        j = u * TT + t
                        last = dve.tensor_scalar(dst[u][:, t, :], src[u][:, t, :], mv[:, j, 0:1], rs[:, j:j + 1],
                                                 ALU.subtract, ALU.mult)
                    last.then_inc(done, 1)

            def pool_xg(pool, b, u):
                pool.wait_ge((s_xr0_in, s_xr1_in)[u], 8 * (b - u + 2))
                pool.wait_ge((s_mx0_in, s_mx1_in)[u], 8 * (b - u + 2))
                pool.tensor_tensor(xr[u][:], xr[u][:], mx[u][:, 1:2, :].to_broadcast([P, TT, D]), ALU.add).then_inc(s_xg_ready, 1)

            def pool_rstd(pool, p, var, mv, rs, rstd):
                pool.wait_ge(var, p + 1)
                pool.tensor_tensor(rs[:], mv[:, :, 1], eps_t[:], ALU.add).then_inc(rstd, 1)
                pool.wait_ge(rstd, 2 * p + 1)
                pool.tensor_tensor(rs[:], rs[:], minus_half[:], ALU.pow).then_inc(rstd, 1)

            def pool_qf(pool, b, u):
                pool.wait_ge(s_qk_lo, b + 1)
                pool.tensor_tensor(qf[u][:], QT[u][0][:, 0, :].bitcast(F32), QT[u][1][:, 0, :].bitcast(F32),
                                   ALU.add).then_inc(s_qf_ready, 1)

            def make_x1(pool, b, u):
                pool.wait_ge(s_xg_ready, b + 1)
                pool.wait_ge(s_y_ready, b + 1)
                pool.tensor_tensor(xr[u][:], xr[u][:], yb[u][:], ALU.add).then_inc(s_x1_ready, 1)

            def make_h2(pool, b, u):
                pool.wait_ge((s_mh0_in, s_mh1_in)[u], 8 * (b - u + 2))
                pool.wait_ge(s_xn2_ready, b + 1)
                if not (type(b) is int and b < 2):
                    pool.wait_ge((s_h2c0, s_h2c1)[u], 8 * (b - u))
                pool.tensor_tensor(h2[u][:], yb[u][:], mh[u][:, 0:1, :].to_broadcast([P, TT, D]), ALU.mult).then_inc(s_h2_chain, 1)
                pool.wait_ge(s_h2_chain, b + 1)
                pool.tensor_tensor(h2[u][:], h2[u][:], mh[u][:, 1:2, :].to_broadcast([P, TT, D]), ALU.add).then_inc(s_h2_ready, 1)

            def pair_of(p):
                return ((2 * p, 0), (2 * p + 1, 1))

            def pe_turn(pe, p, post, front):
                for b, u in pair_of(p):
                    pe_scores(pe, b, u, False)
                for b, u in pair_of(p):
                    pe_v(pe, b, u)
                for b, u in pair_of(p):
                    pe_pt(pe, b, u, False)
                for b, u in pair_of(p):
                    pe_ctx(pe, b, u, False)
                if front:
                    for b, u in pair_of(p + 1):
                        pe_xt(pe, b, u)
                for b, u in pair_of(p):
                    pe_scores(pe, b, u, True)
                if front:
                    pe_qk(pe, 2 * p + 2, 0)
                for b, u in pair_of(p):
                    pe_pt(pe, b, u, True)
                for b, u in pair_of(p):
                    pe_ctx(pe, b, u, True)
                if front:
                    pe_qk(pe, 2 * p + 3, 1)
                for b, u in pair_of(p):
                    pe_out(pe, b, u)
                    if post:
                        pe_h2t(pe, b - 2, u)
                if post:
                    for b, u in pair_of(p - 1):
                        pe_logits(pe, b, u)

            def act_turn(act, p, post, front):
                for b, u in pair_of(p):
                    act_exp(act, b, u, False)
                act_norm(act, 2 * p, 0)
                act_copy(act, s_v_done, 2 * p, VV[0][0][:], bank(QK[0]), s_v_hi)
                act_norm(act, 2 * p + 1, 1)
                act_copy(act, s_pt1_done, 2 * p, PT[0][0][:], bank(TR[0]), s_pt1_hi)
                act_copy(act, s_v_done, 2 * p + 1, VV[1][0][:], bank(QK[1]), s_v_hi)
                act_copy(act, s_pt1_done, 2 * p + 1, PT[1][0][:], bank(TR[1]), s_pt1_hi)
                for b, u in pair_of(p):
                    act_tanh(act, b, u)
                for b, u in pair_of(p):
                    act_copy(act, s_qp_ready, b, QT[u][0][:, 0, :], qf[u][:], s_qp_hi)
                if front:
                    for b, u in pair_of(p + 1):
                        act_h(act, b, u)
                for b, u in pair_of(p):
                    act_exp(act, b, u, True)
                for b, u in pair_of(p):
                    act_copy(act, s_pt2_done, b, PT[u][0][:], bank(TR[u]), s_pt2_hi)
                if front:
                    act_qk(act, 2 * p + 2, 0)
                for b, u in pair_of(p):
                    act_ctx(act, b, u)
                if front:
                    act_qk(act, 2 * p + 3, 1)
                if post:
                    act_post(act, p - 1)

            def act_post(act, p):
                for b, u in pair_of(p):
                    act_copy(act, s_h2t_done, b, h2T[0][:, :, ds(b * S, S)], bank(TR[u]), s_h2_hi)
                for b, u in pair_of(p):
                    act_copy(act, s_lg_done, b, lgall[0:NE, ds(b * S, S)], TR[u][0:NE, 0:S], s_lg_copied)

            def dve_turn(dve, p, post, front, between=None):
                for b, u in pair_of(p):
                    dve_max(dve, b, u, False)
                if front:
                    dve_ln1_stats(dve, p + 1)
                for b, u in pair_of(p):
                    dve_rl(dve, b, u, False)
                for b, u in pair_of(p):
                    dve_lo(dve, s_v_hi, b, bank(QK[u]), VV[u][0][:], VV[u][1][:], s_v_lo)
                    dve_lo(dve, s_pt1_hi, b, bank(TR[u]), PT[u][0][:], PT[u][1][:], s_pt1_lo)
                if front:
                    dve_normalise(dve, p + 1, s_rstd1, xa, xa, mv1, rs1, s_xn_ready)
                for b, u in pair_of(p):
                    dve_qp(dve, b, u)
                for b, u in pair_of(p):
                    dve_lo(dve, s_qp_hi, b, qf[u][:], QT[u][0][:, 0, :], QT[u][1][:, 0, :], s_qp_lo)
                if between:
                    between(dve)
                if front:
                    dve_h(dve, 2 * p + 2, 0)
                for b, u in pair_of(p):
                    dve_max(dve, b, u, True)
                if post:
                    dve_ln2_stats(dve, p - 1)
                if front:
                    dve_h(dve, 2 * p + 3, 1)
                for b, u in pair_of(p):
                    dve_rl(dve, b, u, True)
                for b, u in pair_of(p):
                    dve_lo(dve, s_pt2_hi, b, bank(TR[u]), PT[u][0][:], PT[u][1][:], s_pt2_lo)
                if front:
                    dve_qk(dve, 2 * p + 2, 0)
                if post:
                    dve_normalise(dve, p - 1, s_rstd2, xr, yb, mv2, rs2, s_xn2_ready)
                for b, u in pair_of(p):
                    dve_lo(dve, s_ctx_hi, b, bank(CO[u]), PT[u][0][:], PT[u][1][:], s_ctx_lo)
                if front:
                    dve_qk(dve, 2 * p + 3, 1)
                if post:
                    dve_h2_lo(dve, p - 1)
                for b, u in pair_of(p):
                    dve_x1(dve, b, u)
                if not front:
                    for b, u in pair_of(p):
                        make_x1(dve, b, u)

            def dve_h2_lo(dve, p):
                for b, u in pair_of(p):
                    dve_lo(dve, s_h2_hi, b, bank(TR[u]), h2T[0][:, :, ds(b * S, S)], h2T[1][:, :, ds(b * S, S)], s_h2_lo)

            def pool_turn(pool, p, post, front):
                if front:
                    pool_rstd(pool, p + 1, s_var1, mv1, rs1, s_rstd1)
                if post:
                    pool_rstd(pool, p - 1, s_var2, mv2, rs2, s_rstd2)
                    for b, u in pair_of(p - 1):
                        make_h2(pool, b, u)
                if front:
                    pool_qf(pool, 2 * p + 2, 0)
                    pool_qf(pool, 2 * p + 3, 1)
                for b, u in pair_of(p):
                    pool_xg(pool, b, u)
                if front:
                    for b, u in pair_of(p):
                        make_x1(pool, b, u)

            def sp_front(sp, p):
                for b, u in pair_of(p):
                    if not (type(p) is int and p == 0):
                        sp.wait_ge(s_xt_done, b - 1)
                    sp.dma_start(xa[u][:], x_in[ds(b, 1)].rearrange("o (t p) d -> p (o t) d", p=P)).then_inc((s_xa0_in, s_xa1_in)[u], 16)

            def sp_mid(sp, p, first):
                for b, u in pair_of(p):
                    if not first:
                        sp.wait_ge(s_x1_ready, b - 1)
                    sp.dma_start(mx[u][:], modrow[ds(b, 1), 0:2 * D].to_broadcast([P, 2 * D]).rearrange("p (j d) -> p j d", d=D)).then_inc((s_mx0_in, s_mx1_in)[u], 16)
                    if not first:
                        sp.wait_ge((s_x1_out0, s_x1_out1)[u], 8 * (b - u))
                        sp.wait_ge(s_xn2_ready, b - 1)
                    sp.dma_start(xr[u][:], x_in[ds(b, 1)].rearrange("o (t p) d -> p (o t) d", p=P)).then_inc((s_xr0_in, s_xr1_in)[u], 16)

            def sp_rows(sp, p, first):
                for b, u in pair_of(p):
                    if not first:
                        sp.wait_ge(s_h2_ready, b - 1)
                    sp.dma_start(mh[u][:], modrow[ds(b, 1), 2 * D:4 * D].to_broadcast([P, 2 * D]).rearrange("p (j d) -> p j d", d=D)).then_inc((s_mh0_in, s_mh1_in)[u], 16)

            def sp_store(sp, p):
                for b, u in pair_of(p):
                    sp.wait_ge(s_x1_ready, b + 1)
                    sp.dma_start(x1_dram[ds(b, 1)].rearrange("o (t p) d -> p (o t) d", p=P), xr[u][:]).then_inc((s_x1_out0, s_x1_out1)[u], 16)

            def sp_keep(sp, p):
                for b, u in pair_of(p):
                    sp.wait_ge(s_h2_ready, b + 1)
                    sp.dma_start(h2all[:, ds(b * TT, TT), 0:D], h2[u][:]).then_inc((s_h2c0, s_h2c1)[u], 16)

            with nc.Block() as block:
                @block.sync
                def _(sp):
                    sp_front(sp, 0)
                    sp_setup(sp)
                    sp_front(sp, 1)
                    sp_later(sp)
                    sp_modrow(sp)
                    sp_mid(sp, 0, True)
                    sp_rows(sp, 0, True)
                    with sp.Fori(1, NPAIR - 1) as p:
                        sp_front(sp, p + 1)
                        sp_store(sp, p - 1)
                        sp_mid(sp, p, False)
                        sp_rows(sp, p, False)
                        sp_keep(sp, p - 1)
                    p = NPAIR - 1
                    sp_store(sp, p - 1)
                    sp_mid(sp, p, False)
                    sp_rows(sp, p, False)
                    sp_keep(sp, p - 1)
                    sp_store(sp, p)
                    sp_keep(sp, p)
                    for x in (s_x1_out0, s_x1_out1, s_h2c0, s_h2c1):
                        sp.wait_ge(x, 16 * NPAIR)

                @block.gpsimd
                def _(pool):
                    pool_setup(pool)
                    pool_rstd(pool, 0, s_var1, mv1, rs1, s_rstd1)
                    pool_qf(pool, 0, 0)
                    pool_rows(pool)
                    pool_qf(pool, 1, 1)
                    pool_turn(pool, 0, False, True)
                    with pool.Fori(1, NPAIR - 1) as p:
                        pool_turn(pool, p, True, True)
                    p = NPAIR - 1
                    pool_turn(pool, p, True, False)
                    pool_rstd(pool, p, s_var2, mv2, rs2, s_rstd2)

                @block.scalar
                def _(act):
                    act_setup(act)
                    act.wait_ge(s_sacol_ready, 2)
                    for b, u in pair_of(0):
                        act_h(act, b, u)
                    act_wproj(act)
                    act.wait_ge(s_cols_ready, 3)
                    for b, u in pair_of(0):
                        act_qk(act, b, u)
                    act_later(act)
                    act_turn(act, 0, False, True)
                    with act.Fori(1, NPAIR - 1) as p:
                        act_turn(act, p, True, True)
                    act_turn(act, NPAIR - 1, True, False)
                    act_post(act, NPAIR - 1)

                @block.vector
                def _(dve):
                    dve_silu(dve)
                    dve_kscale(dve)
                    dve_ln1_stats(dve, 0)
                    dve_sacol(dve)
                    dve_normalise(dve, 0, s_rstd1, xa, xa, mv1, rs1, s_xn_ready)
                    dve_cols(dve)
                    dve_wqkv(dve)
                    for b, u in pair_of(0):
                        dve_h(dve, b, u)
                    dve_lw(dve)
                    dve.wait_ge(s_cols_ready, 4)
                    dve_qk(dve, 0, 0)
                    dve_rows(dve)
                    dve_guard(dve)
                    dve_qk(dve, 1, 1)
                    dve_wproj(dve)
                    dve_later(dve)
                    dve_turn(dve, 0, False, True, dve_between)
                    with dve.Fori(1, NPAIR - 1) as p:
                        dve_turn(dve, p, True, True)
                    dve_turn(dve, NPAIR - 1, True, False)
                    p = NPAIR - 1
                    dve_ln2_stats(dve, p)
                    dve_normalise(dve, p, s_rstd2, xr, yb, mv2, rs2, s_xn2_ready)
                    for b, u in pair_of(p):
                        make_h2(dve, b, u)
                    dve_h2_lo(dve, p)

                @block.tensor
                def _(pe):
                    pe.wait_ge(s_ident_ready, 1)
                    pe_modcol(pe)
                    for b, u in pair_of(0):
                        pe_xt(pe, b, u)
                    pe.wait_ge(s_wlo, 2)
                    pe_qk(pe, 0, 0)
                    pe.wait_ge(s_h_lo, 2)
                    pe_modrow(pe)
                    pe_qk(pe, 1, 1)
                    pe.wait_ge(s_bp_ready, 1)
                    pe_turn(pe, 0, False, True)
                    with pe.Fori(1, NPAIR - 1) as p:
                        pe_turn(pe, p, True, True)
                    pe_turn(pe, NPAIR - 1, True, False)
                    p = NPAIR - 1
                    pe.wait_ge(s_lg_copied, 2 * p)
                    for b, u in pair_of(p):
                        pe_h2t(pe, b, u)
                    for b, u in pair_of(p):
                        pe_logits(pe, b, u)

        attention_weights.close()
        with ExitStack() as ffn:
            def tb(name, shape, dt=F32):
                return ffn.enter_context(nc.sbuf_tensor(name, shape, dt))

            def ring(name, n, shape, dt=F32):
                return [tb(f"{name}{r}", shape, dt) for r in range(n)]

            def ring_hilo(name, n, shape):
                return [(tb(f"{name}{r}_hi", shape, F32R), tb(f"{name}{r}_lo", shape, F32R)) for r in range(n)]

            W1 = KD * 2 * F
            wgu = (tb("wgu_hi", [P, KD, NE * 2 * F], F32R), tb("wgu_lo", [P, KD, NE * 2 * F], F32R))
            wdn = (tb("wdn_hi", [FH, 2, NE * D], F32R), tb("wdn_lo", [FH, 2, NE * D], F32R))
            wstage = ring("wstage", 2, [P, W1 + 2 * D])
            res = tb("res", [P, B, TT, D])
            gball = lgall[:].rearrange("p (b o d) -> p b o d", b=B, o=1)
            x1b = ring("x1b", 2, [P, TT, D])
            sact = ring("sact", 2, [P, S])
            aact = ring("aact", 2, [P, S])
            aT = ring_hilo("aT", 2, [P, len(FT), S])
            og = ring("og", 2, [P, TT, D])
            xt_in = ring("xt_in", 4, [P, ROW])
            eT = [tuple(h[:, 0, q * S:(q + 1) * S].rearrange("p (k n) -> p k n", k=KD) for h in h2T) for q in range(4)]
            avT = [tuple(h[0:FH, 1, q * S:(q + 1) * S].rearrange("p (k n) -> p k n", k=2) for h in h2T) for q in range(2)]
            sg = [wstage[q][:, 0:F] for q in range(2)]
            av = [wstage[q][:, F:2 * F] for q in range(2)]
            yo = [wstage[q % 2][:, 2 * F + q // 2 * D:2 * F + (q // 2 + 1) * D] for q in range(4)]
            second = ring("second", 2, [P, 1])
            wt = ring("wt", 2, [P, 1])
            dest = ring("dest", 4, [P, 1], U32)

            NR = T // P
            NG = NE // 2
            taken = [0]

            def scratch(*shape):
                n = int(np.prod(shape))
                at = B // 2 * TT * D + taken[0]
                taken[0] += n
                flat = res[:].rearrange("p b t d -> p (b t d)")[:, at:at + n]
                names = "abc"[:len(shape)]
                return flat.rearrange(f"p ({' '.join(names)}) -> p {' '.join(names)}", **dict(zip(names, shape)))

            r_sc = scratch(NR, NE)
            r_mx = scratch(NR)
            r_gm = scratch(NR, NG)
            r_gt, r_eq = (lgall[:, i * NR * NE * NE:(i + 1) * NR * NE * NE].rearrange("p (t j i) -> p t j i", j=NE, i=NE)
                          for i in range(2))
            r_grank = scratch(NR, NG)
            r_rank = scratch(NR, NE)
            r_sel = scratch(2, NR, NE)
            r_both = scratch(NR, NE // 2).bitcast(BF16)
            r_pos = scratch(NR, NE)
            r_tmp = scratch(2, NR, NE)
            r_slot = scratch(2, NR)
            slot_u = tb("slot_u", [P, 2, NR], U32)
            r_w = scratch(2, NR)
            r_at = scratch(2, NR)
            r_cnt = scratch(NE)
            r_last = scratch(NE)
            r_end = scratch(NE, T // P)
            r_tiles = scratch(NE)
            r_ends = scratch(NE)
            r_done = scratch(NT, NE)
            r_tab = scratch(4, NT)
            pad = tb("pad", [P, ROW])

            def gu_stage(r):
                return wstage[r][:, 0:W1].rearrange("p (k n) -> p k n", k=KD)

            def dn_stage(r):
                return wstage[r][0:FH, W1:].rearrange("p (j n) -> p j n", j=2)

            def bank2(t, n=256):
                return t[:, 0:2 * n].rearrange("p (a n) -> p a n", a=2)

            GUb = [psum[0:3], psum[3:6]]
            DN = psum[6:8]
            XTb, EGU, ATb, EDN = psum[0:2], psum[2:4], psum[4:6], psum[6:8]

            LOG = psum[6][:, 0:NR * NE]
            RNK = psum[7][:, 0:NR * NE]
            TOT = psum[7][:, NR * NE:(NR + 1) * NE]

            def pe_logits_t(pe):
                for j in range(NR):
                    last = pe.transpose(LOG[:, j * NE:(j + 1) * NE], lgall[0:NE, j * P:(j + 1) * P], ident[0:NE, 0:NE])
                last.then_inc(s_lt_done, 1)

            def pe_rank(pe):
                pe.wait_ge(s_both_ready, 1)
                pe.matmul(RNK, before[:], r_both.rearrange("p t e -> p (t e)"), start=True, stop=False)
                for j in range(NR - 1):
                    pe.matmul(RNK[:, (j + 1) * NE:].rearrange("p (t e) -> p t e", e=NE), ones[:],
                              r_both[:, j:j + 1, :].to_broadcast([P, NR - 1 - j, NE]), start=False, stop=(j == NR - 2))
                for j in range(NR):
                    last = pe.matmul(TOT, ones[:], r_both[:, j, :], start=(j == 0), stop=(j == NR - 1))
                last.then_inc(s_rank_done, 1)

            def dve_route_scores(dve):
                dve.wait_ge(s_lt_done, 1)
                L = LOG.rearrange("p (t e) -> p t e", e=NE)
                dve.tensor_reduce(r_mx, L, AX.X, ALU.max).then_inc(s_rt_a, 1)
                dve.wait_ge(s_rt_a, 1)
                dve.tensor_tensor(r_sc, L, r_mx.unsqueeze(2).to_broadcast([P, NR, NE]), ALU.subtract).then_inc(s_rt_a, 1)

            def act_route(act):
                act.wait_ge(s_rt_a, 2)
                act.activation(r_sc, r_sc, ACT.Exp).then_inc(s_rt_exp, 1)

            def dve_route_select(dve):
                k = [0]

                def done(ins):
                    ins.then_inc(s_rt_b, 1)
                    k[0] += 1
                    return k[0]

                dve.wait_ge(s_rt_exp, 1)
                n = done(dve.tensor_reduce(r_mx, r_sc, AX.X, ALU.add))
                dve.wait_ge(s_rt_b, n)
                n = done(dve.reciprocal(r_mx, r_mx))
                dve.wait_ge(s_rt_b, n)
                n = done(dve.tensor_tensor(r_sc, r_sc, r_mx.unsqueeze(2).to_broadcast([P, NR, NE]), ALU.mult))
                dve.wait_ge(s_rt_b, n)
                pairs = r_sc.rearrange("p t (g i) -> p t g i", i=2)
                n = done(dve.tensor_tensor(r_gm, pairs[:, :, :, 0], pairs[:, :, :, 1], ALU.max))
                dve.wait_ge(s_rt_b, n)

                def rank(vals, m, out_ap):
                    a = vals[:].unsqueeze(2).to_broadcast([P, NR, m, m])
                    c = vals[:].unsqueeze(3).to_broadcast([P, NR, m, m])
                    dve.tensor_tensor(r_gt[:, :, 0:m, 0:m], a, c, ALU.is_gt)
                    n = done(dve.tensor_tensor(r_eq[:, :, 0:m, 0:m], a, c, ALU.is_equal))
                    dve.wait_ge(s_rt_b, n)
                    n = done(dve.tensor_tensor(r_eq[:, :, 0:m, 0:m], r_eq[:, :, 0:m, 0:m],
                                               lower[:, 0:m, 0:m].unsqueeze(1).to_broadcast([P, NR, m, m]), ALU.mult))
                    dve.wait_ge(s_rt_b, n)
                    n = done(dve.tensor_tensor(r_gt[:, :, 0:m, 0:m], r_gt[:, :, 0:m, 0:m], r_eq[:, :, 0:m, 0:m], ALU.add))
                    dve.wait_ge(s_rt_b, n)
                    n = done(dve.tensor_reduce(out_ap, r_gt[:, :, 0:m, 0:m], AX.X, ALU.add))
                    dve.wait_ge(s_rt_b, n)

                rank(r_gm, NG, r_grank)
                n = done(dve.tensor_scalar(r_gm, r_grank, 2.0, None, ALU.is_lt))
                dve.wait_ge(s_rt_b, n)
                for i in range(2):
                    last = dve.tensor_tensor(pairs[:, :, :, i], pairs[:, :, :, i], r_gm, ALU.mult)
                n = done(last)
                dve.wait_ge(s_rt_b, n)
                first = [r_sc, r_pos]
                for c in range(2):
                    n = done(dve.tensor_reduce(r_w[:, c], first[c], AX.X, ALU.max))
                    dve.wait_ge(s_rt_b, n)
                    n = done(dve.tensor_tensor(r_rank, first[c], r_w[:, c].unsqueeze(2).to_broadcast([P, NR, NE]), ALU.is_equal))
                    dve.wait_ge(s_rt_b, n)
                    n = done(dve.scalar_tensor_tensor(r_rank, r_rank, -float(NE), eidx[:].unsqueeze(1).to_broadcast([P, NR, NE]),
                                                      ALU.mult, ALU.add))
                    dve.wait_ge(s_rt_b, n)
                    n = done(dve.tensor_reduce(r_at[:, c], r_rank, AX.X, ALU.min))
                    dve.wait_ge(s_rt_b, n)
                    n = done(dve.tensor_tensor(r_sel[:, c], r_rank, r_at[:, c].unsqueeze(2).to_broadcast([P, NR, NE]), ALU.is_equal))
                    dve.wait_ge(s_rt_b, n)
                    if c == 0:
                        n = done(dve.scalar_tensor_tensor(r_pos, r_sel[:, 0], -2.0, r_sc, ALU.mult, ALU.add))
                        dve.wait_ge(s_rt_b, n)
                dve.tensor_tensor(r_both, r_sel[:, 0], r_sel[:, 1], ALU.add).then_inc(s_both_ready, 1)

            def dve_route_slots(dve):
                k = [0]

                def done(ins):
                    ins.then_inc(s_rt_c, 1)
                    k[0] += 1
                    return k[0]

                dve.tensor_copy(h2all[:, :, D], r_w[:, 0, :])
                dve.tensor_tensor(h2all[:, :, D + 1], r_w[:, 1, :], r_w[:, 0, :], ALU.subtract)
                dve.tensor_scalar(h2all[:, :, D + 2], r_at[:, 0], float(NE), None, ALU.add)
                dve.tensor_copy(h2all[:, :, D + 3], token_id[:])
                dve.wait_ge(s_rank_done, 1)
                rk = RNK.rearrange("p (t e) -> p t e", e=NE)
                dve.tensor_copy(r_cnt, TOT).then_inc(s_tab, 1)
                n = done(dve.tensor_tensor(r_pos, rk, erow[:].unsqueeze(1).to_broadcast([P, NR, NE]), ALU.add))
                dve.wait_ge(s_rt_c, n)
                for i in range(2):
                    last = dve.tensor_tensor(r_tmp[:, i], r_pos, r_sel[:, i], ALU.mult)
                n = done(last)
                dve.wait_ge(s_rt_c, n)
                n = done(dve.tensor_reduce(r_slot, r_tmp, AX.X, ALU.add))
                dve.wait_ge(s_rt_c, n)
                dve.tensor_copy(slot_u[:], r_slot).then_inc(s_slots_ready, 1)

            def dve_tables(dve):
                k = [1]

                def done(ins):
                    ins.then_inc(s_tab, 1)
                    k[0] += 1
                    return k[0]

                dve.wait_ge(s_tab, 1)
                dve.tensor_tensor(r_end, r_cnt.unsqueeze(2).to_broadcast([P, NE, T // P]),
                                  step128[:].unsqueeze(1).to_broadcast([P, NE, T // P]), ALU.is_gt)
                n = done(dve.tensor_tensor(r_last, r_cnt, erow[:], ALU.add))
                dve.wait_ge(s_tab, n)
                dve.tensor_copy(pad_u[:], r_last[0:1, :]).then_inc(s_pad_ready, 1)
                n = done(dve.tensor_reduce(r_tiles, r_end, AX.X, ALU.add))
                dve.wait_ge(s_tab, n)
                n = done(dve.tensor_copy(r_ends, r_tiles))
                dve.wait_ge(s_tab, n)
                for e in range(1, NE):
                    n = done(dve.tensor_tensor(r_ends[:, e:e + 1], r_ends[:, e - 1:e], r_tiles[:, e:e + 1], ALU.add))
                    dve.wait_ge(s_tab, n)
                n = done(dve.tensor_tensor(r_done, r_ends.unsqueeze(1).to_broadcast([P, NT, NE]),
                                           tidx[:].unsqueeze(2).to_broadcast([P, NT, NE]), ALU.is_le))
                dve.wait_ge(s_tab, n)
                n = done(dve.tensor_reduce(r_tab[:, 0, :], r_done, AX.X, ALU.add))
                dve.wait_ge(s_tab, n)
                n = done(dve.tensor_tensor(r_done, r_done, r_tiles.unsqueeze(1).to_broadcast([P, NT, NE]), ALU.mult))
                dve.wait_ge(s_tab, n)
                dve.tensor_scalar(eid_f[:], r_tab[:, 0, :], float(NE - 1), None, ALU.min)
                n = done(dve.tensor_reduce(r_tab[:, 1, :], r_done, AX.X, ALU.add))
                dve.wait_ge(s_tab, n)
                dve.tensor_tensor(r_tab[:, 1, :], tidx[:], r_tab[:, 1, :], ALU.subtract)
                dve.tensor_scalar(r_tab[:, 2, :], eid_f[:], float(REGION), None, ALU.mult)
                n = done(dve.tensor_scalar(r_tab[:, 3, :], r_tab[:, 0, :], float(NE), None, ALU.is_ge))
                dve.wait_ge(s_tab, n)
                n = done(dve.scalar_tensor_tensor(r_tab[:, 2, :], r_tab[:, 1, :], float(P), r_tab[:, 2, :], ALU.mult, ALU.add))
                dve.wait_ge(s_tab, n)
                n = done(dve.tensor_scalar(r_tab[:, 0, :], r_tab[:, 2, :], r_last[:, NE - 1:NE], -1.0, ALU.subtract, ALU.mult))
                dve.wait_ge(s_tab, n)
                n = done(dve.tensor_tensor(r_tab[:, 0, :], r_tab[:, 0, :], r_tab[:, 3, :], ALU.mult))
                dve.wait_ge(s_tab, n)
                n = done(dve.tensor_tensor(r_tab[:, 2, :], r_tab[:, 2, :], r_tab[:, 0, :], ALU.add))
                dve.wait_ge(s_tab, n)
                dve.tensor_copy(tile_u[:, 0, :], eid_f[0:1, :])
                dve.tensor_copy(tile_u[:, 1, :], r_tab[0:1, 2, :]).then_inc(s_table_ready, 1)

            def pool_scatter(pool):
                pool.wait_ge(s_slots_ready, 1)
                for j in range(NR):
                    for i in range(2):
                        pool.indirect_dma_start(
                            out=routed_in, out_offset=bass.IndirectOffsetOnAxis(slot_u[:, i, j:j + 1], 0),
                            in_=h2all[:, j, :], in_offset=None).then_inc(s_scattered, 16)

            def sp_weights(sp, e, r):
                if 2 <= e < 2 + NEP:
                    sp.wait_ge(s_split_pool, e - 1)
                elif e >= 2 + NEP:
                    sp.wait_ge(s_split_dve, e - 1 - NEP)
                sp.dma_start(gu_stage(r), gu_t[:, ds(e, 1), :].rearrange("(k p) o n -> p k (o n)", p=P)).then_inc((s_est0_in, s_est1_in)[r], 16)
                sp.dma_start(dn_stage(r), down_t[ds(e, 1)].rearrange("o (j p) n -> p (o j) n", p=FH)).then_inc((s_est0_in, s_est1_in)[r], 16)

            def act_weights(act, e, r):
                act.wait_ge((s_est0_in, s_est1_in)[r], 16 * (e - r) + 32)
                act.activation(wgu[0][:, :, ds(e * (2 * F), 2 * F)], gu_stage(r), ACT.Copy)
                act.activation(wdn[0][:, :, ds(e * D, D)], dn_stage(r), ACT.Copy).then_inc(s_ew_hi, 1)

            NEP = 4

            def lo_gu(eng, e, r):
                eng.wait_ge(s_ew_hi, e + 1)
                return eng.tensor_tensor(wgu[1][:, :, ds(e * (2 * F), 2 * F)], gu_stage(r),
                                         wgu[0][:, :, ds(e * (2 * F), 2 * F)].bitcast(F32), ALU.subtract)

            def lo_dn(eng, e, r):
                return eng.tensor_tensor(wdn[1][:, :, ds(e * D, D)], dn_stage(r),
                                         wdn[0][:, :, ds(e * D, D)].bitcast(F32), ALU.subtract)

            def pool_weights(pool, e, r):
                lo_gu(pool, e, r)
                lo_dn(pool, e, r).then_inc(s_split_pool, 1)

            def sp_shared(sp, b, u, first):
                if not first:
                    sp.wait_ge(s_res_ready, b - 1)
                sp.dma_start(x1b[u][:], x1_dram[ds(b, 1)].rearrange("o (t p) d -> p (o t) d", p=P)).then_inc((s_x1b0_in, s_x1b1_in)[u], 16)

            def pe_shared_up(pe, b, u, first):
                if not first:
                    pe.wait_ge(s_act_mul, len(FT) * (b - 1))
                for j, (f, m) in enumerate(FT):
                    for g in range(2):
                        for k in range(KD):
                            last = mm3(pe, GUb[u][j][0:m, g * S:(g + 1) * S],
                                       parts(wsgu, slice(None), k, slice(g * FS + f, g * FS + f + m)),
                                       parts(h2T, slice(None), k, ds(b * S, S)), k == 0, k == KD - 1)
                    last.then_inc(s_shgu_done, 1)

            def SJ(u, j):
                return (u * len(FT) + j) % 2

            def act_shared(act, b, u):
                def hi(j):
                    f, m = FT[j]
                    act.wait_ge(s_act_mul, b * len(FT) + j + 1)
                    act.activation(aT[u][0][0:m, j, :], aact[SJ(u, j)][0:m, :], ACT.Copy).then_inc(s_a_hi, 1)

                for j, (f, m) in enumerate(FT):
                    n = b * len(FT) + j
                    act.wait_ge(s_shgu_done, n + 1)
                    if not (type(n) is int and n < 2):
                        act.wait_ge(s_act_mul, n - 1)
                    act.activation(sact[SJ(u, j)][0:m, :], GUb[u][j][0:m, 0:S], ACT.Silu).then_inc(s_silu_done, 1)
                    if j:
                        hi(j - 1)
                hi(len(FT) - 1)

            def dve_shared(dve, b, u, weights=False, out=None):
                def lo(j):
                    f, m = FT[j]
                    dve.wait_ge(s_a_hi, b * len(FT) + j + 1)
                    dve.tensor_tensor(aT[u][1][0:m, j, :], aact[SJ(u, j)][0:m, :], aT[u][0][0:m, j, :].bitcast(F32),
                                      ALU.subtract).then_inc(s_a_lo, 1)

                for j, (f, m) in enumerate(FT):
                    n = b * len(FT) + j
                    q = SJ(u, j)
                    dve.wait_ge(s_silu_done, n + 1)
                    if not (type(n) is int and n < 2):
                        dve.wait_ge(s_a_lo, n - 1)
                    dve.tensor_tensor(aact[q][0:m, :], sact[q][0:m, :], GUb[u][j][0:m, S:2 * S], ALU.mult).then_inc(s_act_mul, 1)
                    if j:
                        lo(j - 1)
                lo(len(FT) - 1)
                if out is not None:
                    dve_shared_scale(dve, b - 1, 1 - u)
                if weights:
                    lo_gu(dve, b, u)
                    lo_dn(dve, b, u).then_inc(s_split_dve, 1)
                if out is not None:
                    dve_shared_add(dve, b - 1, 1 - u)

            def pe_shared_down(pe, b, u, first):
                if not first:
                    pe.wait_ge(s_og_ready, b - 1)
                pe.wait_ge(s_a_lo, len(FT) * (b + 1))
                for t in range(TT):
                    for j, (f, m) in enumerate(FT):
                        last = mm3(pe, DN[u][:, t * D:(t + 1) * D],
                                   parts(aT[u], slice(0, m), j, slice(t * P, (t + 1) * P)),
                                   parts(wsd, slice(0, m), j), j == 0, j == len(FT) - 1)
                last.then_inc(s_shdn_done, 1)

            def dve_shared_scale(dve, b, u):
                dve.wait_ge(s_shdn_done, b + 1)
                dve.wait_ge(s_gb_in, 16)
                dve.wait_ge((s_x1b0_in, s_x1b1_in)[u], 8 * (b - u + 2))
                dve.tensor_tensor(og[u][:], bank2(DN[u]), gball[:, ds(b, 1)].rearrange("p b o d -> p (b o) d").to_broadcast([P, TT, D]),
                                  ALU.mult).then_inc(s_og_ready, 1)

            def dve_shared_add(dve, b, u):
                dve.wait_ge(s_og_ready, b + 1)
                dve.tensor_tensor(res[:, ds(b, 1)].rearrange("p o t d -> p (o t) d"), og[u][:], x1b[u][:], ALU.add).then_inc(s_res_ready, 1)

            def sp_tile(sp, t, r, first):
                sp.wait_ge(s_table_ready, 1)
                row = sp.value_load(tile_u[0:1, 1, ds(t, 1)], min_val=0, max_val=NE * REGION - P)
                sp.wait_ge(s_scattered, 32 * NR)
                sp.wait_ge(s_pad_out, 16 * NE)
                if not first:
                    sp.wait_ge(s_ea_ready, t - 3)
                sp.dma_start(xt_in[r][:], routed_in[ds(row, P), :]).then_inc(tile_sems[r], 16)

            tile_sems = [s_tile0_in, s_tile1_in, s_tile2_in, s_tile3_in]
            out_sems = [s_tile0_out, s_tile1_out, s_tile2_out, s_tile3_out]

            def tile_wait(t, r):
                return 4 * (t - r) + 16

            def pe_tile_in(pe, t, r):
                pe.wait_ge(tile_sems[r], tile_wait(t, r))
                for d in range(KD):
                    last = pe.transpose(XTb[r % 2][:, d * P:(d + 1) * P], xt_in[r][:, d * P:(d + 1) * P], ident[:])
                last.then_inc(s_ext_done, 1)

            def pe_expert(pe, experts, t, r):
                pe.wait_ge(s_table_ready, 1)
                pe.reg_load(experts[r], tile_u[0:1, 0, ds(t, 1)])

            def expert_of(pe, experts, r):
                return pe.snap(experts[r], min_val=0, max_val=NE - 1)

            def pe_tile_up(pe, experts, t, r):
                e = expert_of(pe, experts, r)
                pe.wait_ge(s_ex_lo, t + 1)
                for k in range(KD):
                    last = mm3(pe, EGU[r % 2][:, 0:2 * F], parts(eT[r], slice(None), k),
                               parts(wgu, slice(None), k, ds(e * (2 * F), 2 * F)), k == 0, k == KD - 1)
                last.then_inc(s_egu_done, 1)

            def pe_tile_act(pe, t, r):
                pe.wait_ge(s_ea_ready, t + 1)
                for j in range(2):
                    last = pe.transpose(ATb[r % 2][0:FH, j * P:(j + 1) * P], av[r % 2][:, j * FH:(j + 1) * FH], ident[:])
                last.then_inc(s_eat_done, 1)

            def pe_tile_down(pe, experts, t, r):
                e = expert_of(pe, experts, r)
                pe.wait_ge(s_ea_lo, t + 1)
                for j in range(2):
                    last = mm3(pe, EDN[r % 2][:, 0:D], parts(avT[r % 2], slice(None), j),
                               parts(wdn, slice(None), j, ds(e * D, D)), j == 0, j == 1)
                last.then_inc(s_edn_done, 1)

            def act_tile_in(act, t, r):
                act.wait_ge(s_ext_done, t + 1)
                act.activation(eT[r][0], bank2(XTb[r % 2], P), ACT.Copy).then_inc(s_ex_hi, 1)

            def act_tile_silu(act, t, r):
                act.wait_ge(s_egu_done, t + 1)
                act.activation(sg[r % 2], EGU[r % 2][:, 0:F], ACT.Silu).then_inc(s_esilu, 1)

            def act_tile_act(act, t, r):
                act.wait_ge(s_eat_done, t + 1)
                act.activation(avT[r % 2][0], bank2(ATb[r % 2], P)[0:FH], ACT.Copy).then_inc(s_ea_hi, 1)

            def act_tile_out(act, t, r):
                act.wait_ge(s_edn_done, t + 1)
                act.activation(yo[r], EDN[r % 2][:, 0:D], ACT.Copy).then_inc(s_ey_ready, 1)

            def dve_tile_in(dve, t, r):
                dve.wait_ge(s_ex_hi, t + 1)
                dve.tensor_tensor(eT[r][1], bank2(XTb[r % 2], P), eT[r][0].bitcast(F32), ALU.subtract).then_inc(s_ex_lo, 1)

            def dve_tile_meta(dve, t, r):
                q = r % 2
                dve.wait_ge(tile_sems[r], tile_wait(t, r))
                if not (type(t) is int and t < 4):
                    dve.wait_ge(out_sems[r], 4 * (t - r))
                dve.tensor_tensor(second[q][:], xt_in[r][:, D + 2:D + 3], eid_f[:, ds(t, 1)], ALU.not_equal).then_inc(s_esecond, 1)
                dve.wait_ge(s_esecond, t + 1)
                dve.scalar_tensor_tensor(wt[q][:], xt_in[r][:, D + 1:D + 2], second[q][:, 0:1], xt_in[r][:, D:D + 1],
                                         ALU.mult, ALU.add)
                dve.scalar_tensor_tensor(dest[r][:], second[q][:], float(T), xt_in[r][:, D + 3:D + 4],
                                         ALU.mult, ALU.add).then_inc(s_emeta, 1)

            def dve_tile_act(dve, t, r):
                q = r % 2
                dve.wait_ge(s_emeta, t + 1)
                dve.wait_ge(s_esilu, t + 1)
                dve.scalar_tensor_tensor(av[q], sg[q], wt[q][:, 0:1], EGU[q][:, F:2 * F],
                                         ALU.mult, ALU.mult).then_inc(s_ea_ready, 1)

            def dve_tile_lo(dve, t, r):
                q = r % 2
                dve.wait_ge(s_ea_hi, t + 1)
                dve.tensor_tensor(avT[q][1], bank2(ATb[q], P)[0:FH], avT[q][0].bitcast(F32), ALU.subtract).then_inc(s_ea_lo, 1)

            def pool_tile(pool, t, r):
                pool.wait_ge(s_emeta, t + 1)
                pool.wait_ge(s_ey_ready, t + 1)
                pool.indirect_dma_start(out=routed_out, out_offset=bass.IndirectOffsetOnAxis(dest[r][:, 0:1], 0),
                                        in_=yo[r], in_offset=None,
                                        bounds_check=2 * T - 1, oob_is_err=False).then_inc(out_sems[r], 16)

            def steps(eng, one):
                for t in range(4):
                    one(t, t, t >= 1, True, True)
                with eng.Fori(1, (NT - 3) // 4) as i:
                    for v in range(4):
                        one(4 * i + v, v, True, True, True)
                for t in range(NT - 3, NT):
                    one(t, t % 4, True, t < NT - 1, False)

            LASTT = NT - 1

            y_all = (h2all[:, :, 0:D].rearrange("p (b t) d -> p b t d", t=TT),
                     h2T[0][:].bitcast(F32).rearrange("p k (b n) -> p (k b) n", b=B // KD).rearrange("p b (t d) -> p b t d", t=TT))
            y_sems = [s_y0_in, s_y1_in, s_y2_in, s_y3_in, s_y4_in, s_y5_in, s_y6_in, s_y7_in]

            def on_pool(b):
                return b in (1, 4)

            def fin_count(b, step):
                return 3 * sum(on_pool(c) == on_pool(b) for c in range(b)) + step

            def final(eng, b, fin):
                eng.wait_ge(y_sems[b], 32)
                eng.tensor_tensor(y_all[0][:, b], y_all[0][:, b], y_all[1][:, b], ALU.add).then_inc(fin, 1)
                eng.wait_ge(fin, fin_count(b, 1))
                eng.tensor_tensor(y_all[0][:, b], y_all[0][:, b], gball[:, b].to_broadcast([P, TT, D]), ALU.mult).then_inc(fin, 1)
                eng.wait_ge(fin, fin_count(b, 2))
                eng.tensor_tensor(res[:, b], res[:, b], y_all[0][:, b], ALU.add).then_inc(fin, 1)

            with nc.Block() as block:
                @block.sync
                def _(sp):
                    for b in range(2):
                        sp_weights(sp, b, b)
                        sp_shared(sp, b, b, True)
                    for e in range(2, NEP):
                        sp_weights(sp, e, e % 2)
                    sp.wait_ge(s_both_ready, 1)
                    sp.dma_start(gball, modrow[:, 4 * D:5 * D].unsqueeze(0).to_broadcast([P, B, D]).unsqueeze(2)).then_inc(s_gb_in, 16)

                    def padding(e):
                        sp.wait_ge(s_pad_written, 2)
                        sp.wait_ge(s_pad_ready, 1)
                        row = sp.value_load(pad_u[0:1, e:e + 1], min_val=0, max_val=NE * REGION - P)
                        sp.dma_start(routed_in[ds(row, P), :], pad[:]).then_inc(s_pad_out, 16)

                    for b in range(2, B):
                        if b >= NEP:
                            sp_weights(sp, b, b % 2)
                        sp_shared(sp, b, b % 2, False)
                        if b >= B // 2:
                            for e in (2 * b - B, 2 * b - B + 1):
                                padding(e)
                    for t in range(4):
                        sp_tile(sp, t, t, True)
                    with sp.Fori(1, (NT - 3) // 4) as i:
                        for v in range(4):
                            sp_tile(sp, 4 * i + v, v, False)
                    for t in range(NT - 3, NT):
                        sp_tile(sp, t, t % 4, False)
                    for r in range(4):
                        sp.wait_ge(out_sems[r], 16 * ((NT + 3 - r) // 4))

                    for b in range(B):
                        sp.dma_start(y_all[0][:, b], routed_out[b * S:(b + 1) * S, :].rearrange("(t p) d -> p t d", p=P)).then_inc(y_sems[b], 16)
                        sp.dma_start(y_all[1][:, b], routed_out[T + b * S:T + (b + 1) * S, :].rearrange("(t p) d -> p t d", p=P)).then_inc(y_sems[b], 16)
                    for b in range(B):
                        sp.wait_ge(s_fin_pool if on_pool(b) else s_fin_dve, fin_count(b, 3))
                        sp.dma_start(out[b].rearrange("(t p) d -> p t d", p=P), res[:, b]).then_inc(s_stored, 16)
                    sp.wait_ge(s_stored, 16 * B)

                @block.gpsimd
                def _(pool):
                    pool.memset(pad[:], 0.0).then_inc(s_pad_written, 1)
                    pool.wait_ge(s_pad_written, 1)
                    pool.memset(pad[:, D + META - 1:D + META], float(SKIP)).then_inc(s_pad_written, 1)
                    for e in range(NEP):
                        pool_weights(pool, e, e % 2)
                    pool_scatter(pool)
                    for t in range(NT):
                        pool_tile(pool, t, t % 4)
                    for b in range(B):
                        if on_pool(b):
                            final(pool, b, s_fin_pool)

                @block.scalar
                def _(act):
                    act_route(act)
                    for e in range(2):
                        act_weights(act, e, e)
                    act_shared(act, 0, 0)
                    for e in range(2, NEP):
                        act_weights(act, e, e % 2)
                    for b in range(1, NEP):
                        act_shared(act, b, b % 2)
                    with act.Fori(NEP // 2, NPAIR) as p:
                        for u in range(2):
                            act_shared(act, 2 * p + u, u)
                            act_weights(act, 2 * p + u, u)

                    def one(t, r, back, up, ahead):
                        if up:
                            act_tile_silu(act, t + 1, (r + 1) % 4)
                        act_tile_act(act, t, r)
                        if ahead:
                            act_tile_in(act, t + 3, (r + 3) % 4)
                        if back:
                            act_tile_out(act, t - 1, (r - 1) % 4)

                    for t in range(2):
                        act_tile_in(act, t, t)
                    act_tile_silu(act, 0, 0)
                    act_tile_in(act, 2, 2)
                    steps(act, one)
                    act_tile_out(act, LASTT, LASTT % 4)

                @block.vector
                def _(dve):
                    dve_route_scores(dve)
                    dve_route_select(dve)
                    dve_shared(dve, 0, 0)
                    dve_route_slots(dve)
                    for b in (1, 2):
                        dve_shared(dve, b, b % 2, b >= NEP, True)
                    dve_tables(dve)
                    for b in range(3, B):
                        dve_shared(dve, b, b % 2, b >= NEP, True)
                    dve_shared_scale(dve, B - 1, 1)
                    dve_shared_add(dve, B - 1, 1)

                    def one(t, r, back, up, ahead):
                        if up:
                            dve_tile_meta(dve, t + 1, (r + 1) % 4)
                            dve_tile_act(dve, t + 1, (r + 1) % 4)
                        dve_tile_lo(dve, t, r)
                        if ahead:
                            dve_tile_in(dve, t + 3, (r + 3) % 4)

                    for t in range(2):
                        dve_tile_in(dve, t, t)
                    dve_tile_meta(dve, 0, 0)
                    dve_tile_act(dve, 0, 0)
                    dve_tile_in(dve, 2, 2)
                    steps(dve, one)

                    for b in range(B):
                        if not on_pool(b):
                            final(dve, b, s_fin_dve)

                @block.tensor
                def _(pe):
                    experts = [pe.alloc_register(f"expert{q}") for q in range(4)]
                    pe_logits_t(pe)
                    pe_shared_up(pe, 0, 0, True)
                    pe_shared_up(pe, 1, 1, True)
                    pe_rank(pe)
                    pe_shared_down(pe, 0, 0, True)
                    pe_shared_up(pe, 2, 0, False)
                    pe.wait_ge(s_slots_ready, 1)
                    pe_shared_down(pe, 1, 1, True)
                    with pe.Fori(1, NPAIR - 1) as p:
                        for u in range(2):
                            pe_shared_up(pe, 2 * p + 1 + u, 1 - u, False)
                            pe_shared_down(pe, 2 * p + u, u, False)
                    pe_shared_up(pe, B - 1, 1, False)
                    pe_shared_down(pe, B - 2, 0, False)
                    pe_shared_down(pe, B - 1, 1, False)

                    def one(t, r, back, up, ahead):
                        if up:
                            pe_tile_up(pe, experts, t + 1, (r + 1) % 4)
                        if not (type(t) is int and t >= NT - 2):
                            pe_expert(pe, experts, t + 2, (r + 2) % 4)
                        pe_tile_act(pe, t, r)
                        if ahead:
                            pe_tile_in(pe, t + 3, (r + 3) % 4)
                        if back:
                            pe_tile_down(pe, experts, t - 1, (r - 1) % 4)

                    pe.wait_ge(s_split_pool, NEP)
                    pe.wait_ge(s_split_dve, NE - NEP)
                    pe.wait_ge(s_og_ready, B)
                    for t in range(2):
                        pe_tile_in(pe, t, t)
                    for t in range(2):
                        pe_expert(pe, experts, t, t)
                    pe_tile_up(pe, experts, 0, 0)
                    pe_tile_in(pe, 2, 2)
                    steps(pe, one)
                    pe_tile_down(pe, experts, LASTT, LASTT % 4)


def kernel(L0_attn_hidden_states, L0_attn_c_attn_w, L0_attn_c_attn_b, L0_attn_c_proj_w, L0_attn_c_proj_b,
           L0_attn_cam_gate, L0_attn_cam_w0, L0_attn_cam_w1, L0_ffn_gate_weight, L0_ffn_gate_w, L0_ffn_up_w,
           L0_ffn_down_w, L0_ffn_sh_gate_w, L0_ffn_sh_up_w, L0_ffn_sh_down_w, L0_c, L0_wmod):
    import concourse.bacc as bacc
    from concourse.bass_utils import run_bass_kernel_spmd

    def lay(a):
        return np.ascontiguousarray(a)

    gate_w, up_w = np.asarray(L0_ffn_gate_w), np.asarray(L0_ffn_up_w)
    arrays = {
        "x": lay(L0_attn_hidden_states),
        "w_qkv": lay(L0_attn_c_attn_w),
        "b_cols": lay(np.asarray(L0_attn_c_attn_b).reshape(-1, P).T),
        "w_proj": lay(L0_attn_c_proj_w),
        "b_proj": lay(L0_attn_c_proj_b),
        "gate_col": lay(np.asarray(L0_attn_cam_gate).reshape(P, 1)),
        "cam_w0": lay(L0_attn_cam_w0),
        "cam_w1": lay(L0_attn_cam_w1),
        "router_t": lay(np.asarray(L0_ffn_gate_weight).T),
        "gu_t": lay(np.concatenate([gate_w, up_w], axis=1).transpose(2, 0, 1)),
        "down_t": lay(np.asarray(L0_ffn_down_w).transpose(0, 2, 1)),
        "sh_gu_t": lay(np.concatenate([np.asarray(L0_ffn_sh_gate_w), np.asarray(L0_ffn_sh_up_w)], axis=0).T),
        "sh_down_t": lay(np.asarray(L0_ffn_sh_down_w).T),
        "c_t": lay(np.asarray(L0_c).T),
        "w_mod": lay(L0_wmod),
    }
    nc = bacc.Bacc("TRN2", target_bir_lowering=False, num_devices=1)
    args = [nc.dram_tensor(n, a.shape, mybir.dt.from_np(a.dtype), kind="ExternalInput").ap() for n, a in arrays.items()]
    out = nc.dram_tensor("out", arrays["x"].shape, F32, kind="ExternalOutput").ap()
    adaln_block(nc, *args, out)
    r = run_bass_kernel_spmd(nc, [arrays], core_ids=[0])
    return r.results[0]["out"]
```
